# Optimizing a Trainium2 kernel written in Bass

```python
import numpy as np
import jax
import jax.numpy as jnp

def _softmax(x, axis=-1):
    return jax.nn.softmax(x, axis=axis)

def _gelu(x):
    return jax.nn.gelu(x, approximate=True)

def _silu(x):
    return jax.nn.silu(x)

def _sigmoid(x):
    return jax.nn.sigmoid(x)

def _layernorm(x, axis=-1, eps=1e-05):
    m = jnp.mean(x, axis=axis, keepdims=True)
    v = jnp.var(x, axis=axis, keepdims=True)
    return (x - m) / jnp.sqrt(v + eps)

def _scatter_add(tgt, idx, src, axis=0):
    return tgt.at[idx].add(src)

def _segment_sum(src, seg, n):
    return jax.ops.segment_sum(src, seg, n)
kernel_name = 'mk_gnn_resnorm_d4_gnn_r16_a76f2f'

def setup_inputs(seed: int=0):
    np.random.seed(seed)
    _w = jnp.asarray

    def _rec_inputs():
        import jax
        import jax.numpy as jnp
        _gk = jax.random.key(seed)
        x = -0.0002117 + 1 * jax.random.normal(jax.random.fold_in(_gk, 1), (6250, 256), jnp.float32)
        src = jax.random.randint(jax.random.fold_in(_gk, 2), (100000,), 0, 6250, jnp.int32)
        dst = jnp.minimum((6250 * jax.random.uniform(jax.random.fold_in(_gk, 3), (100000,)) ** 2.0).astype(jnp.int32), 99999)
        _o = jnp.argsort(dst, stable=True)
        src = src[_o]
        dst = dst[_o]
        edge_attr_128 = -0.000128692 + 0.999872 * jax.random.normal(jax.random.fold_in(_gk, 12), (100000, 128), jnp.float32)
        edge_weight = jax.random.uniform(jax.random.fold_in(_gk, 14), (100000,), jnp.float32, 0.0, 1)
        return (x, src, dst, edge_attr_128, edge_weight)
    x, src, dst, edge_attr_128, edge_weight = _rec_inputs()

    def _L0_gnn_setup():
        import jax, jax.numpy as jnp
        import numpy as np
        N_NODES = 6250
        N_EDGES = 100000
        D_IN = 256
        D_OUT = 256
        key = jax.random.key(seed)
        k1, k2, k3, k4 = jax.random.split(key, 4)
        x = jax.random.normal(k1, (N_NODES, D_IN), dtype=jnp.float32)
        edge_index = jax.random.randint(k2, (2, N_EDGES), 0, N_NODES, dtype=jnp.int64)
        W = jax.random.normal(k3, (D_OUT, D_IN), dtype=jnp.float32) * (1.0 / np.sqrt(D_IN))
        b = jax.random.normal(k4, (D_OUT,), dtype=jnp.float32) * 0.01
        return {'x': x, 'edge_index': edge_index, 'W': W, 'b': b}
    _L0_gnn_all = _L0_gnn_setup()
    _L0_gnn_in = {k: v for k, v in _L0_gnn_all.items() if k in ('W', 'b')}
    del _L0_gnn_all

    def _L1_gnn_setup():
        import jax, jax.numpy as jnp
        import numpy as np
        N_NODES = 6250
        N_EDGES = 18750
        DIM = 256
        LN_EPS = 1e-05
        key = jax.random.key(seed)
        ks = jax.random.split(key, 4)
        scale = 1.0 / np.sqrt(DIM)
        h = jax.random.normal(ks[0], (N_NODES, DIM), dtype=jnp.float32)
        edge_index = jax.random.randint(ks[1], (2, N_EDGES), 0, N_NODES, dtype=jnp.int64)
        W1 = jax.random.normal(ks[2], (DIM, DIM), dtype=jnp.float32) * scale
        b1 = jnp.zeros((DIM,), dtype=jnp.float32)
        W2 = jax.random.normal(ks[3], (DIM, DIM), dtype=jnp.float32) * scale
        b2 = jnp.zeros((DIM,), dtype=jnp.float32)
        eps = jnp.zeros((), dtype=jnp.float32)
        gamma = jnp.ones((DIM,), dtype=jnp.float32)
        beta = jnp.zeros((DIM,), dtype=jnp.float32)
        return {'h': h, 'edge_index': edge_index, 'W1': W1, 'b1': b1, 'W2': W2, 'b2': b2, 'eps': eps, 'gamma': gamma, 'beta': beta}
    _L1_gnn_all = _L1_gnn_setup()
    _L1_gnn_in = {k: v for k, v in _L1_gnn_all.items() if k in ('W1', 'b1', 'W2', 'b2', 'eps', 'gamma', 'beta')}
    del _L1_gnn_all

    def _L2_gnn_setup():
        import jax, jax.numpy as jnp
        import numpy as np
        N = 6250
        E = 200000
        DI = 256
        DO = 256
        BN_EPS = 1e-05

        def _bn_relu(h, gamma, beta):
            mean = jnp.mean(h, axis=0)
            var = jnp.var(h, axis=0)
            hn = (h - mean) * jax.lax.rsqrt(var + BN_EPS)
            return jax.nn.relu(hn * gamma + beta)
        key = jax.random.key(seed)
        ks = jax.random.split(key, 6)
        x = jax.random.normal(ks[0], (N, DI), dtype=jnp.float32)
        edge_row = jax.random.randint(ks[1], (E,), 0, N, dtype=jnp.int32)
        edge_col = jax.random.randint(ks[2], (E,), 0, N, dtype=jnp.int32)
        edge_vals = jnp.ones((E,), dtype=jnp.float32)
        eps = jnp.zeros((1,), dtype=jnp.float32)
        W1 = jax.random.normal(ks[3], (DI, DO), dtype=jnp.float32) * 0.05
        b1 = jnp.zeros((DO,), dtype=jnp.float32)
        g1 = jnp.ones((DO,), dtype=jnp.float32)
        be1 = jnp.zeros((DO,), dtype=jnp.float32)
        W2 = jax.random.normal(ks[4], (DO, DO), dtype=jnp.float32) * 0.05
        b2 = jnp.zeros((DO,), dtype=jnp.float32)
        g2 = jnp.ones((DO,), dtype=jnp.float32)
        be2 = jnp.zeros((DO,), dtype=jnp.float32)
        return {'x': x, 'edge_row': edge_row, 'edge_col': edge_col, 'edge_vals': edge_vals, 'eps': eps, 'W1': W1, 'b1': b1, 'g1': g1, 'be1': be1, 'W2': W2, 'b2': b2, 'g2': g2, 'be2': be2}
    _L2_gnn_all = _L2_gnn_setup()
    _L2_gnn_in = {k: v for k, v in _L2_gnn_all.items() if k in ('eps', 'W1', 'b1', 'g1', 'be1', 'W2', 'b2', 'g2', 'be2')}
    del _L2_gnn_all

    def _L3_gnn_setup():
        import jax, jax.numpy as jnp
        import numpy as np
        SLOPE = 0.2
        N_NODES = 625
        N_EDGES = 20000
        D_NODE = 256
        D_EDGE = 128
        D_HID = 256
        key = jax.random.key(seed)
        ks = jax.random.split(key, 10)
        node_features = jax.random.normal(ks[0], (N_NODES, D_NODE), dtype=jnp.float32)
        edge_features = jax.random.normal(ks[1], (N_EDGES, D_EDGE), dtype=jnp.float32)
        edge_index = jax.random.randint(ks[2], (2, N_EDGES), 0, N_NODES, dtype=jnp.int64)

        def lin(k, fan_in, fan_out):
            lim = 1.0 / np.sqrt(fan_in)
            kw, kb = jax.random.split(k)
            W = jax.random.uniform(kw, (fan_in, fan_out), minval=-lim, maxval=lim, dtype=jnp.float32)
            b = jax.random.uniform(kb, (fan_out,), minval=-lim, maxval=lim, dtype=jnp.float32)
            return (W, b)
        w_W, w_b = lin(ks[3], D_NODE, D_HID)
        ew_W, ew_b = lin(ks[4], D_EDGE, D_HID)
        a_W, a_b = lin(ks[5], 3 * D_HID, 1)
        return {'node_features': node_features, 'edge_features': edge_features, 'edge_index': edge_index, 'w_W': w_W, 'w_b': w_b, 'ew_W': ew_W, 'ew_b': ew_b, 'a_W': a_W, 'a_b': a_b}
    _L3_gnn_all = _L3_gnn_setup()
    _L3_gnn_in = {k: v for k, v in _L3_gnn_all.items() if k in ('w_W', 'w_b', 'ew_W', 'ew_b', 'a_W', 'a_b')}
    del _L3_gnn_all
    return {'x': x, 'src': src, 'dst': dst, 'edge_attr_128': edge_attr_128, 'edge_weight': edge_weight, 'L0_gnn_W': _L0_gnn_in['W'], 'L0_gnn_b': _L0_gnn_in['b'], 'L1_gnn_W1': _L1_gnn_in['W1'], 'L1_gnn_b1': _L1_gnn_in['b1'], 'L1_gnn_W2': _L1_gnn_in['W2'], 'L1_gnn_b2': _L1_gnn_in['b2'], 'L1_gnn_eps': _L1_gnn_in['eps'], 'L1_gnn_gamma': _L1_gnn_in['gamma'], 'L1_gnn_beta': _L1_gnn_in['beta'], 'L2_gnn_eps': _L2_gnn_in['eps'], 'L2_gnn_W1': _L2_gnn_in['W1'], 'L2_gnn_b1': _L2_gnn_in['b1'], 'L2_gnn_g1': _L2_gnn_in['g1'], 'L2_gnn_be1': _L2_gnn_in['be1'], 'L2_gnn_W2': _L2_gnn_in['W2'], 'L2_gnn_b2': _L2_gnn_in['b2'], 'L2_gnn_g2': _L2_gnn_in['g2'], 'L2_gnn_be2': _L2_gnn_in['be2'], 'L3_gnn_w_W': _L3_gnn_in['w_W'], 'L3_gnn_w_b': _L3_gnn_in['w_b'], 'L3_gnn_ew_W': _L3_gnn_in['ew_W'], 'L3_gnn_ew_b': _L3_gnn_in['ew_b'], 'L3_gnn_a_W': _L3_gnn_in['a_W'], 'L3_gnn_a_b': _L3_gnn_in['a_b']}

def reference(x, src, dst, edge_attr_128, edge_weight, L0_gnn_W, L0_gnn_b, L1_gnn_W1, L1_gnn_b1, L1_gnn_W2, L1_gnn_b2, L1_gnn_eps, L1_gnn_gamma, L1_gnn_beta, L2_gnn_eps, L2_gnn_W1, L2_gnn_b1, L2_gnn_g1, L2_gnn_be1, L2_gnn_W2, L2_gnn_b2, L2_gnn_g2, L2_gnn_be2, L3_gnn_w_W, L3_gnn_w_b, L3_gnn_ew_W, L3_gnn_ew_b, L3_gnn_a_W, L3_gnn_a_b):
    import jax
    import jax.numpy as jnp

    def _L0_gnn_ref(x, edge_index, W, b):
        import jax, jax.numpy as jnp
        import numpy as np
        N_NODES = 6250
        N_EDGES = 100000
        D_IN = 256
        D_OUT = 256
        h = jnp.einsum('nd,od->no', x, W) + b
        row, col = (edge_index[0], edge_index[1])
        msgs = h[col]
        out = jax.ops.segment_sum(msgs, row, num_segments=h.shape[0])
        return out

    def _L1_gnn_ref(h, edge_index, W1, b1, W2, b2, eps, gamma, beta):
        import jax, jax.numpy as jnp
        import numpy as np
        N_NODES = 6250
        N_EDGES = 18750
        DIM = 256
        LN_EPS = 1e-05
        src, dst = (edge_index[0], edge_index[1])
        agg = jax.ops.segment_sum(h[src], dst, num_segments=h.shape[0])
        z = (1.0 + eps) * h + agg
        z = jax.nn.relu(z @ W1 + b1) @ W2 + b2
        r = z + h
        mu = jnp.mean(r, axis=-1, keepdims=True)
        var = jnp.mean(jnp.square(r - mu), axis=-1, keepdims=True)
        ln = (r - mu) * jax.lax.rsqrt(var + LN_EPS) * gamma + beta
        return jax.nn.relu(ln)

    def _L2_gnn_ref(x, edge_row, edge_col, edge_vals, eps, W1, b1, g1, be1, W2, b2, g2, be2):
        import jax, jax.numpy as jnp
        import numpy as np
        N = 6250
        E = 200000
        DI = 256
        DO = 256
        BN_EPS = 1e-05

        def _bn_relu(h, gamma, beta):
            mean = jnp.mean(h, axis=0)
            var = jnp.var(h, axis=0)
            hn = (h - mean) * jax.lax.rsqrt(var + BN_EPS)
            return jax.nn.relu(hn * gamma + beta)
        n = x.shape[0]
        msgs = edge_vals[:, None] * x[edge_col]
        agg = jax.ops.segment_sum(msgs, edge_row, num_segments=n)
        h = (1.0 + eps[0]) * x + agg
        h = _bn_relu(h @ W1 + b1, g1, be1)
        h = _bn_relu(h @ W2 + b2, g2, be2)
        return h

    def _L3_gnn_ref(node_features, edge_features, edge_index, w_W, w_b, ew_W, ew_b, a_W, a_b):
        import jax, jax.numpy as jnp
        import numpy as np
        SLOPE = 0.2
        N_NODES = 625
        N_EDGES = 20000
        D_NODE = 256
        D_EDGE = 128
        D_HID = 256
        N = node_features.shape[0]
        lrelu = lambda x: jax.nn.leaky_relu(x, negative_slope=SLOPE)
        h = lrelu(node_features @ w_W + w_b)
        edge_h = lrelu(edge_features @ ew_W + ew_b)
        tgt = edge_index[0]
        nbr = edge_index[1]
        h_i = h[tgt]
        h_j = h[nbr]
        e_ij = jnp.concatenate([h_i, h_j, edge_h], axis=-1) @ a_W + a_b
        seg_max = jax.ops.segment_max(e_ij, tgt, num_segments=N)
        ex = jnp.exp(e_ij - seg_max[tgt])
        seg_sum = jax.ops.segment_sum(ex, tgt, num_segments=N)
        alpha = ex / seg_sum[tgt]
        msg = alpha * h_j
        out = jax.ops.segment_sum(msg, tgt, num_segments=N)
        return lrelu(out)
    edge_index = jnp.stack([src, dst])
    x = _layernorm(x + _L0_gnn_ref(x, edge_index, L0_gnn_W, L0_gnn_b), axis=-1)
    x = _layernorm(x + _L1_gnn_ref(x, edge_index, L1_gnn_W1, L1_gnn_b1, L1_gnn_W2, L1_gnn_b2, L1_gnn_eps, L1_gnn_gamma, L1_gnn_beta), axis=-1)
    x = _layernorm(x + _L2_gnn_ref(x, src, dst, edge_weight, L2_gnn_eps, L2_gnn_W1, L2_gnn_b1, L2_gnn_g1, L2_gnn_be1, L2_gnn_W2, L2_gnn_b2, L2_gnn_g2, L2_gnn_be2), axis=-1)
    x = _layernorm(x + _L3_gnn_ref(x, edge_attr_128, edge_index, L3_gnn_w_W, L3_gnn_w_b, L3_gnn_ew_W, L3_gnn_ew_b, L3_gnn_a_W, L3_gnn_a_b), axis=-1)
    return x

_drawn_inputs = setup_inputs


def setup_inputs(seed=0):
    import zlib

    import numpy as np

    out = dict(_drawn_inputs(seed))
    spreads = {'L1_gnn_b1': (0.0, 0.8),
     'L1_gnn_b2': (0.0, 0.55),
     'L1_gnn_gamma': (1.0, 0.2),
     'L1_gnn_beta': (0.0, 0.1),
     'L2_gnn_b1': (0.0, 2.0),
     'L2_gnn_g1': (1.0, 0.2),
     'L2_gnn_be1': (0.0, 0.1),
     'L2_gnn_b2': (0.0, 2.0),
     'L2_gnn_g2': (1.0, 0.2),
     'L2_gnn_be2': (0.0, 0.1)}
    factors = {'edge_attr_128': 4.94, 'L3_gnn_ew_W': 5.354, 'L3_gnn_ew_b': 32.076, 'L3_gnn_a_W': 3.822}
    for name, (base, spread) in spreads.items():
        noise = np.random.default_rng([zlib.crc32(name.encode()), seed]).standard_normal(out[name].shape)
        drawn = base * np.exp(spread * noise) if base else spread * noise
        out[name] = jnp.asarray(drawn.astype(out[name].dtype))
    for name, factor in factors.items():
        out[name] = (out[name] * factor).astype(out[name].dtype)
    return out
```

```python
from contextlib import ExitStack

import concourse.bass as bass
from concourse import mybir

P = 128
ALU = mybir.AluOpType
ACT = mybir.ActivationFunctionType
F32 = mybir.dt.float32
I32 = mybir.dt.int32
U8 = mybir.dt.uint8
AX_X = mybir.AxisListType.X

N_NODES = 6250
N_EDGES = 100000
D = 256
D_EDGE = 128
KC = D // P
T = -(-N_NODES // P)
LAST = N_NODES - (T - 1) * P
NPAD = T * P
COLS = 800
EP = N_EDGES // COLS
SLOPE = 0.2
LN_EPS = 1e-5
BN_EPS = 1e-5

G = 8
RG = 4
R = G * RG
MOST_SLOTS = (N_EDGES + T * (P - 1)) // P
ITERS = -(-MOST_SLOTS // R)
SLOTS = ITERS * R
GROUPS = SLOTS // G
RECORDS = P * SLOTS

SC = 8
SG = 4
SITERS = COLS // (SC * SG)
EC = 4
ES = SC * SG // EC
AR = 4
OUT_OF_RANGE = 1 << 20
NOWHERE = 127 + P * 50000
NO_NODE = 8191
BIG = 1e30
FLOOR = -1e20
HW = D + 2
AW = D + 1
SB = 4
NB = -(-T // SB)
assert EP * COLS == N_EDGES and SB * (NB - 1) + 1 == T and NB % 2 and SITERS * SC * SG == COLS


def wait(eng, sem, n):
    if not isinstance(n, int) or n > 0:
        eng.wait_ge(sem, n)


def rounds(eng, n, body, first=True):
    if first:
        body(0)
    with eng.Fori(1 if first else 0, n) as i:
        body(i)


def batches(eng, body):
    body(0, 0, SB)
    body(1, 1, SB)
    with eng.Fori(1, (NB - 1) // 2) as i:
        for q in range(2):
            body(i * 2 + q, q, SB)
    body(NB - 1, 0, 1)


def each_batch(body):
    for b in range(NB):
        body(b, b % 2, min(SB, T - b * SB))


def gnn_program(nc, a, out):
    with ExitStack() as ctx:
        def sb(name, shape, dt=F32):
            return ctx.enter_context(nc.sbuf_tensor(name, shape, dt))

        table = [nc.dram_tensor(f"table{i}", [NPAD, HW if i == 3 else D], F32).ap() for i in range(4)]
        rec_src = nc.dram_tensor("rec_src", [RECORDS, 4], F32).ap()
        rec_dst = nc.dram_tensor("rec_dst", [RECORDS, 2], F32).ap()

        X = sb("X", [P, T, D])
        ACC = sb("ACC", [P, T * AW])
        ZT = sb("ZT", [P, T * HW])
        meta_src = sb("meta_src", [P, SLOTS, 4])
        meta_dst = sb("meta_dst", [P, SLOTS, 2])
        tile_src = sb("tile_src", [P, SLOTS], I32)
        tile_dst = sb("tile_dst", [P, SLOTS], I32)
        reset = sb("reset", [P, SLOTS])
        cslot = sb("cslot", [P, SLOTS])
        W = sb("W", [P, 2 * KC, D])
        bc = sb("bc", [P, 3, D])
        ewW = sb("ewW", [P, D])
        xT = sb("xT", [P, 2, KC, SB * P])
        z1 = sb("z1", [P, SB * D])
        ident = sb("ident", [P, P])
        iota = sb("iota", [P, P])
        ones = sb("ones", [P, P])
        before = sb("before", [P, P])
        col = sb("col", [P, 24])
        ends = sb("ends", [P, 2, 2, T])
        small = sb("small", [P, 6, T])
        s1 = sb("s1", [P, T])
        s2 = sb("s2", [P, T])
        lin = sb("lin", [P, 4])
        endT = sb("endT", [P, 2, 2])
        gidx = sb("gidx", [P, RG, G], I32)
        sidx = sb("sidx", [P, SG, SC], I32)
        spay = sb("spay", [P, SG, SC, 4])
        token = sb("token", [P, 1])
        att = sb("att", [P, 5, G])
        runmax = sb("runmax", [P, 2, 1 + G])
        corr = sb("corr", [P, 2, G])
        bias = sb("bias", [P, 2, G])
        stats = sb("stats", [P, KC, NB, 6])
        mv = sb("mv", [P, KC, 8])

        acc3 = ACC[:, :].rearrange("p (t w) -> p t w", w=AW)
        accd = acc3[:, :, 0:D]
        zt3 = ZT[:, 0:T * D].rearrange("p (t w) -> p t w", w=D)
        ztf = ZT[:, 0:KC * NPAD].rearrange("p (k n) -> p k n", k=KC)
        ht = ZT[:, :].rearrange("p (t w) -> p t w", w=HW)

        ring = ZT[:, 0:R * HW].rearrange("p (s w) -> p s w", w=HW)
        o = R * HW
        sel = ZT[:, o:o + 2 * G * P].rearrange("p (b s e) -> p b s e", b=2, e=P)
        o += 2 * G * P
        logit = ZT[:, o:o + G * P].rearrange("p (s e) -> p s e", e=P)
        o += G * P
        probT = ZT[:, o:o + G * P].rearrange("p (s e) -> p s e", e=P)
        assert o + G * P <= T * HW

        rows_ = ZT[:, 0:15 * COLS].rearrange("p (r c) -> p r c", c=COLS)
        key = [rows_[:, 0].bitcast(I32), rows_[:, 1].bitcast(I32)]
        bucket, pos = rows_[:, 2], rows_[:, 3]
        run = [rows_[:, 4], rows_[:, 5]]
        ibuf = rows_[:, 6].bitcast(I32)
        rec_of = [rows_[:, 7].bitcast(I32), rows_[:, 8].bitcast(I32)]
        pay_src = ZT[:, 9 * COLS:13 * COLS].rearrange("p (c f) -> p c f", f=4)
        pay_dst = ZT[:, 13 * COLS:15 * COLS].rearrange("p (c f) -> p c f", f=2)
        pay = [pay_src, pay_dst]
        mask = ACC[:, 0:T * COLS // 4].bitcast(U8).rearrange("p (b c) -> p b c", b=T)
        o = T * COLS // 4
        attr = ACC[:, o:o + AR * EC * D_EDGE].rearrange("p (b c d) -> p b c d", b=AR, d=D_EDGE)
        assert o + AR * EC * D_EDGE <= T * AW
        slot_no, past = reset, cslot
        meta = [meta_src, meta_dst, meta_src, meta_src]
        slot_tile = [tile_src, tile_dst, tile_src, tile_src]

        EWB, A3, B1, L2B1, G1, BE1, L2B2, G2, BE2 = range(0, 18, 2)
        EPS1, EPS2, AB = 18, 19, 20

        ps = ctx.enter_context(nc.psum_tensor("ps", [P, 8, 512], F32))
        psf = ps[:, :, :].rearrange("p b c -> p (b c)")

        names = """prefix_out ew_psum lin_ready consts ident_ready zeroed keys_in x_in fill_in records_in table_in stored weights_in cols_in
          dve_chain counted prefix base_ready scanned ranked record_ready ends_ready endT_psum endT_ready
          past_ready tile_psum tile_ready wT_psum wT_ready xT_psum xT_sbuf z_psum z_sbuf y_psum y_used
          attrT_psum attrT_sbuf ez_psum lr_ready logit_psum pay_ready scat_ready
          idx_ready idx_token sel_ready summed added acc_zero agg_ready
          ln_center ln_square ln_var ln_sqrt ln_done bn_in bn_var bn_sqrt bn_scale bn_applied back_psum back_used
          s1_ready c_psum c_ready ht_ready ev_ready ne_ready mask_logit t_psum max_ready bias_ready corr_ready
          probT_ready p_psum"""
        sem = {n: ctx.enter_context(nc.semaphore(n)) for n in names.split()}
        gathered = [ctx.enter_context(nc.semaphore(f"gathered{i}")) for i in range(RG)]
        scattered = [ctx.enter_context(nc.semaphore(f"scattered{i}")) for i in range(SG)]
        attr_in = [ctx.enter_context(nc.semaphore(f"attr_in{i}")) for i in range(AR)]

        TABLE_IN = [16 * NB, 16 * (NB + 1), 16 * (NB + 2), 16 * (NB + 3)]
        WEIGHTS = [48, 128, 160, 224]
        ZB = {1: 0, 2: NB, "2b": 2 * NB}
        YB = {0: 0, 1: NB, 3: 2 * NB}
        ESTEPS = COLS // EC

        def tiles(view, b, nt):
            return view[:, b * SB:b * SB + nt] if isinstance(b, int) else view[:, bass.ds(b * SB, nt)]

        def nodes(b, n):
            return slice(b * SB * P, b * SB * P + n) if isinstance(b, int) else bass.ds(b * (SB * P), n)

        block = ctx.enter_context(nc.Block())

        @block.sync
        def _(sp):
            sp.wait_ge(sem["zeroed"], 6)
            for into, dram in ((key[0], a["src"]), (key[1], a["dst"]), (run[0], a["edge_weight"])):
                rows = dram.rearrange("(p c) -> p c", c=COLS)
                sp.dma_start(into[0:120, :], rows[0:120, :]).then_inc(sem["keys_in"], 16)
                sp.dma_start(into[120:EP, :], rows[120:EP, :]).then_inc(sem["keys_in"], 16)
            sp.dma_start(X[:, 0:T - 1, :], a["x"][0:(T - 1) * P, :].rearrange("(t p) d -> p t d", p=P)).then_inc(sem["x_in"], 16)
            sp.dma_start(X[0:LAST, T - 1, :], a["x"][(T - 1) * P:, :]).then_inc(sem["x_in"], 16)
            sp.dma_start(W[:, 0:KC, :], a["L0_gnn_W"].rearrange("(m p) d -> p m d", p=P)).then_inc(sem["weights_in"], 16)
            sp.dma_start(bc[:, 0, :], a["L0_gnn_b"].rearrange("(a d) -> a d", a=1).to_broadcast([P, D])).then_inc(sem["weights_in"], 16)
            sp.dma_start(ewW[:, :], a["L3_gnn_ew_W"]).then_inc(sem["weights_in"], 16)
            aw = a["L3_gnn_a_W"].rearrange("n o -> (n o)")
            with nc.allow_non_contiguous_dma(reason="a few hundred words, once"):
                for c, v in ((EWB, a["L3_gnn_ew_b"]), (A3, aw[2 * D:3 * D]), (B1, a["L1_gnn_b1"]),
                             (L2B1, a["L2_gnn_b1"]), (G1, a["L2_gnn_g1"]), (BE1, a["L2_gnn_be1"]),
                             (L2B2, a["L2_gnn_b2"]), (G2, a["L2_gnn_g2"]), (BE2, a["L2_gnn_be2"])):
                    sp.dma_start(col[:, c:c + 2], v.rearrange("(m p) -> p m", p=P)).then_inc(sem["cols_in"], 16)
                for c, v in ((EPS1, a["L1_gnn_eps"]), (EPS2, a["L2_gnn_eps"]), (AB, a["L3_gnn_a_b"])):
                    sp.dma_start(col[:, c:c + 1], v.rearrange("(a d) -> a d", a=1).to_broadcast([P, 1])).then_inc(sem["cols_in"], 16)
            sp.dma_start(rec_src.rearrange("(l s) f -> l s f", l=P), meta_src[:, :, :]).then_inc(sem["fill_in"], 16)
            sp.dma_start(rec_dst.rearrange("(l s) f -> l s f", l=P), meta_dst[:, :, :]).then_inc(sem["fill_in"], 16)

            def store0(b, q, nt):
                wait(sp, sem["y_used"], b + 1)
                rows = table[0][nodes(b, nt * P), :]
                sp.dma_start(rows.rearrange("(t p) d -> p t d", p=P),
                             z1[:, 0:nt * D].rearrange("p (t d) -> p t d", d=D)).then_inc(sem["table_in"], 16)
            batches(sp, store0)

            rows = a["edge_attr_128"].rearrange("(p c) d -> p c d", c=COLS)

            def load_attr(i):
                for u in range(ES):
                    n = i * ES + u
                    wait(sp, sem["attrT_psum"], n - (AR - 1))
                    c = bass.ds(n * EC, EC)
                    sp.dma_start(attr[0:120, u % AR, :, :], rows[0:120, c, :]).then_inc(attr_in[u % AR], 16)
                    sp.dma_start(attr[120:EP, u % AR, :, :], rows[120:EP, c, :]).then_inc(attr_in[u % AR], 16)
            rounds(sp, SITERS, load_attr)

            for k in range(SG):
                sp.wait_ge(scattered[k], 16 * SC * SITERS)
            sp.dma_start(meta_src[:, :, :], rec_src.rearrange("(l s) f -> l s f", l=P)).then_inc(sem["records_in"], 16)
            for k in range(SG):
                sp.wait_ge(scattered[k], 2 * 16 * SC * SITERS)
            sp.dma_start(meta_dst[:, :, :], rec_dst.rearrange("(l s) f -> l s f", l=P)).then_inc(sem["records_in"], 16)

            def load_weights(w1, w2, vectors):
                for j, w in ((0, w1), (KC, w2)):
                    if w is not None:
                        sp.dma_start(W[:, j:j + KC, :], w.rearrange("(m p) d -> p m d", p=P)).then_inc(sem["weights_in"], 16)
                for j, v in enumerate(vectors):
                    sp.dma_start(bc[:, j, :], v.rearrange("(a d) -> a d", a=1).to_broadcast([P, D])).then_inc(sem["weights_in"], 16)

            def store_x(layer, n):
                sp.wait_ge(sem["ln_done"], n)
                sp.dma_start(table[layer].rearrange("(t p) d -> p t d", p=P), X[:, :, :]).then_inc(sem["table_in"], 16)

            store_x(1, 1)
            load_weights(a["L1_gnn_W1"], a["L1_gnn_W2"], (a["L1_gnn_b2"], a["L1_gnn_gamma"], a["L1_gnn_beta"]))
            store_x(2, 3)
            load_weights(a["L2_gnn_W1"], a["L2_gnn_W2"], ())
            sp.wait_ge(sem["ln_done"], 4)
            load_weights(a["L3_gnn_w_W"], None, (a["L3_gnn_w_b"], aw[0:D], aw[D:2 * D]))
            sp.wait_ge(sem["ht_ready"], 1)
            sp.dma_start(table[3].rearrange("(t p) d -> p t d", p=P), ht).then_inc(sem["table_in"], 16)
            sp.wait_ge(sem["ln_done"], 5)
            sp.dma_start(out[0:(T - 1) * P, :].rearrange("(t p) d -> p t d", p=P), X[:, 0:T - 1, :]).then_inc(sem["stored"], 16)
            sp.dma_start(out[(T - 1) * P:, :], X[0:LAST, T - 1, :]).then_inc(sem["stored"], 16)
            sp.wait_ge(sem["stored"], 32)

        @block.gpsimd
        def _(pool):
            pool.memset(ones[:, :], 1.0).then_inc(sem["consts"], 1)
            pool.memset(ident[:, :], 0.0).then_inc(sem["consts"], 1)
            pool.memset(token[:, :], 0.0).then_inc(sem["idx_token"], 1)
            pool.iota(iota[:, :], [[1, P]], base=0, channel_multiplier=0,
                      allow_small_or_imprecise_dtypes=True).then_inc(sem["consts"], 1)
            pool.iota(slot_no[:, :], [[1, SLOTS]], base=0, channel_multiplier=0,
                      allow_small_or_imprecise_dtypes=True).then_inc(sem["consts"], 1)
            pool.wait_ge(sem["consts"], 4)
            pool.affine_select(out=ident[:, :], in_=ident[:, :], compare_op=ALU.not_equal, fill=1.0, base=0,
                               pattern=[[-1, P]], channel_multiplier=1).then_inc(sem["ident_ready"], 1)
            pool.affine_select(out=before[:, :], in_=ones[:, :], compare_op=ALU.is_gt, fill=0.0, base=0,
                               pattern=[[1, P]], channel_multiplier=-1).then_inc(sem["ident_ready"], 1)
            record_bound = pool.to_reg(RECORDS - 1)
            node_bound = pool.to_reg(N_NODES - 1)

            def hold(before_this, ready, n):
                pool.wait_ge(sem["idx_token"], before_this)
                pool.wait_ge(ready, n)
                pool.tensor_tensor(token[0:1, :], token[0:1, :], token[0:1, :], ALU.add).then_inc(sem["idx_token"], 1)

            def scatter(n, dram, fields):
                with pool.Fori(0, SITERS) as i:
                    for k in range(SG):
                        g = i * SG + (n * SITERS * SG + k)
                        hold(g + 1, sem["scat_ready"], g * 2 + 2)
                        for c in range(SC):
                            pool.indirect_dma_start(
                                dram, bass.IndirectOffsetOnAxis(ap=sidx[:, k, c:c + 1], axis=0),
                                spay[:, k, c, 0:fields], None,
                                bounds_check=record_bound, oob_is_err=False).then_inc(scattered[k], 16)

            def gather(layer):
                width = HW if layer == 3 else D
                pool.wait_ge(sem["table_in"], TABLE_IN[layer])
                if layer == 0:
                    pool.wait_ge(sem["acc_zero"], 1)
                with pool.Fori(0, ITERS) as i:
                    for k in range(RG):
                        g = i * RG + (layer * GROUPS + k)
                        hold(g + (2 * SITERS * SG + 1), sem["idx_ready"], g + 1)
                        for j in range(G):
                            pool.indirect_dma_start(
                                ring[:, k * G + j, 0:width], None, table[layer],
                                bass.IndirectOffsetOnAxis(ap=gidx[:, k, j:j + 1], axis=0),
                                bounds_check=node_bound, oob_is_err=False).then_inc(gathered[k], 16)

            pool.wait_ge(sem["fill_in"], 32)
            scatter(0, rec_src, 4)
            scatter(1, rec_dst, 2)
            for layer in range(4):
                gather(layer)

        @block.scalar
        def _(act):
            def copy_xT(phase, used, used0):
                def body(b, q, nt):
                    wait(act, sem["xT_psum"], b + (phase * NB + 1))
                    wait(act, sem[used], b + (used0 - 1))
                    for k in range(KC):
                        nc.scalar.copy(xT[:, q, k, 0:nt * P], ps[:, 2 * q + k, 0:nt * P]).then_inc(sem["xT_sbuf"], 1)
                return body

            act.wait_ge(sem["wT_psum"], 1)
            act.wait_ge(sem["weights_in"], WEIGHTS[0])
            nc.scalar.copy(W[:, KC:2 * KC, :], ps[:, 6, :].rearrange("p (k d) -> p k d", k=KC)).then_inc(sem["wT_ready"], 1)
            batches(act, copy_xT(0, "y_psum", YB[0]))

            act.wait_ge(sem["cols_in"], 16 * 12)
            act.wait_ge(sem["table_in"], TABLE_IN[0])
            act.wait_ge(sem["ew_psum"], 1)
            nc.scalar.copy(z1[:, 0:D], ps[:, 6, 0:D]).then_inc(sem["lin_ready"], 1)
            nc.scalar.activation(lin[:, 0:2], col[:, A3:A3 + 2], ACT.Copy, scale=1.0 - SLOPE).then_inc(sem["lin_ready"], 1)
            act.wait_ge(sem["ew_psum"], 2)
            nc.scalar.activation(lin[:, 2:4], ps[:, 6, D:D + 2], ACT.Copy, scale=SLOPE).then_inc(sem["lin_ready"], 1)
            act.wait_ge(sem["lin_ready"], 3)
            def edge_step(n, u):
                q = u % 2
                wait(act, sem["attrT_psum"], n + 1)
                wait(act, sem["logit_psum"], n - 1)
                nc.scalar.copy(xT[:, q, 0, :], ps[:, q, :]).then_inc(sem["attrT_sbuf"], 1)
                wait(act, sem["ez_psum"], n + 1)
                for m, lr in enumerate((z1[:, q * 512:q * 512 + 512], xT[:, q, 1, :])):
                    nc.scalar.activation(lr, ps[:, 2 + 2 * q + m, :], ACT.Relu,
                                         bias=col[:, EWB + m:EWB + m + 1]).then_inc(sem["lr_ready"], 1)
                wait(act, sem["logit_psum"], n + 1)
                c = bass.ds(n * EC, EC)
                nc.scalar.activation(pay_src[:, c, 3], ps[:, 6 + q, 0:EC], ACT.Identity,
                                     bias=lin[:, 3:4]).then_inc(sem["pay_ready"], 1)

            def hand_scatter(n, i, fields):
                for k in range(SG):
                    wait(act, scattered[k], i * (16 * SC) + n * 16 * SC * SITERS)
                    c = bass.ds(i * (SG * SC) + k * SC, SC)
                    nc.scalar.copy(sidx[:, k, :], rec_of[n][:, c]).then_inc(sem["scat_ready"], 1)
                    nc.scalar.copy(spay[:, k, :, 0:fields], pay[n][:, c, :]).then_inc(sem["scat_ready"], 1)

            def edge_round(i):
                for u in range(ES):
                    edge_step(i * ES + u, u)
                wait(act, sem["record_ready"], 1)
                wait(act, sem["pay_ready"], (i + 1) * ES)
                hand_scatter(0, i, 4)
            rounds(act, SITERS, edge_round)
            act.wait_ge(sem["record_ready"], 2)
            rounds(act, SITERS, lambda i: hand_scatter(1, i, 2), first=False)

            def hand_gather(layer, i):
                for k in range(RG):
                    wait(act, sem["summed"], i * R + (layer * SLOTS + (k - RG + 1) * G))
                    src = meta[layer][:, bass.ds(i * R + k * G, G), 0].bitcast(I32)
                    nc.scalar.copy(gidx[:, k, :], src).then_inc(sem["idx_ready"], 1)

            def square(n):
                act.wait_ge(sem["ln_center"], n)
                nc.scalar.activation(zt3, accd, ACT.Square).then_inc(sem["ln_square"], 1)
                act.wait_ge(sem["ln_var"], n)
                nc.scalar.activation(small[:, 4, :], small[:, 3, :], ACT.Sqrt).then_inc(sem["ln_sqrt"], 1)

            act.wait_ge(sem["records_in"], 32)
            rounds(act, ITERS, lambda i: hand_gather(0, i))
            square(1)
            rounds(act, ITERS, lambda i: hand_gather(1, i), first=False)

            def mlp1(b, q, nt):
                copy_xT(1, "z_psum", ZB[1])(b, q, nt)
                wait(act, sem["z_psum"], b + 1)
                wait(act, sem["y_psum"], b + YB[1])
                for m in range(KC):
                    nc.scalar.activation(z1[:, m * 512:m * 512 + nt * P], ps[:, 4 + m, 0:nt * P], ACT.Relu,
                                         bias=col[:, B1 + m:B1 + m + 1]).then_inc(sem["z_sbuf"], 1)
            batches(act, mlp1)
            square(2)
            square(3)
            rounds(act, ITERS, lambda i: hand_gather(2, i), first=False)

            def lin2(which):
                def body(b, q, nt):
                    if which == 0:
                        copy_xT(2, "z_psum", ZB[2])(b, q, nt)
                    wait(act, sem["z_psum"], b + (ZB[2] + which * NB + 1))
                    bcol = (L2B1, L2B2)[which]
                    for m in range(KC):
                        nc.scalar.activation(ztf[:, m, nodes(b, nt * P)], ps[:, 4 + m, 0:nt * P], ACT.Identity,
                                             bias=col[:, bcol + m:bcol + m + 1]).then_inc(sem["z_sbuf"], 1)
                return body

            def norm2(which):
                act.wait_ge(sem["bn_var"], which + 1)
                nc.scalar.activation(mv[:, :, 3], mv[:, :, 2], ACT.Sqrt).then_inc(sem["bn_sqrt"], 1)
                act.wait_ge(sem["bn_scale"], which + 1)
                for m in range(KC):
                    nc.scalar.activation(ztf[:, m, :], ztf[:, m, :], ACT.Relu, bias=mv[:, m, 6:7],
                                         scale=mv[:, m, 5:6]).then_inc(sem["bn_applied"], 1)
            for which in range(2):
                batches(act, lin2(which))
                norm2(which)
            square(4)
            batches(act, copy_xT(3, "y_psum", YB[3]))
            def attend(g, k):
                q = k % 2
                wait(act, sem["bias_ready"], g * 2 + 2)
                wait(act, sem["added"], g * G + (3 * SLOTS - G))
                nc.scalar.activation(corr[:, q, :], att[:, 4, :], ACT.Exp).then_inc(sem["corr_ready"], 1)
                wait(act, sem["p_psum"], g)
                for j in range(G):
                    nc.scalar.activation(probT[:, j, :], psf[:, 4 * 512 + j * P:4 * 512 + (j + 1) * P], ACT.Exp,
                                         bias=bias[:, q, j:j + 1]).then_inc(sem["probT_ready"], 1)
                wait(act, sem["p_psum"], g + 1)
                wait(act, sem["summed"], g * G + (3 * SLOTS - G))
                nc.scalar.copy(sel[:, q, :, :].rearrange("p s e -> p (s e)"), psf[:, 6 * 512:8 * 512]).then_inc(sem["sel_ready"], 1)

            def attend_round(i, last=False):
                for k in range(RG):
                    if not last or k < RG - 1:
                        attend(i * RG + k + 1, (k + 1) % RG)
                    if not last:
                        wait(act, sem["summed"], i * R + (3 * SLOTS + (k + 1) * G))
                        src = meta_src[:, bass.ds(i * R + (R + k * G), G), 0].bitcast(I32)
                        nc.scalar.copy(gidx[:, k, :], src).then_inc(sem["idx_ready"], 1)

            hand_gather(3, 0)
            attend(0, 0)
            attend_round(0)
            with act.Fori(1, ITERS - 1) as i:
                attend_round(i)
            attend_round(ITERS - 1, last=True)
            square(5)

        @block.tensor
        def _(pe):
            def counts(n):
                pe.wait_ge(sem["counted"], (n + 1) * T)
                pe.wait_ge(sem["ident_ready"], 2)
                nc.tensor.matmul(ps[:, 7, 0:T], before[:, :], small[:, n, :], start=True, stop=True)
                nc.tensor.matmul(ps[:, 7, 64:64 + T], ones[:, :], small[:, n, :], start=True, stop=True).then_inc(sem["prefix"], 1)

            def end_columns(n):
                pe.wait_ge(sem["ends_ready"], n + 1)
                for j in range(2):
                    mm = nc.tensor.matmul(ps[0:T, 7, 128 + j:129 + j], ends[0:1, n, j, :], ones[0:1, 0:1],
                                          start=True, stop=True)
                mm.then_inc(sem["endT_psum"], 1)

            def slot_tiles(n):
                pe.wait_ge(sem["past_ready"], n + 1)
                h = SLOTS // 2
                nc.tensor.matmul(ps[:, 7, 0:h], ones[0:T, :], past[0:T, 0:h], start=True, stop=True).then_inc(sem["tile_psum"], 1)
                pe.wait_ge(sem["tile_ready"], 2 * n + 1)
                nc.tensor.matmul(ps[:, 7, 0:h], ones[0:T, :], past[0:T, h:], start=True, stop=True).then_inc(sem["tile_psum"], 1)

            def turn(phase, view):
                def body(b, q, nt):
                    wait(pe, sem["xT_sbuf"], b * 2 + (2 * phase * NB - 2))
                    src = tiles(view, b, nt)
                    for k in range(KC):
                        for j in range(nt):
                            mm = nc.tensor.transpose(ps[:, 2 * q + k, j * P:(j + 1) * P],
                                                     src[:, j, k * P:(k + 1) * P], ident[:, :])
                    mm.then_inc(sem["xT_psum"], 1)
                return body

            def rows_out(b, nt, lhs, w0, b0, used0):
                wait(pe, sem["y_used"], b + used0)
                for j in range(nt):
                    for k in range(KC):
                        mm = nc.tensor.matmul(ps[:, b0 + j // 2, (j % 2) * D:(j % 2 + 1) * D], lhs(k, j),
                                              W[:, w0 + k, :], start=(k == 0), stop=(k == KC - 1))
                mm.then_inc(sem["y_psum"], 1)

            def columns_out(b, nt, rhs, w0, batch0):
                wait(pe, sem["z_sbuf"], b * 2 + 2 * batch0)
                for m in range(KC):
                    for k in range(KC):
                        mm = nc.tensor.matmul(ps[:, 4 + m, 0:nt * P], W[:, w0 + k, m * P:(m + 1) * P], rhs(k),
                                              start=(k == 0), stop=(k == KC - 1))
                mm.then_inc(sem["z_psum"], 1)

            counts(0)
            pe.wait_ge(sem["weights_in"], WEIGHTS[0])
            for k in range(KC):
                for m in range(KC):
                    mm = nc.tensor.transpose(ps[:, 6, k * D + m * P:k * D + (m + 1) * P],
                                             W[:, m, k * P:(k + 1) * P], ident[:, :])
            mm.then_inc(sem["wT_psum"], 1)
            pe.wait_ge(sem["wT_ready"], 1)
            pe.wait_ge(sem["x_in"], 32)
            pe.wait_ge(sem["zeroed"], 6)

            def first_rows(b, q, nt):
                turn(0, X)(b, q, nt)
                wait(pe, sem["xT_sbuf"], b * 2 + 2)
                rows_out(b, nt, lambda k, j: xT[:, q, k, j * P:(j + 1) * P], KC, 4, YB[0])
            each_batch(first_rows)
            end_columns(0)
            slot_tiles(0)

            pe.wait_ge(sem["cols_in"], 16 * 12)
            for m in range(KC):
                mm = nc.tensor.transpose(ps[:, 6, m * P:(m + 1) * P], ewW[:, m * P:(m + 1) * P], ident[:, :])
            mm.then_inc(sem["ew_psum"], 1)
            pe.wait_ge(sem["lin_ready"], 1)
            for j in range(2):
                for m in range(KC):
                    lhs = z1[:, m * P:(m + 1) * P] if j == 0 else col[:, EWB + m:EWB + m + 1].to_broadcast([P, P])
                    mm = nc.tensor.matmul(ps[:, 6, D + j:D + j + 1], lhs, col[:, A3 + m:A3 + m + 1],
                                          start=(m == 0), stop=(m == KC - 1))
            mm.then_inc(sem["ew_psum"], 1)
            pe.wait_ge(sem["lin_ready"], 3)
            pe.wait_ge(sem["y_used"], NB)
            pe.wait_ge(sem["tile_ready"], 2)

            def edge_round(i):
                for u in range(ES):
                    q, n = u % 2, i * ES + u
                    wait(pe, attr_in[u % AR], i * (32 * ES // AR) + 32 * (u // AR + 1))
                    wait(pe, sem["attrT_sbuf"], n - 1)
                    for j in range(EC):
                        mm = nc.tensor.transpose(ps[:, q, j * P:(j + 1) * P], attr[:, u % AR, j, :], ident[:, :])
                    mm.then_inc(sem["attrT_psum"], 1)
                    wait(pe, sem["attrT_sbuf"], n + 1)
                    wait(pe, sem["lr_ready"], n * 2 - 2)
                    for m in range(KC):
                        mm = nc.tensor.matmul(ps[:, 2 + 2 * q + m, :], ewW[:, m * P:(m + 1) * P], xT[:, q, 0, :],
                                              start=True, stop=True)
                    mm.then_inc(sem["ez_psum"], 1)
                    wait(pe, sem["lr_ready"], n * 2 + 2)
                    wait(pe, sem["pay_ready"], n - 1)
                    for j in range(EC):
                        for m, lhs in enumerate((z1[:, q * 512:q * 512 + 512], xT[:, q, 1, :], xT[:, q, 0, :])):
                            mm = nc.tensor.matmul(ps[:, 6 + q, j:j + 1], lhs[:, j * P:(j + 1) * P],
                                                  lin[:, m:m + 1], start=(m == 0), stop=(m == KC))
                    mm.then_inc(sem["logit_psum"], 1)
            edge_round(0)
            with pe.Fori(1, SITERS // 2) as i:
                edge_round(i)
            pe.wait_ge(sem["pay_ready"], SITERS // 2 * ES)
            counts(1)
            pe.wait_ge(sem["prefix_out"], 2)
            with pe.Fori(SITERS // 2, SITERS) as i:
                edge_round(i)
            pe.wait_ge(sem["pay_ready"], ESTEPS)
            end_columns(1)
            slot_tiles(1)

            def aggregate(layer, i, width=D):
                for k in range(RG):
                    slot_sums(layer, i * RG + k, i, k, width)

            def slot_sums(layer, g, i, k, width):
                wait(pe, gathered[k], i * (16 * G) + (layer * ITERS + 1) * 16 * G)
                wait(pe, sem["sel_ready"], g + (layer * GROUPS + 1))
                for j in range(G):
                    n = g * G + (layer * SLOTS + j)
                    wait(pe, sem["added"], n - 3)
                    nc.tensor.matmul(ps[:, j % 4, 0:width], sel[:, k % 2, j, :], ring[:, k * G + j, 0:width],
                                     start=True, stop=True).then_inc(sem["summed"], 1)

            rounds(pe, ITERS, lambda i: aggregate(0, i))
            rounds(pe, ITERS, lambda i: aggregate(1, i), first=False)
            pe.wait_ge(sem["agg_ready"], 1)
            pe.wait_ge(sem["weights_in"], WEIGHTS[1])

            def mlp1(b, q, nt):
                turn(1, accd)(b, q, nt)
                wait(pe, sem["xT_sbuf"], b * 2 + (2 * NB + 2))
                columns_out(b, nt, lambda k: xT[:, q, k, 0:nt * P], 0, ZB[1])
                wait(pe, sem["z_sbuf"], b * 2 + 2)
                rows_out(b, nt, lambda k, j: z1[:, k * 512 + j * P:k * 512 + (j + 1) * P], KC, 6, YB[1])
            each_batch(mlp1)
            rounds(pe, ITERS, lambda i: aggregate(2, i), first=False)
            pe.wait_ge(sem["agg_ready"], 2)
            pe.wait_ge(sem["weights_in"], WEIGHTS[2])

            def lin2a(b, q, nt):
                turn(2, accd)(b, q, nt)
                wait(pe, sem["xT_sbuf"], b * 2 + (4 * NB + 2))
                columns_out(b, nt, lambda k: xT[:, q, k, 0:nt * P], 0, ZB[2])
            each_batch(lin2a)
            pe.wait_ge(sem["bn_applied"], KC)
            each_batch(lambda b, q, nt: columns_out(b, nt, lambda k: ztf[:, k, nodes(b, nt * P)], KC, ZB["2b"]))
            pe.wait_ge(sem["bn_applied"], 2 * KC)

            def turn_back(b, q, nt):
                wait(pe, sem["back_used"], b - 1)
                for j in range(nt):
                    for k in range(KC):
                        c = (j % 2) * D + k * P
                        src = ztf[:, k, nodes(b, nt * P)][:, j * P:(j + 1) * P]
                        mm = nc.tensor.transpose(ps[:, 2 * q + j // 2, c:c + P], src, ident[:, :])
                mm.then_inc(sem["back_psum"], 1)
            each_batch(turn_back)
            pe.wait_ge(sem["ln_done"], 4)
            pe.wait_ge(sem["weights_in"], WEIGHTS[3])

            def node_rows(b, q, nt):
                turn(3, X)(b, q, nt)
                wait(pe, sem["xT_sbuf"], b * 2 + (6 * NB + 2))
                rows_out(b, nt, lambda k, j: xT[:, q, k, j * P:(j + 1) * P], 0, 4, YB[3])
            each_batch(node_rows)
            pe.wait_ge(sem["s1_ready"], 1)
            nc.tensor.transpose(ps[0:T, 6, 0:P], s1[:, :], ident[:, :]).then_inc(sem["c_psum"], 1)
            pe.wait_ge(sem["c_ready"], 1)
            h = SLOTS // 2
            for j in range(2):
                nc.tensor.matmul(ps[:, 4 + j, 0:h], before[0:T, :], reset[0:T, j * h:(j + 1) * h], start=True,
                                 stop=True).then_inc(sem["c_psum"], 1)
            pe.wait_ge(sem["c_ready"], 4)

            def turn_logits(g):
                wait(pe, sem["mask_logit"], g + 1)
                wait(pe, sem["probT_ready"], g * G)
                for j in range(G):
                    mm = nc.tensor.transpose(psf[:, 4 * 512 + j * P:4 * 512 + (j + 1) * P], logit[:, j, :], ident[:, :])
                mm.then_inc(sem["t_psum"], 1)

            def turn_probs(g):
                wait(pe, sem["probT_ready"], (g + 1) * G)
                wait(pe, sem["sel_ready"], g + 3 * GROUPS)
                for j in range(G):
                    mm = nc.tensor.transpose(psf[:, 6 * 512 + j * P:6 * 512 + (j + 1) * P], probT[:, j, :], ident[:, :])
                mm.then_inc(sem["p_psum"], 1)

            turn_logits(0)
            turn_probs(0)
            turn_logits(1)

            def attend_round(i, last=False):
                for k in range(RG):
                    g = i * RG + k
                    slot_sums(3, g, i, k, AW)
                    if not last or g + 1 < GROUPS:
                        turn_probs(g + 1)
                    if not last or g + 2 < GROUPS:
                        turn_logits(g + 2)
            attend_round(0)
            with pe.Fori(1, ITERS - 1) as i:
                attend_round(i)
            attend_round(ITERS - 1, last=True)

        @block.vector
        def _(dve):
            chain = [0]

            def link(ins):
                chain[0] += 1
                ins.then_inc(sem["dve_chain"], 1)
                dve.wait_ge(sem["dve_chain"], chain[0])

            v = nc.vector
            link(v.memset(X[:, T - 1, :], 0.0))
            v.memset(key[0][96:P, :], NO_NODE).then_inc(sem["zeroed"], 1)
            v.memset(key[1][96:P, :], NO_NODE).then_inc(sem["zeroed"], 1)
            v.memset(run[0][96:P, :], 0.0).then_inc(sem["zeroed"], 1)
            v.memset(attr[96:P, :, :, :], 0.0).then_inc(sem["zeroed"], 1)
            for rec in (meta_src, meta_dst):
                link(v.memset(rec[:, :, :], 0.0))
                link(v.memset(rec[:, :, 0].bitcast(I32), OUT_OF_RANGE))
                v.memset(rec[:, :, 1], -1.0).then_inc(sem["zeroed"], 1)
            dve.wait_ge(sem["keys_in"], 96)
            dve.wait_ge(sem["consts"], 4)
            link(v.tensor_copy(pay_src[:, :, 2], run[0]))
            link(v.tensor_copy(pay_src[:, :, 0].bitcast(I32), key[1]))
            link(v.tensor_copy(pay_dst[:, :, 0].bitcast(I32), key[0]))

            def sort_edges(n):
                link(v.tensor_scalar(ibuf, key[n], 7, None, ALU.arith_shift_right))
                link(v.tensor_copy(bucket, ibuf))
                link(v.tensor_scalar(rec_of[n], key[n], P - 1, None, ALU.bitwise_and))
                link(v.tensor_copy(pay[n][:, :, 1], rec_of[n]))
                link(v.memset(pos, float(NOWHERE)))
                with dve.Fori(0, T) as b:
                    v.tensor_scalar(mask[:, bass.ds(b, 1), :].rearrange("p o c -> p (o c)"), bucket,
                                    iota[:, bass.ds(b, 1)], None, ALU.is_equal, ALU.add,
                                    accum_out=small[:, n, bass.ds(b, 1)]).then_inc(sem["counted"], 1)
                dve.wait_ge(sem["prefix"], n + 1)
                link(v.tensor_copy(small[:, 5, :], ps[:, 7, 0:T]))
                v.tensor_copy(small[:, 2, :], ps[:, 7, 64:64 + T]).then_inc(sem["prefix_out"], 1)
                dve.wait_ge(sem["prefix_out"], n + 1)
                link(v.tensor_scalar(small[:, 3, :].bitcast(I32), small[:, 2, :], float(P - 1), None, ALU.add))
                link(v.tensor_scalar(small[:, 3, :].bitcast(I32), small[:, 3, :].bitcast(I32), 7, None, ALU.arith_shift_right))
                link(v.tensor_copy(small[:, 4, :], small[:, 3, :].bitcast(I32)))
                link(v.tensor_tensor_scan(ends[:, n, 0, :], ones[:, 0:T], small[:, 4, :], 0.0, ALU.mult, ALU.add))
                v.tensor_tensor(ends[:, n, 1, :], ends[:, n, 0, :], small[:, 4, :], ALU.subtract).then_inc(sem["ends_ready"], 1)
                dve.wait_ge(sem["ends_ready"], n + 1)
                link(v.scalar_tensor_tensor(small[:, 5, :], ends[:, n, 1, :], float(P), small[:, 5, :], ALU.mult, ALU.add))
                link(v.tensor_scalar(small[:, 5, :], small[:, 5, :], -1.0, None, ALU.add))

                for b in range(T):
                    wait(dve, sem["ranked"], n * T + b - 1)
                    v.tensor_tensor_scan(run[b % 2], ones[:, 0:1].to_broadcast([P, COLS]), mask[:, b, :],
                                         small[:, 5, b:b + 1], ALU.mult, ALU.add).then_inc(sem["scanned"], 1)
                    dve.wait_ge(sem["scanned"], n * T + b + 1)
                    wait(dve, sem["ranked"], n * T + b)
                    v.copy_predicated(pos, mask[:, b, :], run[b % 2]).then_inc(sem["ranked"], 1)
                dve.wait_ge(sem["ranked"], (n + 1) * T)
                lane, slot = run[0].bitcast(I32), run[1].bitcast(I32)
                link(v.tensor_copy(ibuf, pos))
                link(v.tensor_scalar(lane, ibuf, P - 1, None, ALU.bitwise_and))
                link(v.tensor_scalar(slot, ibuf, 7, None, ALU.arith_shift_right))
                v.scalar_tensor_tensor(rec_of[n], lane, float(SLOTS), slot, ALU.mult, ALU.add).then_inc(sem["record_ready"], 1)
                dve.wait_ge(sem["record_ready"], n + 1)

            def tiles_of_slots(n, into):
                dve.wait_ge(sem["endT_psum"], n + 1)
                v.tensor_copy(endT[0:T, n, :], ps[0:T, 7, 128:130]).then_inc(sem["endT_ready"], 1)
                dve.wait_ge(sem["endT_ready"], n + 1)
                v.tensor_scalar(past[0:T, :], slot_no[0:T, :], endT[0:T, n, 0:1], None, ALU.is_ge).then_inc(sem["past_ready"], 1)
                h = SLOTS // 2
                for j in range(2):
                    dve.wait_ge(sem["tile_psum"], 2 * n + j + 1)
                    v.tensor_scalar(into[:, j * h:(j + 1) * h], ps[:, 7, 0:h], float(T - 1), None,
                                    ALU.min).then_inc(sem["tile_ready"], 1)

            def rows_from(bank, b, nt, into, add, signal):
                src = psf[:, 512 * bank:512 * bank + nt * D].rearrange("p (t d) -> p t d", d=D)
                v.tensor_tensor(into, src, add, ALU.add).then_inc(sem[signal], 1)

            dve.wait_ge(sem["weights_in"], WEIGHTS[0])

            def stage0(b, q, nt):
                wait(dve, sem["y_psum"], b + 1)
                wait(dve, sem["table_in"], b * 16)
                rows_from(4, b, nt, z1[:, 0:nt * D].rearrange("p (t d) -> p t d", d=D),
                          bc[:, 0:1, :].to_broadcast([P, nt, D]), "y_used")

            sort_edges(0)
            batches(dve, stage0)
            tiles_of_slots(0, tile_src)
            sort_edges(1)
            tiles_of_slots(1, tile_dst)
            for k in range(SG):
                dve.wait_ge(scattered[k], 2 * 16 * SC * SITERS)
            dve.wait_ge(sem["logit_psum"], ESTEPS)
            link(v.memset(ACC[:, :], 0.0))
            v.memset(ZT[:, :], 0.0).then_inc(sem["acc_zero"], 1)
            dve.wait_ge(sem["acc_zero"], 1)

            def select(layer, i, k, first_group=False):
                g = i * RG + k
                wait(dve, sem["summed"], g * G + (layer * SLOTS - G))
                m = meta[layer]
                c0 = i * R + k * G
                if layer != 2:
                    v.tensor_tensor(sel[:, k % 2, :, :], iota[:, :].rearrange("p (o e) -> p o e", o=1).to_broadcast([P, G, P]),
                                    m[:, bass.ds(c0, G), 1:2].to_broadcast([P, G, P]), ALU.is_equal).then_inc(sem["sel_ready"], 1)
                else:
                    for j in range(G):
                        e = m[:, bass.ds(c0 + j, 1), :]
                        ins = v.tensor_scalar(sel[:, k % 2, j, :], iota[:, :], e[:, 0, 1:2], e[:, 0, 2:3],
                                              ALU.is_equal, ALU.mult)
                    ins.then_inc(sem["sel_ready"], 1)

            def accumulate(layer, i, k):
                for j in range(G):
                    c = i * R + (k * G + j)
                    n = c + layer * SLOTS
                    t = dve.value_load(slot_tile[layer][0:1, bass.ds(c, 1)], min_val=0, max_val=T - 1)
                    dst = acc3[:, bass.ds(t, 1), 0:D].rearrange("p o d -> p (o d)")
                    wait(dve, sem["added"], n)
                    wait(dve, sem["summed"], n + 1)
                    v.tensor_tensor(dst, ps[:, j % 4, 0:D], dst, ALU.add).then_inc(sem["added"], 1)

            def aggregate(layer, i, last=False):
                for k in range(RG):
                    if not (last and k == RG - 1):
                        if k < RG - 1:
                            select(layer, i, k + 1)
                        else:
                            select(layer, i + 1, 0)
                    accumulate(layer, i, k)

            def aggregate_all(layer):
                select(layer, 0, 0)
                if layer == 0:
                    aggregate(layer, 0)
                with dve.Fori(1 if layer == 0 else 0, ITERS - 1) as i:
                    aggregate(layer, i)
                aggregate(layer, ITERS - 1, last=True)
                dve.wait_ge(sem["added"], (layer + 1) * SLOTS)

            def by_tile(vec):
                return vec.rearrange("p (t o) -> p t o", o=1).to_broadcast([P, T, D])

            def by_feature(vec):
                return vec.rearrange("p (o d) -> p o d", o=1).to_broadcast([P, T, D])

            def layer_norm(n, affine):
                link(v.tensor_reduce(small[:, 0, :], accd, AX_X, ALU.add))
                link(v.tensor_scalar(small[:, 1, :], small[:, 0, :], 1.0 / D, None, ALU.mult))
                v.tensor_tensor(accd, accd, by_tile(small[:, 1, :]), ALU.subtract).then_inc(sem["ln_center"], 1)
                dve.wait_ge(sem["ln_square"], n)
                link(v.tensor_reduce(small[:, 2, :], zt3, AX_X, ALU.add))
                v.tensor_scalar(small[:, 3, :], small[:, 2, :], 1.0 / D, LN_EPS, ALU.mult, ALU.add).then_inc(sem["ln_var"], 1)
                dve.wait_ge(sem["ln_sqrt"], n)
                link(v.reciprocal(small[:, 5, :], small[:, 4, :]))
                if not affine:
                    v.tensor_tensor(X[:, :, :], accd, by_tile(small[:, 5, :]), ALU.mult).then_inc(sem["ln_done"], 1)
                    dve.wait_ge(sem["ln_done"], n)
                    return
                link(v.tensor_tensor(accd, accd, by_tile(small[:, 5, :]), ALU.mult))
                link(v.tensor_tensor(accd, accd, by_feature(bc[:, 1, :]), ALU.mult))
                link(v.tensor_tensor(accd, accd, by_feature(bc[:, 2, :]), ALU.add))
                v.scalar_tensor_tensor(accd, accd, 0.0, X[:, :, :], ALU.max, ALU.add).then_inc(sem["ln_done"], 1)
                dve.wait_ge(sem["ln_done"], n)

            dve.wait_ge(sem["records_in"], 32)
            aggregate_all(0)
            link(v.tensor_tensor(accd, accd, X[:, :, :], ALU.add))
            layer_norm(1, False)
            link(v.memset(ACC[:, :], 0.0))
            aggregate_all(1)
            link(v.tensor_scalar(small[:, 0, 0:2], col[:, EPS1:EPS2 + 1], 1.0, None, ALU.add))
            v.scalar_tensor_tensor(accd, X[:, :, :], small[:, 0, 0:1], accd, ALU.mult, ALU.add).then_inc(sem["agg_ready"], 1)
            dve.wait_ge(sem["weights_in"], WEIGHTS[1])

            def mlp1(b, q, nt):
                wait(dve, sem["y_psum"], b + (YB[1] + 1))
                rows_from(6, b, nt, tiles(accd, b, nt), tiles(X[:, :, :], b, nt), "y_used")
            batches(dve, mlp1)
            dve.wait_ge(sem["y_used"], YB[1] + NB)
            link(v.tensor_tensor(accd, accd, by_feature(bc[:, 0, :]), ALU.add))
            layer_norm(2, True)
            layer_norm(3, False)
            link(v.memset(ACC[:, :], 0.0))
            aggregate_all(2)
            link(v.tensor_scalar(small[:, 0, 0:2], col[:, EPS1:EPS2 + 1], 1.0, None, ALU.add))
            v.scalar_tensor_tensor(accd, X[:, :, :], small[:, 0, 1:2], accd, ALU.mult, ALU.add).then_inc(sem["agg_ready"], 1)
            for which, (g, be) in enumerate(((G1, BE1), (G2, BE2))):
                def gather_stats(b, q, nt):
                    wait(dve, sem["z_sbuf"], b * 2 + 2 * (ZB[2] + which * NB + 1))
                    n = nt * P if not isinstance(b, int) else min(nt * P, N_NODES - b * SB * P)
                    for m in range(KC):
                        v.bn_stats(stats[:, m, bass.ds(b, 1), :].rearrange("p o s -> p (o s)"),
                                   ztf[:, m, nodes(b, n)]).then_inc(sem["bn_in"], 1)
                if which:
                    dve.wait_ge(sem["bn_applied"], KC)
                batches(dve, gather_stats)
                dve.wait_ge(sem["bn_in"], (which + 1) * NB * KC)
                for m in range(KC):
                    link(v.bn_aggr(mv[:, m, 0:2], stats[:, m, :, :].rearrange("p b s -> p (b s)")))
                v.tensor_scalar(mv[:, :, 2], mv[:, :, 1], BN_EPS, None, ALU.add).then_inc(sem["bn_var"], 1)
                dve.wait_ge(sem["bn_sqrt"], which + 1)
                link(v.reciprocal(mv[:, :, 4], mv[:, :, 3]))
                link(v.tensor_tensor(mv[:, :, 5], mv[:, :, 4], col[:, g:g + 2], ALU.mult))
                link(v.tensor_tensor(mv[:, :, 7], mv[:, :, 0], mv[:, :, 5], ALU.mult))
                v.tensor_tensor(mv[:, :, 6], col[:, be:be + 2], mv[:, :, 7], ALU.subtract).then_inc(sem["bn_scale"], 1)
                dve.wait_ge(sem["bn_scale"], which + 1)

            def back(b, q, nt):
                wait(dve, sem["back_psum"], b + 1)
                rows_from(2 * q, b, nt, tiles(accd, b, nt), tiles(X[:, :, :], b, nt), "back_used")
            batches(dve, back)
            dve.wait_ge(sem["back_used"], NB)
            layer_norm(4, False)
            dve.wait_ge(sem["weights_in"], WEIGHTS[3])

            def node_rows(b, q, nt):
                wait(dve, sem["y_psum"], b + (YB[3] + 1))
                wait(dve, sem["ln_square"], 4)
                rows_from(4, b, nt, tiles(ht, b, nt)[:, :, 0:D], bc[:, 0:1, :].to_broadcast([P, nt, D]), "y_used")
            batches(dve, node_rows)
            dve.wait_ge(sem["y_used"], YB[3] + NB)
            link(v.memset(ht[:, :, D:D + 1], 1.0))
            link(v.scalar_tensor_tensor(ht[:, :, 0:D], ht[:, :, 0:D], SLOPE, ht[:, :, 0:D], ALU.mult, ALU.max))
            link(v.tensor_tensor(accd, ht[:, :, 0:D], by_feature(bc[:, 1, :]), ALU.mult))
            link(v.tensor_reduce(s1[:, :], accd, AX_X, ALU.add))
            v.tensor_scalar(s1[:, :], s1[:, :], col[:, AB:AB + 1], None, ALU.add).then_inc(sem["s1_ready"], 1)
            link(v.tensor_tensor(accd, ht[:, :, 0:D], by_feature(bc[:, 2, :]), ALU.mult))
            link(v.tensor_reduce(s2[:, :], accd, AX_X, ALU.add))
            v.tensor_copy(ht[:, :, D + 1], s2[:, :]).then_inc(sem["ht_ready"], 1)
            link(v.tensor_scalar(cslot[0:T, :], slot_no[0:T, :], endT[0:T, 0, 0:1], None, ALU.is_ge))
            link(v.tensor_scalar(reset[0:T, :], slot_no[0:T, :], endT[0:T, 0, 1:2], None, ALU.is_ge))
            link(v.tensor_tensor(reset[0:T, :], reset[0:T, :], cslot[0:T, :], ALU.subtract))
            dve.wait_ge(sem["c_psum"], 1)
            v.tensor_copy(before[0:T, :], ps[0:T, 6, 0:P]).then_inc(sem["c_ready"], 1)
            h = SLOTS // 2
            for j in range(2):
                dve.wait_ge(sem["c_psum"], 2 + j)
                v.tensor_copy(cslot[:, j * h:(j + 1) * h], ps[:, 4 + j, 0:h]).then_inc(sem["c_ready"], 1)
            link(v.memset(reset[:, 0:1], -BIG))
            link(v.tensor_tensor(reset[:, 1:], tile_src[:, 1:], tile_src[:, 0:SLOTS - 1], ALU.not_equal))
            link(v.tensor_scalar(reset[:, 1:], reset[:, 1:], -BIG, None, ALU.mult))
            link(v.memset(ACC[:, :], 0.0))
            v.memset(runmax[:, :, :], FLOOR).then_inc(sem["c_ready"], 1)
            dve.wait_ge(sem["c_ready"], 4)
            dve.wait_ge(sem["table_in"], TABLE_IN[3])

            def mask_logits(i, k):
                g = i * RG + k
                dve.wait_ge(gathered[k], i * (16 * G) + (3 * ITERS + 1) * 16 * G)
                slots = bass.ds(i * R + k * G, G)
                wait(dve, sem["mask_logit"], g)
                v.tensor_tensor(att[:, 0, :], ring[:, k * G:(k + 1) * G, D + 1], meta_src[:, slots, 3],
                                ALU.add).then_inc(sem["ev_ready"], 1)
                wait(dve, sem["t_psum"], g)
                v.tensor_tensor(logit, iota[:, :].rearrange("p (o e) -> p o e", o=1).to_broadcast([P, G, P]),
                                meta_src[:, slots, 1:2].to_broadcast([P, G, P]), ALU.not_equal).then_inc(sem["ne_ready"], 1)
                wait(dve, sem["ev_ready"], g + 1)
                wait(dve, sem["ne_ready"], g + 1)
                v.scalar_tensor_tensor(logit, logit, -BIG, att[:, 0, :].rearrange("p (s o) -> p s o", o=1).to_broadcast([P, G, P]),
                                       ALU.mult, ALU.add).then_inc(sem["mask_logit"], 1)

            MAX_STEPS = 5

            def maxima(i, k):
                g, q = i * RG + k, k % 2
                slots = bass.ds(i * R + k * G, G)
                now = runmax[:, q, 1:1 + G]
                steps = [0]

                def step(ins):
                    steps[0] += 1
                    ins.then_inc(sem["max_ready"], 1)
                    dve.wait_ge(sem["max_ready"], g * MAX_STEPS + steps[0])
                dve.wait_ge(sem["t_psum"], g + 1)
                step(v.tensor_reduce(att[:, 1, :], psf[:, 4 * 512:6 * 512].rearrange("p (s e) -> p s e", e=P), AX_X, ALU.max))
                step(v.scalar_tensor_tensor(att[:, 2, :], att[:, 1, :], FLOOR, cslot[:, slots], ALU.max, ALU.add))
                step(v.tensor_copy(runmax[:, q, 0:1], runmax[:, 1 - q, G:G + 1]))
                step(v.tensor_tensor_scan(now, reset[:, slots], att[:, 2, :], runmax[:, q, 0:1], ALU.add, ALU.max))
                step(v.tensor_tensor(att[:, 3, :], runmax[:, q, 0:G], reset[:, slots], ALU.add))
                wait(dve, sem["corr_ready"], g)
                v.tensor_tensor(att[:, 4, :], att[:, 3, :], now, ALU.subtract).then_inc(sem["bias_ready"], 1)
                v.tensor_tensor(bias[:, q, :], cslot[:, slots], now, ALU.subtract).then_inc(sem["bias_ready"], 1)

            def rescale_add(i, k):
                q = k % 2
                dve.wait_ge(sem["corr_ready"], i * RG + (k + 1))
                for j in range(G):
                    c = i * R + (k * G + j)
                    n = c + 3 * SLOTS
                    t = dve.value_load(tile_src[0:1, bass.ds(c, 1)], min_val=0, max_val=T - 1)
                    dst = acc3[:, bass.ds(t, 1), :].rearrange("p o d -> p (o d)")
                    wait(dve, sem["added"], n)
                    wait(dve, sem["summed"], n + 1)
                    v.scalar_tensor_tensor(dst, dst, corr[:, q, j:j + 1], ps[:, j % 4, 0:AW], ALU.mult,
                                           ALU.add).then_inc(sem["added"], 1)

            def after(i, k, n):
                return (i, k + n) if k + n < RG else (i + 1, k + n - RG)

            def attend_round(i, last=False):
                for k in range(RG):
                    if not last or k + 1 < RG:
                        maxima(*after(i, k, 1))
                    rescale_add(i, k)
                    if not last or k + 2 < RG:
                        mask_logits(*after(i, k, 2))
            mask_logits(0, 0)
            maxima(0, 0)
            mask_logits(0, 1)
            attend_round(0)
            with dve.Fori(1, ITERS - 1) as i:
                attend_round(i)
            attend_round(ITERS - 1, last=True)
            dve.wait_ge(sem["added"], 4 * SLOTS)
            link(v.tensor_scalar(small[:, 0, :], acc3[:, :, D], 1e-30, None, ALU.max))
            link(v.reciprocal(small[:, 1, :], small[:, 0, :]))
            link(v.tensor_tensor(accd, accd, by_tile(small[:, 1, :]), ALU.mult))
            link(v.scalar_tensor_tensor(accd, accd, SLOPE, accd, ALU.mult, ALU.max))
            link(v.tensor_tensor(accd, accd, X[:, :, :], ALU.add))
            layer_norm(5, False)


INPUTS = ["x", "src", "dst", "edge_attr_128", "edge_weight", "L0_gnn_W", "L0_gnn_b", "L1_gnn_W1", "L1_gnn_b1",
          "L1_gnn_W2", "L1_gnn_b2", "L1_gnn_eps", "L1_gnn_gamma", "L1_gnn_beta", "L2_gnn_eps", "L2_gnn_W1",
          "L2_gnn_b1", "L2_gnn_g1", "L2_gnn_be1", "L2_gnn_W2", "L2_gnn_b2", "L2_gnn_g2", "L2_gnn_be2",
          "L3_gnn_w_W", "L3_gnn_w_b", "L3_gnn_ew_W", "L3_gnn_ew_b", "L3_gnn_a_W", "L3_gnn_a_b"]


def kernel(**inputs):
    import numpy as np
    import concourse.bacc as bacc
    from concourse import mybir
    from concourse.bass_utils import run_bass_kernel_spmd as run

    nc = bacc.Bacc("TRN2", target_bir_lowering=False, num_devices=1)
    arrays, args = {}, {}
    for name in INPUTS:
        v = np.ascontiguousarray(inputs[name])
        if v.ndim == 0:
            v = v.reshape(1)
        arrays[f"in_{name}"] = v
        args[name] = nc.dram_tensor(f"in_{name}", v.shape, mybir.dt.from_np(v.dtype), kind="ExternalInput").ap()
    out = nc.dram_tensor("out", (N_NODES, D), mybir.dt.float32, kind="ExternalOutput").ap()
    gnn_program(nc, args, out)
    return run(nc, [arrays], core_ids=[0]).results[0]["out"]
```

```python
from contextlib import ExitStack

import concourse.bass as bass
from concourse import mybir

P = 128
ALU = mybir.AluOpType
ACT = mybir.ActivationFunctionType
F32 = mybir.dt.float32
I32 = mybir.dt.int32
BF16 = mybir.dt.bfloat16
U8 = mybir.dt.uint8
AX_X = mybir.AxisListType.X

N_NODES = 6250
N_EDGES = 100000
D = 256
D_EDGE = 128
KC = D // P
T = -(-N_NODES // P)
LAST = N_NODES - (T - 1) * P
NPAD = T * P
COLS = 800
EP = N_EDGES // COLS
SLOPE = 0.2
LN_EPS = 1e-5
BN_EPS = 1e-5

G = 7
RG = 6
R = G * RG
MOST_SLOTS = (N_EDGES + T * (P - 1)) // P
ITERS = -(-MOST_SLOTS // R)
SLOTS = ITERS * R
GROUPS = SLOTS // G
RECORDS = P * SLOTS
UC = -(-SLOTS // P)
assert N_EDGES // P + 1 + T - 1 <= SLOTS

SC = 8
SG = 4
SITERS = COLS // (SC * SG)
EC = 4
ES = SC * SG // EC
AR = 4
OUT_OF_RANGE = 1 << 20
NOWHERE = 127 + P * 50000
NO_NODE = 8191
BIG = 1e30
FLOOR = -1e20
HW = D + 2
SB = 4
NB = -(-T // SB)
assert EP * COLS == N_EDGES and SB * (NB - 1) + 1 == T and NB % 2 and SITERS * SC * SG == COLS


def wait(eng, sem, n):
    if not isinstance(n, int) or n > 0:
        eng.wait_ge(sem, n)


def rounds(eng, n, body, first=True):
    if first:
        body(0)
    with eng.Fori(1 if first else 0, n) as i:
        body(i)


def batches(eng, body):
    body(0, 0, SB)
    body(1, 1, SB)
    with eng.Fori(1, (NB - 1) // 2) as i:
        for q in range(2):
            body(i * 2 + q, q, SB)
    body(NB - 1, 0, 1)


def each_batch(body):
    for b in range(NB):
        body(b, b % 2, min(SB, T - b * SB))


def gnn_program(nc, a, out):
    with ExitStack() as ctx:
        def sb(name, shape, dt=F32):
            return ctx.enter_context(nc.sbuf_tensor(name, shape, dt))

        table = [nc.dram_tensor(f"table{i}", [NPAD, HW if i == 3 else D], F32).ap() for i in range(4)]
        rec_src = nc.dram_tensor("rec_src", [RECORDS, 4], F32).ap()
        rec_dst = nc.dram_tensor("rec_dst", [RECORDS, 2], F32).ap()
        row_src = nc.dram_tensor("row_src", [P * COLS // P, P], I32).ap()
        row_dst = nc.dram_tensor("row_dst", [P * COLS // P, P], I32).ap()

        X = sb("X", [P, T, D])
        ACC = sb("ACC", [P, T * D])
        ZT = sb("ZT", [P, T * HW])
        meta_src = sb("meta_src", [P, SLOTS, 4])
        meta_dst = sb("meta_dst", [P, SLOTS, 2])
        tile_src = sb("tile_src", [P, SLOTS], I32)
        tile_dst = sb("tile_dst", [P, SLOTS], I32)
        reset = sb("reset", [P, SLOTS])
        cslot = sb("cslot", [P, SLOTS])
        W = sb("W", [P, 2 * KC, D])
        bc = sb("bc", [P, 3, D])
        ewW = sb("ewW", [P, D])
        xT = sb("xT", [P, 2, KC, SB * P])
        z1 = sb("z1", [P, SB * D])
        ident = sb("ident", [P, P])
        iota = sb("iota", [P, P])
        ones = sb("ones", [P, P])
        before = sb("before", [P, P])
        col = sb("col", [P, 24])
        ends = sb("ends", [P, 3, 3, T])
        small = sb("small", [P, 6, T])
        s1 = sb("s1", [P, T])
        s2 = sb("s2", [P, T])
        lin = sb("lin", [P, KC + 1])
        zsum = sb("zsum", [P, 2, 2, EC])
        endT = sb("endT", [P, 3, 3])
        next_key = sb("next_key", [P, 1], I32)
        unordered = sb("unordered", [P, 2])
        seen = sb("seen", [P, 1], I32)
        gidx = sb("gidx", [P, RG, G], I32)
        sidx = sb("sidx", [P, SG, SC], I32)
        spay = sb("spay", [P, SG, SC, 4])
        token = sb("token", [P, 1])
        lane_no = sb("lane_no", [P, 1])
        att = sb("att", [P, 5, G])
        runmax = sb("runmax", [P, 2, 1 + G])
        corr = sb("corr", [P, 2, G])
        rsum = sb("rsum", [P, 2, G])
        ev = sb("ev", [P, G])
        bias = sb("bias", [P, 2, G])
        mv = sb("mv", [P, KC, 8])

        acc3 = ACC[:, :].rearrange("p (t w) -> p t w", w=D)
        accd = acc3[:, :, 0:D]
        zt3 = ZT[:, 0:T * D].rearrange("p (t w) -> p t w", w=D)
        ztf = ZT[:, 0:KC * NPAD].rearrange("p (k n) -> p k n", k=KC)
        ht = ZT[:, :].rearrange("p (t w) -> p t w", w=HW)

        ring = ZT[:, 0:R * HW].rearrange("p (s w) -> p s w", w=HW)
        o = R * HW
        logit = ZT[:, o:o + G * P].rearrange("p (s e) -> p s e", e=P)
        o += G * P
        probT = ZT[:, o:o + G * P].rearrange("p (s e) -> p s e", e=P)
        assert o + G * P <= T * HW
        sel = xT[:, :, :, :].rearrange("p q k n -> p q (k n)")[:, :, 0:G * P].rearrange("p b (s e) -> p b s e", e=P)
        other = z1[:, 0:G * P].rearrange("p (s e) -> p s e", e=P)

        rows_ = ZT[:, 0:15 * COLS].rearrange("p (r c) -> p r c", c=COLS)
        key = [rows_[:, 0].bitcast(I32), rows_[:, 1].bitcast(I32)]
        bucket, pos = rows_[:, 2], rows_[:, 3]
        run = [rows_[:, 4], rows_[:, 5]]
        ibuf = rows_[:, 6].bitcast(I32)
        rec_of = [rows_[:, 7].bitcast(I32), rows_[:, 8].bitcast(I32)]
        pay_src = ZT[:, 9 * COLS:13 * COLS].rearrange("p (c f) -> p c f", f=4)
        pay_dst = ZT[:, 13 * COLS:15 * COLS].rearrange("p (c f) -> p c f", f=2)
        pay = [pay_src, pay_dst]
        mask = ACC[:, 0:T * COLS // 4].bitcast(U8).rearrange("p (b c) -> p b c", b=T)
        o = T * COLS // 4
        attr = ACC[:, o:o + AR * EC * D_EDGE].rearrange("p (b c d) -> p b c d", b=AR, d=D_EDGE)
        assert o + AR * EC * D_EDGE <= T * D
        slot_no, past = reset, cslot
        stats = cslot[:, 0:KC * NB * 6].rearrange("p (k b s) -> p k b s", k=KC, b=NB)
        o = 2 * COLS
        slot_of = ZT[:, o:o + SLOTS]
        o += SLOTS
        unit_row = [ZT[:, o + i * UC * P:o + (i + 1) * UC * P].bitcast(I32).rearrange("p (c e) -> p c e", e=P)
                    for i in range(2)]
        unit_val = [ZT[:, o + i * UC * P:o + (i + 1) * UC * P].rearrange("p (c e) -> p c e", e=P)
                    for i in range(2)]
        o += 2 * UC * P
        unit_at = ZT[:, o:o + UC].bitcast(I32)
        unit_tile = ZT[:, o + UC:o + 2 * UC]
        assert o + 2 * UC <= 6 * COLS
        wsum = meta_dst[:, :, :].rearrange("p s f -> p (s f)")[:, 0:SLOTS + 1]
        flat_src = meta_src[:, :, :].rearrange("p s f -> p (s f)")
        relu_out = flat_src[:, 0:2 * EC * D].rearrange("p (q j d) -> p q j d", q=2, j=EC)
        line_out = flat_src[:, 2 * EC * D:2 * EC * (D + P)].rearrange("p (q j d) -> p q j d", q=2, j=EC)
        a_relu = bc[:, 1, :]
        ewT = z1[:, 0:D]
        w_line = z1[:, D:D + P]
        z_bias = z1[:, 384:640].bitcast(BF16)
        ones16 = z1[:, 640:704].bitcast(BF16)
        term = z1[:, 704:832].bitcast(BF16)
        left = [bc[:, 2, :], relu_out[:, 0, 0, :]]
        attrT = xT[:, :, :, :].rearrange("p q k n -> p (q k) n")
        meta = [meta_src, meta_dst, meta_src, meta_src]
        slot_tile = [tile_src, tile_dst, tile_src, tile_src]

        EWB, A3, B1, L2B1, G1, BE1, L2B2, G2, BE2 = range(0, 18, 2)
        EPS1, EPS2, AB = 18, 19, 20

        ps = ctx.enter_context(nc.psum_tensor("ps", [P, 8, 512], F32))
        psf = ps[:, :, :].rearrange("p b c -> p (b c)")

        def slot_sum(j):
            return ps[:, j // 2, (j % 2) * D:(j % 2 + 1) * D]

        def slot_done(n, j):
            return n + (2 if j % 2 == 0 and j + 1 < G else 1)

        def att_bank(q):
            return psf[:, (4 + 2 * q) * 512:(4 + 2 * q) * 512 + G * P]

        names = """units_known units_in unit_values unit_psum dst_sorted order_known branch_chain records_dst scat2_ready token2 edge_part attr_lin split_ready w_ready weighed one_ready scaled mask_part run_done weight_ready prefix_out ew_psum lin_ready consts ident_ready zeroed keys_in x_in fill_in records_in table_in stored weights_in cols_in
          dve_chain counted prefix base_ready scanned ranked record_ready ends_ready endT_psum endT_ready
          past_ready tile_psum tile_ready wT_psum wT_ready xT_psum xT_sbuf z_psum z_sbuf y_psum y_used
          attrT_psum attrT_sbuf ez_psum lr_ready logit_psum pay_ready scat_ready
          idx_ready idx_token sel_ready summed added acc_zero agg_ready
          ln_center ln_square ln_var ln_sqrt ln_done bn_in bn_var bn_sqrt bn_scale bn_applied back_psum back_used
          s1_ready c_psum c_ready ht_ready ev_ready ne_ready mask_logit t_psum max_ready bias_ready corr_ready
          probT_ready p_psum"""
        sem = {n: ctx.enter_context(nc.semaphore(n)) for n in names.split()}
        gathered = [ctx.enter_context(nc.semaphore(f"gathered{i}")) for i in range(RG)]
        scattered = [ctx.enter_context(nc.semaphore(f"scattered{i}")) for i in range(SG)]
        scattered2 = [ctx.enter_context(nc.semaphore(f"scattered2_{i}")) for i in range(SG)]
        attr_in = [ctx.enter_context(nc.semaphore(f"attr_in{i}")) for i in range(AR)]

        TABLE_IN = [16 * NB, 16 * (NB + 1), 16 * (NB + 2), 16 * (NB + 3)]
        WEIGHTS = [80, 160, 192, 256]
        ZB = {1: 0, 2: NB, "2b": 2 * NB}
        YB = {0: 0, 1: NB, 3: 2 * NB}
        ESTEPS = COLS // EC
        KEYS_IN = 7 * 16
        FILL_IN = 4 * 16

        def tiles(view, b, nt):
            return view[:, b * SB:b * SB + nt] if isinstance(b, int) else view[:, bass.ds(b * SB, nt)]

        def nodes(b, n):
            return slice(b * SB * P, b * SB * P + n) if isinstance(b, int) else bass.ds(b * (SB * P), n)

        block = ctx.enter_context(nc.Block())

        def read_order(eng):
            eng.wait_ge(sem["order_known"], 1)
            return eng.value_load(seen[0:1, 0:1], min_val=0, max_val=1)

        @block.sync
        def _(sp):
            sp.wait_ge(sem["zeroed"], 7)
            with nc.allow_non_contiguous_dma(reason="one word a partition, once"):
                sp.dma_start(next_key[0:EP - 1, :], a["dst"].rearrange("(p c) -> p c", c=COLS)[1:EP, 0:1]).then_inc(sem["keys_in"], 16)
            for into, dram in ((key[0], a["src"]), (key[1], a["dst"]), (run[0], a["edge_weight"])):
                rows = dram.rearrange("(p c) -> p c", c=COLS)
                sp.dma_start(into[0:120, :], rows[0:120, :]).then_inc(sem["keys_in"], 16)
                sp.dma_start(into[120:EP, :], rows[120:EP, :]).then_inc(sem["keys_in"], 16)
            sp.dma_start(X[:, 0:T - 1, :], a["x"][0:(T - 1) * P, :].rearrange("(t p) d -> p t d", p=P)).then_inc(sem["x_in"], 16)
            sp.dma_start(X[0:LAST, T - 1, :], a["x"][(T - 1) * P:, :]).then_inc(sem["x_in"], 16)
            sp.dma_start(W[:, 0:KC, :], a["L0_gnn_W"].rearrange("(m p) d -> p m d", p=P)).then_inc(sem["weights_in"], 16)
            sp.dma_start(bc[:, 0, :], a["L0_gnn_b"].rearrange("(a d) -> a d", a=1).to_broadcast([P, D])).then_inc(sem["weights_in"], 16)
            sp.dma_start(ewW[:, :], a["L3_gnn_ew_W"]).then_inc(sem["weights_in"], 16)
            aw = a["L3_gnn_a_W"].rearrange("n o -> (n o)")
            sp.dma_start(bc[:, 1, :], aw[2 * D:3 * D].rearrange("(a d) -> a d", a=1).to_broadcast([P, D])).then_inc(sem["weights_in"], 16)
            sp.dma_start(bc[:, 2, :], a["L3_gnn_ew_b"].rearrange("(a d) -> a d", a=1).to_broadcast([P, D])).then_inc(sem["weights_in"], 16)
            with nc.allow_non_contiguous_dma(reason="a few hundred words, once"):
                for c, v in ((EWB, a["L3_gnn_ew_b"]), (A3, aw[2 * D:3 * D]), (B1, a["L1_gnn_b1"]),
                             (L2B1, a["L2_gnn_b1"]), (G1, a["L2_gnn_g1"]), (BE1, a["L2_gnn_be1"]),
                             (L2B2, a["L2_gnn_b2"]), (G2, a["L2_gnn_g2"]), (BE2, a["L2_gnn_be2"])):
                    sp.dma_start(col[:, c:c + 2], v.rearrange("(m p) -> p m", p=P)).then_inc(sem["cols_in"], 16)
                for c, v in ((EPS1, a["L1_gnn_eps"]), (EPS2, a["L2_gnn_eps"]), (AB, a["L3_gnn_a_b"])):
                    sp.dma_start(col[:, c:c + 1], v.rearrange("(a d) -> a d", a=1).to_broadcast([P, 1])).then_inc(sem["cols_in"], 16)
            sp.dma_start(rec_src.rearrange("(l s) f -> l s f", l=P), meta_src[:, :, :]).then_inc(sem["fill_in"], 16)
            sp.dma_start(rec_dst.rearrange("(l s) f -> l s f", l=P), meta_dst[:, :, :]).then_inc(sem["fill_in"], 16)

            sp.wait_ge(sem["keys_in"], KEYS_IN)
            for rows, into in ((row_src, key[0]), (row_dst, key[1])):
                sp.dma_start(rows.rearrange("r e -> (r e)").rearrange("(p c) -> p c", c=COLS), into).then_inc(sem["fill_in"], 16)

            def store0(b, q, nt):
                wait(sp, sem["y_used"], b + 1)
                rows = table[0][nodes(b, nt * P), :]
                sp.dma_start(rows.rearrange("(t p) d -> p t d", p=P),
                             z1[:, 0:nt * D].rearrange("p (t d) -> p t d", d=D)).then_inc(sem["table_in"], 16)
            batches(sp, store0)

            rows = a["edge_attr_128"].rearrange("(p c) d -> p c d", c=COLS)

            def load_attr(i):
                for u in range(ES):
                    n = i * ES + u
                    wait(sp, sem["pay_ready"], n - (AR - 1))
                    c = bass.ds(n * EC, EC)
                    sp.dma_start(attr[0:120, u % AR, :, :], rows[0:120, c, :]).then_inc(attr_in[u % AR], 16)
                    sp.dma_start(attr[120:EP, u % AR, :, :], rows[120:EP, c, :]).then_inc(attr_in[u % AR], 16)
            rounds(sp, SITERS, load_attr)

            for k in range(SG):
                sp.wait_ge(scattered[k], 16 * SC * SITERS)
            sp.dma_start(meta_src[:, :, :], rec_src.rearrange("(l s) f -> l s f", l=P)).then_inc(sem["records_in"], 16)
            with sp.If(read_order(sp) > 0):
                sp.wait_ge(sem["dst_sorted"], 1)
                for k in range(SG):
                    sp.wait_ge(scattered2[k], 16 * SC * SITERS)
                sp.dma_start(meta_dst[:, :, :], rec_dst.rearrange("(l s) f -> l s f", l=P)).then_inc(sem["records_dst"], 16)
                sp.wait_ge(sem["records_dst"], 16)

            def load_weights(w1, w2, vectors):
                for j, w in ((0, w1), (KC, w2)):
                    if w is not None:
                        sp.dma_start(W[:, j:j + KC, :], w.rearrange("(m p) d -> p m d", p=P)).then_inc(sem["weights_in"], 16)
                for j, v in enumerate(vectors):
                    sp.dma_start(bc[:, j, :], v.rearrange("(a d) -> a d", a=1).to_broadcast([P, D])).then_inc(sem["weights_in"], 16)

            def store_x(layer, n):
                sp.wait_ge(sem["ln_done"], n)
                sp.dma_start(table[layer].rearrange("(t p) d -> p t d", p=P), X[:, :, :]).then_inc(sem["table_in"], 16)

            store_x(1, 1)
            load_weights(a["L1_gnn_W1"], a["L1_gnn_W2"], (a["L1_gnn_b2"], a["L1_gnn_gamma"], a["L1_gnn_beta"]))
            store_x(2, 3)
            load_weights(a["L2_gnn_W1"], a["L2_gnn_W2"], ())
            sp.wait_ge(sem["ln_done"], 4)
            load_weights(a["L3_gnn_w_W"], None, (a["L3_gnn_w_b"], aw[0:D], aw[D:2 * D]))
            sp.wait_ge(sem["ht_ready"], 1)
            sp.dma_start(table[3].rearrange("(t p) d -> p t d", p=P), ht).then_inc(sem["table_in"], 16)
            sp.wait_ge(sem["ln_done"], 5)
            sp.dma_start(out[0:(T - 1) * P, :].rearrange("(t p) d -> p t d", p=P), X[:, 0:T - 1, :]).then_inc(sem["stored"], 16)
            sp.dma_start(out[(T - 1) * P:, :], X[0:LAST, T - 1, :]).then_inc(sem["stored"], 16)
            sp.wait_ge(sem["stored"], 32)

        @block.gpsimd
        def _(pool):
            pool.memset(ones[:, :], 1.0).then_inc(sem["consts"], 1)
            pool.memset(ident[:, :], 0.0).then_inc(sem["consts"], 1)
            pool.memset(token[:, :], 0.0).then_inc(sem["idx_token"], 1)
            pool.iota(iota[:, :], [[1, P]], base=0, channel_multiplier=0,
                      allow_small_or_imprecise_dtypes=True).then_inc(sem["consts"], 1)
            pool.iota(slot_no[:, :], [[1, SLOTS]], base=0, channel_multiplier=0,
                      allow_small_or_imprecise_dtypes=True).then_inc(sem["consts"], 1)
            pool.iota(lane_no[:, :], [[0, 1]], base=0, channel_multiplier=1,
                      allow_small_or_imprecise_dtypes=True).then_inc(sem["consts"], 1)
            pool.wait_ge(sem["consts"], 5)
            pool.affine_select(out=ident[:, :], in_=ident[:, :], compare_op=ALU.not_equal, fill=1.0, base=0,
                               pattern=[[-1, P]], channel_multiplier=1).then_inc(sem["ident_ready"], 1)
            pool.affine_select(out=before[:, :], in_=ones[:, :], compare_op=ALU.is_gt, fill=0.0, base=0,
                               pattern=[[1, P]], channel_multiplier=-1).then_inc(sem["ident_ready"], 1)
            record_bound = pool.to_reg(RECORDS - 1)
            node_bound = pool.to_reg(N_NODES - 1)
            row_bound = pool.to_reg(COLS - 1)

            def hold(held, before_this, ready, n):
                pool.wait_ge(sem[held], before_this)
                pool.wait_ge(ready, n)
                pool.tensor_tensor(token[0:1, :], token[0:1, :], token[0:1, :], ALU.add).then_inc(sem[held], 1)

            def scatter(dram, fields, held, ready, scattered):
                with pool.Fori(0, SITERS) as i:
                    for k in range(SG):
                        g = i * SG + k
                        hold(held, g + 1, sem[ready], g * 2 + 2)
                        for c in range(SC):
                            pool.indirect_dma_start(
                                dram, bass.IndirectOffsetOnAxis(ap=sidx[:, k, c:c + 1], axis=0),
                                spay[:, k, c, 0:fields], None,
                                bounds_check=record_bound, oob_is_err=False).then_inc(scattered[k], 16)

            def gather(layer):
                width = HW if layer == 3 else D
                pool.wait_ge(sem["table_in"], TABLE_IN[layer])
                if layer == 0:
                    pool.wait_ge(sem["acc_zero"], 1)
                with pool.Fori(0, ITERS) as i:
                    for k in range(RG):
                        g = i * RG + (layer * GROUPS + k)
                        hold("idx_token", g + (SITERS * SG + 1), sem["idx_ready"], g + 1)
                        for j in range(G):
                            pool.indirect_dma_start(
                                ring[:, k * G + j, 0:width], None, table[layer],
                                bass.IndirectOffsetOnAxis(ap=gidx[:, k, j:j + 1], axis=0),
                                bounds_check=node_bound, oob_is_err=False).then_inc(gathered[k], 16)

            pool.wait_ge(sem["fill_in"], FILL_IN)
            scatter(rec_src, 4, "idx_token", "scat_ready", scattered)
            pool.wait_ge(sem["units_known"], 1)
            for rows, into in zip((row_src, row_dst), unit_row):
                for c in range(UC):
                    n = min(P, SLOTS - c * P)
                    pool.indirect_dma_start(into[0:n, c, :], None, rows,
                                            bass.IndirectOffsetOnAxis(ap=unit_at[0:n, c:c + 1], axis=0),
                                            bounds_check=row_bound, oob_is_err=False).then_inc(sem["units_in"], 16)
            with pool.If(read_order(pool) > 0):
                pool.wait_ge(sem["idx_token"], SITERS * SG + 1)
                pool.tensor_tensor(token[0:1, :], token[0:1, :], token[0:1, :], ALU.add).then_inc(sem["token2"], 1)
                scatter(rec_dst, 2, "token2", "scat2_ready", scattered2)
                pool.wait_ge(sem["token2"], SITERS * SG + 1)
            for layer in range(4):
                gather(layer)

        @block.scalar
        def _(act):
            def copy_xT(phase, used, used0):
                def body(b, q, nt):
                    wait(act, sem["xT_psum"], b + (phase * NB + 1))
                    wait(act, sem[used], b + (used0 - 1))
                    for k in range(KC):
                        nc.scalar.copy(xT[:, q, k, 0:nt * P], ps[:, 2 * q + k, 0:nt * P]).then_inc(sem["xT_sbuf"], 1)
                return body

            act.wait_ge(sem["wT_psum"], 1)
            act.wait_ge(sem["weights_in"], WEIGHTS[0])
            nc.scalar.copy(W[:, KC:2 * KC, :], ps[:, 6, :].rearrange("p (k d) -> p k d", k=KC)).then_inc(sem["wT_ready"], 1)

            def rows0(b, q, nt):
                copy_xT(0, "y_psum", YB[0])(b, q, nt)
                wait(act, sem["y_psum"], b + 1)
                wait(act, sem["table_in"], b * 16)
                nc.scalar.copy(z1[:, 0:nt * D], psf[:, 512 * 4:512 * 4 + nt * D]).then_inc(sem["y_used"], 1)
            batches(act, rows0)

            act.wait_ge(sem["cols_in"], 16 * 12)
            act.wait_ge(sem["table_in"], TABLE_IN[0])
            act.wait_ge(sem["ew_psum"], 1)
            nc.scalar.copy(ewT, ps[:, 6, 0:D]).then_inc(sem["lin_ready"], 1)
            nc.scalar.activation(lin[:, 0:KC], col[:, A3:A3 + KC], ACT.Copy, scale=SLOPE).then_inc(sem["lin_ready"], 1)
            nc.scalar.activation(a_relu, a_relu, ACT.Copy, scale=1.0 - SLOPE).then_inc(sem["w_ready"], 1)
            act.wait_ge(sem["ew_psum"], 2)
            nc.scalar.copy(w_line, ps[:, 6, D:D + P]).then_inc(sem["w_ready"], 1)
            nc.scalar.copy(lin[:, KC:KC + 1], ps[:, 6, D + P:D + P + 1]).then_inc(sem["w_ready"], 1)

            def copy_attrT(n, u):
                wait(act, sem["attrT_psum"], n + 1)
                wait(act, sem["ez_psum"], n - 3)
                nc.scalar.copy(attrT[:, u % 4, :], ps[:, u % 2, :]).then_inc(sem["attrT_sbuf"], 1)

            def hand_scatter(n, i, fields, ready, scattered):
                for k in range(SG):
                    wait(act, scattered[k], i * (16 * SC))
                    c = bass.ds(i * (SG * SC) + k * SC, SC)
                    nc.scalar.copy(sidx[:, k, :], rec_of[n][:, c]).then_inc(sem[ready], 1)
                    nc.scalar.copy(spay[:, k, :, 0:fields], pay[n][:, c, :]).then_inc(sem[ready], 1)

            def edge_round(i, first=False, last=False):
                for u in range(ES):
                    if not (last and u == ES - 1):
                        copy_attrT(i * ES + u + 1, u + 1)
                if not first:
                    wait(act, sem["record_ready"], 1)
                    wait(act, sem["pay_ready"], i * ES)
                    hand_scatter(0, i - 1, 4, "scat_ready", scattered)
            copy_attrT(0, 0)
            edge_round(0, first=True)
            edge_round(1)
            with act.Fori(2, SITERS - 1) as i:
                edge_round(i)
            edge_round(SITERS - 1, last=True)
            act.wait_ge(sem["pay_ready"], ESTEPS)
            hand_scatter(0, SITERS - 1, 4, "scat_ready", scattered)
            with act.If(read_order(act) > 0):
                act.wait_ge(sem["record_ready"], 2)
                for k in range(SG):
                    act.wait_ge(scattered[k], 16 * SC * SITERS)
                rounds(act, SITERS, lambda i: hand_scatter(1, i, 2, "scat2_ready", scattered2))
                act.wait_ge(sem["records_dst"], 16)

            def hand_gather(layer, i):
                for k in range(RG):
                    wait(act, sem["summed"], i * R + (layer * SLOTS + (k - RG + 1) * G))
                    src = meta[layer][:, bass.ds(i * R + k * G, G), 0].bitcast(I32)
                    nc.scalar.copy(gidx[:, k, :], src).then_inc(sem["idx_ready"], 1)

            def square(n):
                act.wait_ge(sem["ln_center"], n)
                nc.scalar.activation(zt3, accd, ACT.Square).then_inc(sem["ln_square"], 1)
                act.wait_ge(sem["ln_var"], n)
                nc.scalar.activation(small[:, 4, :], small[:, 3, :], ACT.Sqrt).then_inc(sem["ln_sqrt"], 1)

            act.wait_ge(sem["records_in"], 16)
            rounds(act, ITERS, lambda i: hand_gather(0, i))
            square(1)
            act.wait_ge(sem["dst_sorted"], 1)
            rounds(act, ITERS, lambda i: hand_gather(1, i), first=False)

            def mlp1(b, q, nt):
                copy_xT(1, "z_psum", ZB[1])(b, q, nt)
                wait(act, sem["z_psum"], b + 1)
                wait(act, sem["y_psum"], b + YB[1])
                for m in range(KC):
                    nc.scalar.activation(z1[:, m * 512:m * 512 + nt * P], ps[:, 4 + m, 0:nt * P], ACT.Relu,
                                         bias=col[:, B1 + m:B1 + m + 1]).then_inc(sem["z_sbuf"], 1)
            batches(act, mlp1)
            square(2)
            square(3)
            def weigh(g, c0, q):
                wait(act, sem["one_ready"], g + 1)
                wait(act, sem["summed"], g * G + (2 * SLOTS - G))
                for j in range(G):
                    nc.scalar.activation(sel[:, q, j, :], other[:, j, :], ACT.Copy,
                                         scale=meta_src[:, bass.ds(c0 + j, 1), 2:3].rearrange("p o f -> p (o f)")).then_inc(sem["weighed"], 1)
                act.wait_ge(sem["weighed"], g * G + G)
                act.sem_inc(sem["scaled"], 1)
                act.sem_inc(sem["sel_ready"], 1)

            def weighted_round(i, last=False):
                for k in range(RG):
                    weigh(i * RG + k, i * R + k * G, k % 2)
                    if not last and k > 0:
                        hand_next(2, i, k - 1)
                if not last:
                    hand_next(2, i, RG - 1)

            def hand_next(layer, i, k):
                wait(act, sem["summed"], i * R + (layer * SLOTS + (k + 1) * G))
                src = meta[layer][:, bass.ds(i * R + (R + k * G), G), 0].bitcast(I32)
                nc.scalar.copy(gidx[:, k, :], src).then_inc(sem["idx_ready"], 1)
            hand_gather(2, 0)
            weighted_round(0)
            with act.Fori(1, ITERS - 1) as i:
                weighted_round(i)
            weighted_round(ITERS - 1, last=True)

            def lin2(which):
                def body(b, q, nt):
                    if which == 0:
                        copy_xT(2, "z_psum", ZB[2])(b, q, nt)
                    wait(act, sem["z_psum"], b + (ZB[2] + which * NB + 1))
                    bcol = (L2B1, L2B2)[which]
                    for m in range(KC):
                        nc.scalar.activation(ztf[:, m, nodes(b, nt * P)], ps[:, 4 + m, 0:nt * P], ACT.Identity,
                                             bias=col[:, bcol + m:bcol + m + 1]).then_inc(sem["z_sbuf"], 1)
                return body

            def norm2(which):
                act.wait_ge(sem["bn_var"], which + 1)
                nc.scalar.activation(mv[:, :, 3], mv[:, :, 2], ACT.Sqrt).then_inc(sem["bn_sqrt"], 1)
                act.wait_ge(sem["bn_scale"], which + 1)
                for m in range(KC):
                    nc.scalar.activation(ztf[:, m, :], ztf[:, m, :], ACT.Relu, bias=mv[:, m, 6:7],
                                         scale=mv[:, m, 5:6]).then_inc(sem["bn_applied"], 1)
            for which in range(2):
                batches(act, lin2(which))
                norm2(which)
            square(4)
            batches(act, copy_xT(3, "y_psum", YB[3]))
            def mask_logits(g):
                wait(act, sem["ne_ready"], g + 1)
                wait(act, sem["ev_ready"], g + 1)
                wait(act, sem["t_psum"], g)
                for j in range(G):
                    nc.scalar.activation(logit[:, j, :], other[:, j, :], ACT.Identity, scale=-BIG,
                                         bias=ev[:, j:j + 1]).then_inc(sem["mask_part"], 1)
                act.wait_ge(sem["mask_part"], g * G + G)
                act.sem_inc(sem["mask_logit"], 1)

            def exponentials(g, q):
                wait(act, sem["bias_ready"], g * 2 + 2)
                wait(act, sem["run_done"], g - 1)
                wait(act, sem["added"], g * G + (3 * SLOTS - G))
                nc.scalar.activation(corr[:, q, :], att[:, 4, :], ACT.Exp).then_inc(sem["corr_ready"], 1)
                wait(act, sem["p_psum"], g)
                for j in range(G):
                    nc.scalar.activation(probT[:, j, :], att_bank(q)[:, j * P:(j + 1) * P], ACT.Exp,
                                         bias=bias[:, q, j:j + 1], accum_out=rsum[:, q, j:j + 1]).then_inc(sem["probT_ready"], 1)

            def copy_probs(g, q):
                wait(act, sem["p_psum"], g + 1)
                wait(act, sem["summed"], g * G + (3 * SLOTS - G))
                nc.scalar.copy(sel[:, q, :, :].rearrange("p s e -> p (s e)"), att_bank(q)).then_inc(sem["sel_ready"], 1)

            def attend_round(i, last=False):
                for k in range(RG):
                    g = i * RG + k
                    if not last or k + 1 < RG:
                        exponentials(g + 1, (k + 1) % 2)
                    if not last or k + 3 < RG:
                        mask_logits(g + 3)
                    if not last or k + 1 < RG:
                        copy_probs(g + 1, (k + 1) % 2)
                    if not last:
                        wait(act, sem["summed"], i * R + (3 * SLOTS + (k + 1) * G))
                        src = meta_src[:, bass.ds(i * R + (R + k * G), G), 0].bitcast(I32)
                        nc.scalar.copy(gidx[:, k, :], src).then_inc(sem["idx_ready"], 1)

            hand_gather(3, 0)
            mask_logits(0)
            mask_logits(1)
            exponentials(0, 0)
            mask_logits(2)
            copy_probs(0, 0)
            attend_round(0)
            with act.Fori(1, ITERS - 1) as i:
                attend_round(i)
            attend_round(ITERS - 1, last=True)
            square(5)

        @block.tensor
        def _(pe):
            def counts(n):
                pe.wait_ge(sem["counted"], (n + 1) * T)
                pe.wait_ge(sem["ident_ready"], 2)
                nc.tensor.matmul(ps[:, 7, 64:64 + T], ones[:, :], small[:, min(n, 1), :], start=True, stop=True)
                if n == 1:
                    nc.tensor.matmul(ps[:, 7, 120:121], ones[:, :], unordered[:, 1:2], start=True, stop=True)
                nc.tensor.matmul(ps[:, 7, 0:T], before[:, :], small[:, min(n, 1), :], start=True, stop=True).then_inc(sem["prefix"], 1)

            def end_columns(n):
                pe.wait_ge(sem["ends_ready"], n + 1)
                for j in range(3 if n == 1 else 2):
                    mm = nc.tensor.matmul(ps[0:T, 7, 128 + j:129 + j], ends[0:1, n, j, :], ones[0:1, 0:1],
                                          start=True, stop=True)
                mm.then_inc(sem["endT_psum"], 1)

            def slot_tiles(n):
                pe.wait_ge(sem["past_ready"], n + 1)
                h = SLOTS // 2
                nc.tensor.matmul(ps[:, 7, 0:h], ones[0:T, :], past[0:T, 0:h], start=True, stop=True).then_inc(sem["tile_psum"], 1)
                pe.wait_ge(sem["tile_ready"], 2 * n + 1)
                nc.tensor.matmul(ps[:, 7, 0:h], ones[0:T, :], past[0:T, h:], start=True, stop=True).then_inc(sem["tile_psum"], 1)

            def turn(phase, view):
                def body(b, q, nt):
                    wait(pe, sem["xT_sbuf"], b * 2 + (2 * phase * NB - 2))
                    src = tiles(view, b, nt)
                    for k in range(KC):
                        for j in range(nt):
                            mm = nc.tensor.transpose(ps[:, 2 * q + k, j * P:(j + 1) * P],
                                                     src[:, j, k * P:(k + 1) * P], ident[:, :])
                    mm.then_inc(sem["xT_psum"], 1)
                return body

            def rows_out(b, nt, lhs, w0, b0, used0, bias_row=None):
                wait(pe, sem["y_used"], b + used0)
                for j in range(nt):
                    o = ps[:, b0 + j // 2, (j % 2) * D:(j % 2 + 1) * D]
                    if bias_row is not None:
                        nc.tensor.matmul(o, ones[0:1, :], bias_row, start=True, stop=False)
                    for k in range(KC):
                        mm = nc.tensor.matmul(o, lhs(k, j), W[:, w0 + k, :], start=(k == 0 and bias_row is None),
                                              stop=(k == KC - 1))
                mm.then_inc(sem["y_psum"], 1)

            def columns_out(b, nt, rhs, w0, batch0):
                wait(pe, sem["z_sbuf"], b * 2 + 2 * batch0)
                for m in range(KC):
                    for k in range(KC):
                        mm = nc.tensor.matmul(ps[:, 4 + m, 0:nt * P], W[:, w0 + k, m * P:(m + 1) * P], rhs(k),
                                              start=(k == 0), stop=(k == KC - 1))
                mm.then_inc(sem["z_psum"], 1)

            counts(0)
            pe.wait_ge(sem["weights_in"], WEIGHTS[0])
            for k in range(KC):
                for m in range(KC):
                    mm = nc.tensor.transpose(ps[:, 6, k * D + m * P:k * D + (m + 1) * P],
                                             W[:, m, k * P:(k + 1) * P], ident[:, :])
            mm.then_inc(sem["wT_psum"], 1)
            pe.wait_ge(sem["wT_ready"], 1)
            pe.wait_ge(sem["x_in"], 32)
            pe.wait_ge(sem["zeroed"], 7)

            def first_rows(b, q, nt):
                turn(0, X)(b, q, nt)
                wait(pe, sem["xT_sbuf"], b * 2 + 2)
                rows_out(b, nt, lambda k, j: xT[:, q, k, j * P:(j + 1) * P], KC, 4, YB[0], bc[0:1, 0, :])
            each_batch(first_rows)

            pe.wait_ge(sem["cols_in"], 16 * 12)
            for m in range(KC):
                mm = nc.tensor.transpose(ps[:, 6, m * P:(m + 1) * P], ewW[:, m * P:(m + 1) * P], ident[:, :])
            mm.then_inc(sem["ew_psum"], 1)
            pe.wait_ge(sem["lin_ready"], 2)
            for m in range(KC):
                nc.tensor.matmul(ps[:, 6, D:D + P], lin[:, m:m + 1].to_broadcast([P, P]), ewT[:, m * P:(m + 1) * P],
                                 start=(m == 0), stop=(m == KC - 1))
            for m in range(KC):
                mm = nc.tensor.matmul(ps[:, 6, D + P:D + P + 1], col[:, EWB + m:EWB + m + 1].to_broadcast([P, P]),
                                      lin[:, m:m + 1], start=(m == 0), stop=(m == KC - 1))
            mm.then_inc(sem["ew_psum"], 1)
            pe.wait_ge(sem["y_used"], NB)
            pe.wait_ge(sem["split_ready"], 2)

            def turn_attr(i, u):
                q, n = u % 2, i * ES + u
                wait(pe, attr_in[u % AR], i * (32 * ES // AR) + 32 * (u // AR + 1))
                wait(pe, sem["attrT_sbuf"], n - 1)
                for j in range(EC):
                    mm = nc.tensor.transpose(ps[:, q, j * P:(j + 1) * P], attr[:, u % AR, j, :], ident[:, :])
                mm.then_inc(sem["attrT_psum"], 1)

            def edge_z(i, u):
                q, n = u % 2, i * ES + u
                wait(pe, sem["attrT_sbuf"], n + 1)
                wait(pe, sem["pay_ready"], n - 1)
                for j in range(EC):
                    o = ps[:, 2 + 2 * q + j // 2, (j % 2) * D:(j % 2 + 1) * D]
                    nc.tensor.matmul(o, ones16, z_bias[:, 0:D], start=True, stop=False)
                    mm = nc.tensor.matmul(o, attrT[:, u % 4, j * P:(j + 1) * P], ewW[:, :], start=False, stop=True)
                mm.then_inc(sem["ez_psum"], 1)

            def edge_round(i, last=False):
                for u in range(ES):
                    if not (last and u == ES - 1):
                        turn_attr(i, u + 1)
                    edge_z(i, u)
            turn_attr(0, 0)
            edge_round(0)
            end_columns(0)
            slot_tiles(0)
            with pe.Fori(1, SITERS - 1) as i:
                edge_round(i)
            edge_round(SITERS - 1, last=True)
            pe.wait_ge(sem["tile_ready"], 2)
            counts(1)
            pe.wait_ge(sem["prefix_out"], 2)
            end_columns(1)
            slot_tiles(1)
            pe.wait_ge(sem["tile_ready"], 4)
            pe.wait_ge(sem["unit_values"], 1)
            for c in range(UC):
                n = min(P, SLOTS - c * P)
                for j, (of, val) in enumerate(((slot_of, endT[0:T, 1, 2:3]), (past, ones[0:T, 0:1]))):
                    mm = nc.tensor.matmul(ps[0:n, 7, j * UC + c:j * UC + c + 1], of[0:T, c * P:c * P + n], val,
                                          start=True, stop=True)
            mm.then_inc(sem["unit_psum"], 1)
            pe.wait_ge(sem["unit_values"], 2)
            for i in range(2):
                for c in range(UC):
                    n = min(P, SLOTS - c * P)
                    mm = nc.tensor.transpose(ps[:, 3 + 2 * i + c // 4, (c % 4) * P:(c % 4) * P + n],
                                             unit_val[i][0:n, c, :], ident[0:n, 0:n])
            mm.then_inc(sem["unit_psum"], 1)
            with pe.If(read_order(pe) > 0):
                counts(2)
                pe.wait_ge(sem["prefix_out"], 3)
                end_columns(2)
                slot_tiles(2)

            def aggregate(layer, i):
                for k in range(RG):
                    slot_sums(layer, i * RG + k, i, k)

            def slot_sums(layer, g, i, k):
                wait(pe, gathered[k], i * (16 * G) + (layer * ITERS + 1) * 16 * G)
                wait(pe, sem["sel_ready"], g + (layer * GROUPS + 1))
                for j in range(G):
                    n = g * G + (layer * SLOTS + j)
                    if j % 2 == 0:
                        wait(pe, sem["added"], n - G + min(2, G - j))
                    nc.tensor.matmul(slot_sum(j), sel[:, k % 2, j, :], ring[:, k * G + j, 0:D],
                                     start=True, stop=True).then_inc(sem["summed"], 1)

            rounds(pe, ITERS, lambda i: aggregate(0, i))
            rounds(pe, ITERS, lambda i: aggregate(1, i), first=False)
            pe.wait_ge(sem["agg_ready"], 1)
            pe.wait_ge(sem["weights_in"], WEIGHTS[1])

            def mlp1(b, q, nt):
                turn(1, accd)(b, q, nt)
                wait(pe, sem["xT_sbuf"], b * 2 + (2 * NB + 2))
                columns_out(b, nt, lambda k: xT[:, q, k, 0:nt * P], 0, ZB[1])
                wait(pe, sem["z_sbuf"], b * 2 + 2)
                rows_out(b, nt, lambda k, j: z1[:, k * 512 + j * P:k * 512 + (j + 1) * P], KC, 6, YB[1])
            each_batch(mlp1)
            rounds(pe, ITERS, lambda i: aggregate(2, i), first=False)
            pe.wait_ge(sem["agg_ready"], 2)
            pe.wait_ge(sem["weights_in"], WEIGHTS[2])

            def lin2a(b, q, nt):
                turn(2, accd)(b, q, nt)
                wait(pe, sem["xT_sbuf"], b * 2 + (4 * NB + 2))
                columns_out(b, nt, lambda k: xT[:, q, k, 0:nt * P], 0, ZB[2])
            each_batch(lin2a)
            pe.wait_ge(sem["bn_applied"], KC)
            each_batch(lambda b, q, nt: columns_out(b, nt, lambda k: ztf[:, k, nodes(b, nt * P)], KC, ZB["2b"]))
            pe.wait_ge(sem["bn_applied"], 2 * KC)

            def turn_back(b, q, nt):
                wait(pe, sem["back_used"], b - 1)
                for j in range(nt):
                    for k in range(KC):
                        c = (j % 2) * D + k * P
                        src = ztf[:, k, nodes(b, nt * P)][:, j * P:(j + 1) * P]
                        mm = nc.tensor.transpose(ps[:, 2 * q + j // 2, c:c + P], src, ident[:, :])
                mm.then_inc(sem["back_psum"], 1)
            each_batch(turn_back)
            pe.wait_ge(sem["ln_done"], 4)
            pe.wait_ge(sem["weights_in"], WEIGHTS[3])

            def node_rows(b, q, nt):
                turn(3, X)(b, q, nt)
                wait(pe, sem["xT_sbuf"], b * 2 + (6 * NB + 2))
                rows_out(b, nt, lambda k, j: xT[:, q, k, j * P:(j + 1) * P], 0, 4, YB[3])
            each_batch(node_rows)
            pe.wait_ge(sem["s1_ready"], 1)
            nc.tensor.transpose(ps[0:T, 6, 0:P], s1[:, :], ident[:, :]).then_inc(sem["c_psum"], 1)
            pe.wait_ge(sem["c_ready"], 1)
            h = SLOTS // 2
            for j in range(2):
                nc.tensor.matmul(ps[:, 4 + j, 0:h], before[0:T, :], reset[0:T, j * h:(j + 1) * h], start=True,
                                 stop=True).then_inc(sem["c_psum"], 1)
            pe.wait_ge(sem["c_ready"], 4)

            def turn_logits(g, q):
                wait(pe, sem["mask_logit"], g + 1)
                wait(pe, sem["sel_ready"], g + (3 * GROUPS - 1))
                for j in range(G):
                    mm = nc.tensor.transpose(att_bank(q)[:, j * P:(j + 1) * P], logit[:, j, :], ident[:, :])
                mm.then_inc(sem["t_psum"], 1)

            def turn_probs(g, q):
                wait(pe, sem["probT_ready"], (g + 1) * G)
                for j in range(G):
                    mm = nc.tensor.transpose(att_bank(q)[:, j * P:(j + 1) * P], probT[:, j, :], ident[:, :])
                mm.then_inc(sem["p_psum"], 1)

            turn_logits(0, 0)
            turn_logits(1, 1)
            turn_probs(0, 0)

            def attend_round(i, last=False):
                for k in range(RG):
                    g = i * RG + k
                    if not last or k + 2 < RG:
                        turn_logits(g + 2, k % 2)
                    slot_sums(3, g, i, k)
                    if not last or k + 1 < RG:
                        turn_probs(g + 1, (k + 1) % 2)
            attend_round(0)
            with pe.Fori(1, ITERS - 1) as i:
                attend_round(i)
            attend_round(ITERS - 1, last=True)

        @block.vector
        def _(dve):
            chain = {"dve_chain": 0, "branch_chain": 0}
            linked = ["dve_chain"]

            def link(ins):
                n = linked[0]
                chain[n] += 1
                ins.then_inc(sem[n], 1)
                dve.wait_ge(sem[n], chain[n])

            v = nc.vector
            link(v.memset(X[:, T - 1, :], 0.0))
            v.memset(key[0][96:P, :], NO_NODE).then_inc(sem["zeroed"], 1)
            v.memset(key[1][96:P, :], NO_NODE).then_inc(sem["zeroed"], 1)
            v.memset(run[0][96:P, :], 0.0).then_inc(sem["zeroed"], 1)
            v.memset(attr[96:P, :, :, :], 0.0).then_inc(sem["zeroed"], 1)
            v.memset(next_key[:, :], NO_NODE).then_inc(sem["zeroed"], 1)
            for rec in (meta_src, meta_dst):
                link(v.memset(rec[:, :, :], 0.0))
                link(v.memset(rec[:, :, 0].bitcast(I32), OUT_OF_RANGE))
                v.memset(rec[:, :, 1], -1.0).then_inc(sem["zeroed"], 1)
            dve.wait_ge(sem["keys_in"], KEYS_IN)
            dve.wait_ge(sem["consts"], 5)
            link(v.tensor_copy(pay_src[:, :, 2], run[0]))
            link(v.tensor_copy(pay_src[:, :, 0].bitcast(I32), key[1]))
            link(v.tensor_copy(pay_dst[:, :, 0].bitcast(I32), key[0]))

            def tile_counts(n, which):
                link(v.tensor_scalar(ibuf, key[which], 7, None, ALU.arith_shift_right))
                link(v.tensor_copy(bucket, ibuf))
                if n == 1:
                    link(v.tensor_tensor(run[0][:, 0:COLS - 1], bucket[:, 1:], bucket[:, 0:COLS - 1], ALU.is_lt))
                    link(v.tensor_scalar(next_key[:, :], next_key[:, :], 7, None, ALU.arith_shift_right))
                    link(v.tensor_copy(unordered[:, 0:1], next_key[:, :]))
                    link(v.tensor_tensor(run[0][:, COLS - 1:], unordered[:, 0:1], bucket[:, COLS - 1:], ALU.is_lt))
                    link(v.tensor_reduce(unordered[:, 1:2], run[0], AX_X, ALU.add))
                with dve.Fori(0, T) as b:
                    v.tensor_scalar(mask[:, bass.ds(b, 1), :].rearrange("p o c -> p (o c)"), bucket,
                                    iota[:, bass.ds(b, 1)], None, ALU.is_equal, ALU.add,
                                    accum_out=small[:, which, bass.ds(b, 1)]).then_inc(sem["counted"], 1)
                dve.wait_ge(sem["prefix"], n + 1)
                link(v.tensor_copy(small[:, 5, :], ps[:, 7, 0:T]))
                if n == 1:
                    v.tensor_scalar(seen[:, :], ps[:, 7, 120:121], 1.0, None, ALU.min).then_inc(sem["order_known"], 1)
                    dve.wait_ge(sem["order_known"], 1)
                v.tensor_copy(small[:, 2, :], ps[:, 7, 64:64 + T]).then_inc(sem["prefix_out"], 1)
                dve.wait_ge(sem["prefix_out"], n + 1)

            def cut(into, x, add=0.0):
                link(v.tensor_scalar(small[:, 3, :].bitcast(I32), x, add, None, ALU.add))
                link(v.tensor_scalar(small[:, 3, :].bitcast(I32), small[:, 3, :].bitcast(I32), 7, None, ALU.arith_shift_right))
                link(v.tensor_copy(into, small[:, 3, :].bitcast(I32)))

            def tile_ends(n):
                link(v.tensor_tensor_scan(ends[:, n, 0, :], ones[:, 0:T], small[:, 4, :], 0.0, ALU.mult, ALU.add))
                v.tensor_tensor(ends[:, n, 1, :], ends[:, n, 0, :], small[:, 4, :], ALU.subtract).then_inc(sem["ends_ready"], 1)
                dve.wait_ge(sem["ends_ready"], n + 1)

            def rank_edges(n, which):
                link(v.tensor_scalar(rec_of[which], key[which], P - 1, None, ALU.bitwise_and))
                link(v.tensor_copy(pay[which][:, :, 1], rec_of[which]))
                link(v.memset(pos, float(NOWHERE)))
                cut(small[:, 4, :], small[:, 2, :], float(P - 1))
                tile_ends(n)
                link(v.scalar_tensor_tensor(small[:, 5, :], ends[:, n, 1, :], float(P), small[:, 5, :], ALU.mult, ALU.add))
                link(v.tensor_scalar(small[:, 5, :], small[:, 5, :], -1.0, None, ALU.add))

                for b in range(T):
                    wait(dve, sem["ranked"], which * T + b - 1)
                    v.tensor_tensor_scan(run[b % 2], ones[:, 0:1].to_broadcast([P, COLS]), mask[:, b, :],
                                         small[:, 5, b:b + 1], ALU.mult, ALU.add).then_inc(sem["scanned"], 1)
                    dve.wait_ge(sem["scanned"], which * T + b + 1)
                    wait(dve, sem["ranked"], which * T + b)
                    v.copy_predicated(pos, mask[:, b, :], run[b % 2]).then_inc(sem["ranked"], 1)
                dve.wait_ge(sem["ranked"], (which + 1) * T)
                lane, slot = run[0].bitcast(I32), run[1].bitcast(I32)
                link(v.tensor_copy(ibuf, pos))
                link(v.tensor_scalar(lane, ibuf, P - 1, None, ALU.bitwise_and))
                link(v.tensor_scalar(slot, ibuf, 7, None, ALU.arith_shift_right))
                v.scalar_tensor_tensor(rec_of[which], lane, float(SLOTS), slot, ALU.mult, ALU.add).then_inc(sem["record_ready"], 1)
                dve.wait_ge(sem["record_ready"], which + 1)

            def tiles_of_slots(n, into):
                dve.wait_ge(sem["endT_psum"], n + 1)
                w = 3 if n == 1 else 2
                v.tensor_copy(endT[0:T, n, 0:w], ps[0:T, 7, 128:128 + w]).then_inc(sem["endT_ready"], 1)
                dve.wait_ge(sem["endT_ready"], n + 1)
                v.tensor_scalar(past[0:T, :], slot_no[0:T, :], endT[0:T, n, 0:1], None, ALU.is_ge).then_inc(sem["past_ready"], 1)
                h = SLOTS // 2
                for j in range(2):
                    dve.wait_ge(sem["tile_psum"], 2 * n + j + 1)
                    v.tensor_scalar(into[:, j * h:(j + 1) * h], ps[:, 7, 0:h], float(T - 1), None,
                                    ALU.min).then_inc(sem["tile_ready"], 1)

            def rows_from(bank, b, nt, into, add, signal):
                src = psf[:, 512 * bank:512 * bank + nt * D].rearrange("p (t d) -> p t d", d=D)
                v.tensor_tensor(into, src, add, ALU.add).then_inc(sem[signal], 1)

            tile_counts(0, 0)
            rank_edges(0, 0)
            dve.wait_ge(sem["weights_in"], WEIGHTS[0])
            dve.wait_ge(sem["fill_in"], FILL_IN)
            dve.wait_ge(sem["table_in"], TABLE_IN[0])
            link(v.memset(z_bias, 0.0))
            for i in range(3):
                link(v.tensor_copy(term, left[i % 2]))
                link(v.tensor_copy(z_bias[32 * i:32 * i + 1, 0:D], term[32 * i:32 * i + 1, :]))
                if i < 2:
                    link(v.tensor_tensor(left[1 - i], left[i], term, ALU.subtract))
            v.memset(ones16, 1.0).then_inc(sem["split_ready"], 1)
            dve.wait_ge(sem["dve_chain"], chain["dve_chain"])
            v.memset(zsum[:, :, :, :], 0.0).then_inc(sem["split_ready"], 1)
            dve.wait_ge(sem["split_ready"], 2)
            dve.wait_ge(sem["w_ready"], 3)

            def edge_sums(i, u):
                q, n = u % 2, i * ES + u
                wait(dve, sem["edge_part"], n * 8)
                wait(dve, sem["ez_psum"], n + 1)
                for j in range(EC):
                    z = ps[:, 2 + 2 * q + j // 2, (j % 2) * D:(j % 2 + 1) * D]
                    v.scalar_tensor_tensor(relu_out[:, q, j, :], z, 0.0, a_relu, ALU.max, ALU.mult,
                                           accum_out=zsum[:, q, 0, j:j + 1]).then_inc(sem["edge_part"], 1)
                for j in range(EC):
                    v.scalar_tensor_tensor(line_out[:, q, j, :], attr[:, u % AR, j, :], 1.0, w_line, ALU.mult, ALU.mult,
                                           accum_out=zsum[:, q, 1, j:j + 1]).then_inc(sem["edge_part"], 1)
                wait(dve, sem["edge_part"], n * 8 + 8)
                v.scalar_tensor_tensor(pay_src[:, bass.ds(n * EC, EC), 3], zsum[:, q, 0, :], lin[:, KC:KC + 1],
                                       zsum[:, q, 1, :], ALU.add, ALU.add).then_inc(sem["pay_ready"], 1)

            def edge_round(i):
                for u in range(ES):
                    edge_sums(i, u)
            edge_round(0)
            tiles_of_slots(0, tile_src)
            with dve.Fori(1, SITERS) as i:
                edge_round(i)
            dve.wait_ge(sem["pay_ready"], ESTEPS)

            tile_counts(1, 1)
            link(v.tensor_tensor_scan(ends[:, 1, 0, :], ones[:, 0:T], small[:, 2, :], 0.0, ALU.mult, ALU.add))
            link(v.tensor_tensor(ends[:, 1, 1, :], ends[:, 1, 0, :], small[:, 2, :], ALU.subtract))
            cut(small[:, 4, :], ends[:, 1, 0, :], float(P - 1))
            cut(ends[:, 1, 2, :], ends[:, 1, 1, :])
            link(v.tensor_scalar(small[:, 3, :], small[:, 2, :], 1.0, None, ALU.min))
            link(v.tensor_tensor(small[:, 4, :], small[:, 4, :], ends[:, 1, 2, :], ALU.subtract))
            link(v.tensor_tensor(small[:, 4, :], small[:, 4, :], small[:, 3, :], ALU.mult))
            link(v.tensor_tensor_scan(ends[:, 1, 0, :], ones[:, 0:T], small[:, 4, :], 0.0, ALU.mult, ALU.add))
            link(v.tensor_tensor(ends[:, 1, 1, :], ends[:, 1, 0, :], small[:, 4, :], ALU.subtract))
            v.tensor_tensor(ends[:, 1, 2, :], ends[:, 1, 2, :], ends[:, 1, 1, :], ALU.subtract).then_inc(sem["ends_ready"], 1)
            tiles_of_slots(1, tile_dst)
            dve.wait_ge(sem["tile_ready"], 4)
            link(v.tensor_scalar(slot_of[0:T, :], slot_no[0:T, :], endT[0:T, 1, 1:2], None, ALU.is_ge))
            v.tensor_tensor(slot_of[0:T, :], slot_of[0:T, :], past[0:T, :], ALU.subtract).then_inc(sem["unit_values"], 1)
            dve.wait_ge(sem["unit_psum"], 1)
            link(v.memset(unit_at, 0))
            link(v.memset(unit_tile, 0.0))
            for c in range(UC):
                n = min(P, SLOTS - c * P)
                link(v.tensor_scalar(unit_tile[0:n, c:c + 1], ps[0:n, 7, UC + c:UC + c + 1], float(P), None, ALU.mult))
                link(v.tensor_scalar(unit_at[0:n, c:c + 1], ps[0:n, 7, c:c + 1], lane_no[0:n, 0:1], float(c * P), ALU.add, ALU.add))
            v.tensor_scalar(unit_at, unit_at, float(COLS - 1), None, ALU.min).then_inc(sem["units_known"], 1)
            dve.wait_ge(sem["units_in"], 16 * 2 * UC)
            rest = SLOTS - (UC - 1) * P
            for c0, c1, n in ((0, UC - 1, P), (UC - 1, UC, rest)):
                link(v.tensor_copy(unit_val[0][0:n, c0:c1, :], unit_row[0][0:n, c0:c1, :]))
                link(v.tensor_tensor(unit_val[1][0:n, c0:c1, :], unit_row[1][0:n, c0:c1, :],
                                     unit_tile[0:n, c0:c1].rearrange("p (c o) -> p c o", o=1).to_broadcast([n, c1 - c0, P]),
                                     ALU.subtract))
            dve.sem_inc(sem["unit_values"], 1)
            dve.wait_ge(sem["unit_psum"], 2)
            for i, col_i in enumerate((meta_dst[:, :, 0].bitcast(I32), meta_dst[:, :, 1])):
                for h in range(2):
                    n = min(4 * P, SLOTS - h * 4 * P)
                    link(v.tensor_copy(col_i[:, h * 4 * P:h * 4 * P + n], ps[:, 3 + 2 * i + h, 0:n]))
            dve.sem_inc(sem["dst_sorted"], 1)
            link(v.memset(ACC[:, :], 0.0))

            with dve.If(read_order(dve) > 0):
                linked[0] = "branch_chain"
                tile_counts(2, 1)
                rank_edges(2, 1)
                tiles_of_slots(2, tile_dst)
                dve.wait_ge(sem["records_dst"], 16)
                link(v.memset(ACC[:, :], 0.0))
                linked[0] = "dve_chain"
            for k in range(SG):
                dve.wait_ge(scattered[k], 16 * SC * SITERS)
            v.memset(ZT[:, :], 0.0).then_inc(sem["acc_zero"], 1)
            dve.wait_ge(sem["acc_zero"], 1)

            def select(layer, i, k):
                g = i * RG + k
                if layer != 2:
                    wait(dve, sem["summed"], g * G + (layer * SLOTS - G))
                m = meta[layer]
                c0 = i * R + k * G
                if layer == 2:
                    wait(dve, sem["scaled"], g)
                into, done = (other, "one_ready") if layer == 2 else (sel[:, k % 2, :, :], "sel_ready")
                v.tensor_tensor(into, iota[:, :].rearrange("p (o e) -> p o e", o=1).to_broadcast([P, G, P]),
                                m[:, bass.ds(c0, G), 1:2].to_broadcast([P, G, P]), ALU.is_equal).then_inc(sem[done], 1)

            def accumulate(layer, i, k):
                for j in range(G):
                    c = i * R + (k * G + j)
                    n = c + layer * SLOTS
                    t = dve.value_load(slot_tile[layer][0:1, bass.ds(c, 1)], min_val=0, max_val=T - 1)
                    dst = acc3[:, bass.ds(t, 1), 0:D].rearrange("p o d -> p (o d)")
                    wait(dve, sem["added"], n)
                    wait(dve, sem["summed"], slot_done(n, j))
                    v.tensor_tensor(dst, slot_sum(j), dst, ALU.add).then_inc(sem["added"], 1)

            def aggregate(layer, i, last=False):
                for k in range(RG):
                    if not (last and k == RG - 1):
                        if k < RG - 1:
                            select(layer, i, k + 1)
                        else:
                            select(layer, i + 1, 0)
                    accumulate(layer, i, k)

            def aggregate_all(layer):
                select(layer, 0, 0)
                if layer == 0:
                    aggregate(layer, 0)
                with dve.Fori(1 if layer == 0 else 0, ITERS - 1) as i:
                    aggregate(layer, i)
                aggregate(layer, ITERS - 1, last=True)
                dve.wait_ge(sem["added"], (layer + 1) * SLOTS)

            def by_tile(vec):
                return vec.rearrange("p (t o) -> p t o", o=1).to_broadcast([P, T, D])

            def by_feature(vec):
                return vec.rearrange("p (o d) -> p o d", o=1).to_broadcast([P, T, D])

            def layer_norm(n, affine):
                link(v.tensor_reduce(small[:, 0, :], accd, AX_X, ALU.add))
                link(v.tensor_scalar(small[:, 1, :], small[:, 0, :], 1.0 / D, None, ALU.mult))
                v.tensor_tensor(accd, accd, by_tile(small[:, 1, :]), ALU.subtract).then_inc(sem["ln_center"], 1)
                dve.wait_ge(sem["ln_square"], n)
                link(v.tensor_reduce(small[:, 2, :], zt3, AX_X, ALU.add))
                v.tensor_scalar(small[:, 3, :], small[:, 2, :], 1.0 / D, LN_EPS, ALU.mult, ALU.add).then_inc(sem["ln_var"], 1)
                dve.wait_ge(sem["ln_sqrt"], n)
                link(v.reciprocal(small[:, 5, :], small[:, 4, :]))
                if not affine:
                    v.tensor_tensor(X[:, :, :], accd, by_tile(small[:, 5, :]), ALU.mult).then_inc(sem["ln_done"], 1)
                    dve.wait_ge(sem["ln_done"], n)
                    return
                link(v.tensor_tensor(accd, accd, by_tile(small[:, 5, :]), ALU.mult))
                link(v.tensor_tensor(accd, accd, by_feature(bc[:, 1, :]), ALU.mult))
                link(v.tensor_tensor(accd, accd, by_feature(bc[:, 2, :]), ALU.add))
                v.scalar_tensor_tensor(accd, accd, 0.0, X[:, :, :], ALU.max, ALU.add).then_inc(sem["ln_done"], 1)
                dve.wait_ge(sem["ln_done"], n)

            dve.wait_ge(sem["records_in"], 16)
            aggregate_all(0)
            link(v.tensor_tensor(accd, accd, X[:, :, :], ALU.add))
            layer_norm(1, False)
            link(v.memset(ACC[:, :], 0.0))
            aggregate_all(1)
            link(v.tensor_scalar(small[:, 0, 0:2], col[:, EPS1:EPS2 + 1], 1.0, None, ALU.add))
            v.scalar_tensor_tensor(accd, X[:, :, :], small[:, 0, 0:1], accd, ALU.mult, ALU.add).then_inc(sem["agg_ready"], 1)
            dve.wait_ge(sem["weights_in"], WEIGHTS[1])

            def mlp1(b, q, nt):
                wait(dve, sem["y_psum"], b + (YB[1] + 1))
                rows_from(6, b, nt, tiles(accd, b, nt), tiles(X[:, :, :], b, nt), "y_used")
            batches(dve, mlp1)
            dve.wait_ge(sem["y_used"], YB[1] + NB)
            link(v.tensor_tensor(accd, accd, by_feature(bc[:, 0, :]), ALU.add))
            layer_norm(2, True)
            layer_norm(3, False)
            link(v.memset(ACC[:, :], 0.0))
            aggregate_all(2)
            link(v.tensor_scalar(small[:, 0, 0:2], col[:, EPS1:EPS2 + 1], 1.0, None, ALU.add))
            v.scalar_tensor_tensor(accd, X[:, :, :], small[:, 0, 1:2], accd, ALU.mult, ALU.add).then_inc(sem["agg_ready"], 1)
            for which, (g, be) in enumerate(((G1, BE1), (G2, BE2))):
                def gather_stats(b, q, nt):
                    wait(dve, sem["z_sbuf"], b * 2 + 2 * (ZB[2] + which * NB + 1))
                    n = nt * P if not isinstance(b, int) else min(nt * P, N_NODES - b * SB * P)
                    for m in range(KC):
                        v.bn_stats(stats[:, m, bass.ds(b, 1), :].rearrange("p o s -> p (o s)"),
                                   ztf[:, m, nodes(b, n)]).then_inc(sem["bn_in"], 1)
                if which:
                    dve.wait_ge(sem["bn_applied"], KC)
                batches(dve, gather_stats)
                dve.wait_ge(sem["bn_in"], (which + 1) * NB * KC)
                for m in range(KC):
                    link(v.bn_aggr(mv[:, m, 0:2], stats[:, m, :, :].rearrange("p b s -> p (b s)")))
                v.tensor_scalar(mv[:, :, 2], mv[:, :, 1], BN_EPS, None, ALU.add).then_inc(sem["bn_var"], 1)
                dve.wait_ge(sem["bn_sqrt"], which + 1)
                link(v.reciprocal(mv[:, :, 4], mv[:, :, 3]))
                link(v.tensor_tensor(mv[:, :, 5], mv[:, :, 4], col[:, g:g + 2], ALU.mult))
                link(v.tensor_tensor(mv[:, :, 7], mv[:, :, 0], mv[:, :, 5], ALU.mult))
                v.tensor_tensor(mv[:, :, 6], col[:, be:be + 2], mv[:, :, 7], ALU.subtract).then_inc(sem["bn_scale"], 1)
                dve.wait_ge(sem["bn_scale"], which + 1)

            def back(b, q, nt):
                wait(dve, sem["back_psum"], b + 1)
                rows_from(2 * q, b, nt, tiles(accd, b, nt), tiles(X[:, :, :], b, nt), "back_used")
            batches(dve, back)
            dve.wait_ge(sem["back_used"], NB)
            layer_norm(4, False)
            dve.wait_ge(sem["weights_in"], WEIGHTS[3])

            def node_rows(b, q, nt):
                wait(dve, sem["y_psum"], b + (YB[3] + 1))
                wait(dve, sem["ln_square"], 4)
                rows_from(4, b, nt, tiles(ht, b, nt)[:, :, 0:D], bc[:, 0:1, :].to_broadcast([P, nt, D]), "y_used")
            batches(dve, node_rows)
            dve.wait_ge(sem["y_used"], YB[3] + NB)
            link(v.memset(ht[:, :, D:D + 1], 1.0))
            link(v.scalar_tensor_tensor(ht[:, :, 0:D], ht[:, :, 0:D], SLOPE, ht[:, :, 0:D], ALU.mult, ALU.max))
            link(v.tensor_tensor(accd, ht[:, :, 0:D], by_feature(bc[:, 1, :]), ALU.mult))
            link(v.tensor_reduce(s1[:, :], accd, AX_X, ALU.add))
            v.tensor_scalar(s1[:, :], s1[:, :], col[:, AB:AB + 1], None, ALU.add).then_inc(sem["s1_ready"], 1)
            link(v.tensor_tensor(accd, ht[:, :, 0:D], by_feature(bc[:, 2, :]), ALU.mult))
            link(v.tensor_reduce(s2[:, :], accd, AX_X, ALU.add))
            v.tensor_copy(ht[:, :, D + 1], s2[:, :]).then_inc(sem["ht_ready"], 1)
            link(v.tensor_scalar(cslot[0:T, :], slot_no[0:T, :], endT[0:T, 0, 0:1], None, ALU.is_ge))
            link(v.tensor_scalar(reset[0:T, :], slot_no[0:T, :], endT[0:T, 0, 1:2], None, ALU.is_ge))
            link(v.tensor_tensor(reset[0:T, :], reset[0:T, :], cslot[0:T, :], ALU.subtract))
            dve.wait_ge(sem["c_psum"], 1)
            v.tensor_copy(before[0:T, :], ps[0:T, 6, 0:P]).then_inc(sem["c_ready"], 1)
            h = SLOTS // 2
            for j in range(2):
                dve.wait_ge(sem["c_psum"], 2 + j)
                v.tensor_copy(cslot[:, j * h:(j + 1) * h], ps[:, 4 + j, 0:h]).then_inc(sem["c_ready"], 1)
            link(v.memset(reset[:, 0:1], -BIG))
            link(v.tensor_tensor(reset[:, 1:], tile_src[:, 1:], tile_src[:, 0:SLOTS - 1], ALU.not_equal))
            link(v.tensor_scalar(reset[:, 1:], reset[:, 1:], -BIG, None, ALU.mult))
            link(v.memset(wsum[:, :], 0.0))
            link(v.memset(ACC[:, :], 0.0))
            v.memset(runmax[:, :, :], FLOOR).then_inc(sem["c_ready"], 1)
            dve.wait_ge(sem["c_ready"], 4)
            dve.wait_ge(sem["table_in"], TABLE_IN[3])

            def edge_values(i, k):
                g = i * RG + k
                dve.wait_ge(gathered[k], i * (16 * G) + (3 * ITERS + 1) * 16 * G)
                slots = bass.ds(i * R + k * G, G)
                wait(dve, sem["mask_part"], g * G)
                v.tensor_tensor(ev[:, :], ring[:, k * G:(k + 1) * G, D + 1], meta_src[:, slots, 3],
                                ALU.add).then_inc(sem["ev_ready"], 1)
                v.tensor_tensor(other, iota[:, :].rearrange("p (o e) -> p o e", o=1).to_broadcast([P, G, P]),
                                meta_src[:, slots, 1:2].to_broadcast([P, G, P]), ALU.not_equal).then_inc(sem["ne_ready"], 1)

            MAX_STEPS = 5

            def maxima(i, k):
                g, q = i * RG + k, k % 2
                slots = bass.ds(i * R + k * G, G)
                now = runmax[:, q, 1:1 + G]
                steps = [0]

                def step(ins):
                    steps[0] += 1
                    ins.then_inc(sem["max_ready"], 1)
                    dve.wait_ge(sem["max_ready"], g * MAX_STEPS + steps[0])
                dve.wait_ge(sem["t_psum"], g + 1)
                step(v.tensor_reduce(att[:, 1, :], att_bank(q).rearrange("p (s e) -> p s e", e=P), AX_X, ALU.max))
                step(v.scalar_tensor_tensor(att[:, 2, :], att[:, 1, :], FLOOR, cslot[:, slots], ALU.max, ALU.add))
                step(v.tensor_copy(runmax[:, q, 0:1], runmax[:, 1 - q, G:G + 1]))
                step(v.tensor_tensor_scan(now, reset[:, slots], att[:, 2, :], runmax[:, q, 0:1], ALU.add, ALU.max))
                step(v.tensor_tensor(att[:, 3, :], runmax[:, q, 0:G], reset[:, slots], ALU.add))
                wait(dve, sem["corr_ready"], g)
                v.tensor_tensor(att[:, 4, :], att[:, 3, :], now, ALU.subtract).then_inc(sem["bias_ready"], 1)
                v.tensor_tensor(bias[:, q, :], cslot[:, slots], now, ALU.subtract).then_inc(sem["bias_ready"], 1)

            def rescale_add(i, k):
                g, q = i * RG + k, k % 2
                dve.wait_ge(sem["corr_ready"], g + 1)
                dve.wait_ge(sem["probT_ready"], g * G + G)
                wait(dve, sem["run_done"], g)
                c = bass.ds(i * R + (k * G + 1), G)
                v.tensor_tensor_scan(wsum[:, c], corr[:, q, :], rsum[:, q, :], wsum[:, bass.ds(i * R + k * G, 1)],
                                     ALU.mult, ALU.add).then_inc(sem["run_done"], 1)
                for j in range(G):
                    c = i * R + (k * G + j)
                    n = c + 3 * SLOTS
                    t = dve.value_load(tile_src[0:1, bass.ds(c, 1)], min_val=0, max_val=T - 1)
                    dst = acc3[:, bass.ds(t, 1), 0:D].rearrange("p o d -> p (o d)")
                    wait(dve, sem["added"], n)
                    wait(dve, sem["summed"], slot_done(n, j))
                    v.scalar_tensor_tensor(dst, dst, corr[:, q, j:j + 1], slot_sum(j), ALU.mult,
                                           ALU.add).then_inc(sem["added"], 1)

            def after(i, k, n):
                return (i, k + n) if k + n < RG else (i + 1, k + n - RG)

            def attend_round(i, last=False):
                for k in range(RG):
                    if not last or k + 1 < RG:
                        maxima(*after(i, k, 1))
                    if not last or k + 3 < RG:
                        edge_values(*after(i, k, 3))
                    rescale_add(i, k)
            edge_values(0, 0)
            edge_values(0, 1)
            edge_values(0, 2)
            maxima(0, 0)
            attend_round(0)
            with dve.Fori(1, ITERS - 1) as i:
                attend_round(i)
            attend_round(ITERS - 1, last=True)
            dve.wait_ge(sem["added"], 4 * SLOTS)
            dve.wait_ge(sem["run_done"], GROUPS)
            link(v.tensor_copy(small[:, 1, :].bitcast(I32), ends[:, 0, 0, :]))
            with dve.Fori(0, T) as t:
                e = dve.value_load(small[0:1, 1, bass.ds(t, 1)].bitcast(I32), min_val=0, max_val=SLOTS)
                v.tensor_copy(small[:, 2, bass.ds(t, 1)], wsum[:, bass.ds(e, 1)]).then_inc(sem["weight_ready"], 1)
            dve.wait_ge(sem["weight_ready"], T)
            link(v.tensor_scalar(small[:, 0, :], small[:, 2, :], 1e-30, None, ALU.max))
            link(v.reciprocal(small[:, 1, :], small[:, 0, :]))
            link(v.tensor_tensor(accd, accd, by_tile(small[:, 1, :]), ALU.mult))
            link(v.scalar_tensor_tensor(accd, accd, SLOPE, accd, ALU.mult, ALU.max))
            link(v.tensor_tensor(accd, accd, X[:, :, :], ALU.add))
            layer_norm(5, False)


INPUTS = ["x", "src", "dst", "edge_attr_128", "edge_weight", "L0_gnn_W", "L0_gnn_b", "L1_gnn_W1", "L1_gnn_b1",
          "L1_gnn_W2", "L1_gnn_b2", "L1_gnn_eps", "L1_gnn_gamma", "L1_gnn_beta", "L2_gnn_eps", "L2_gnn_W1",
          "L2_gnn_b1", "L2_gnn_g1", "L2_gnn_be1", "L2_gnn_W2", "L2_gnn_b2", "L2_gnn_g2", "L2_gnn_be2",
          "L3_gnn_w_W", "L3_gnn_w_b", "L3_gnn_ew_W", "L3_gnn_ew_b", "L3_gnn_a_W", "L3_gnn_a_b"]


def kernel(**inputs):
    import numpy as np
    import concourse.bacc as bacc
    from concourse import mybir
    from concourse.bass_utils import run_bass_kernel_spmd as run

    nc = bacc.Bacc("TRN2", target_bir_lowering=False, num_devices=1)
    arrays, args = {}, {}
    for name in INPUTS:
        v = np.ascontiguousarray(inputs[name])
        if v.ndim == 0:
            v = v.reshape(1)
        arrays[f"in_{name}"] = v
        args[name] = nc.dram_tensor(f"in_{name}", v.shape, mybir.dt.from_np(v.dtype), kind="ExternalInput").ap()
    out = nc.dram_tensor("out", (N_NODES, D), mybir.dt.float32, kind="ExternalOutput").ap()
    gnn_program(nc, args, out)
    return run(nc, [arrays], core_ids=[0]).results[0]["out"]
```

```python
from contextlib import ExitStack

import concourse.bass as bass
from concourse import mybir

P = 128
ALU = mybir.AluOpType
ACT = mybir.ActivationFunctionType
F32 = mybir.dt.float32
I32 = mybir.dt.int32
BF16 = mybir.dt.bfloat16
U8 = mybir.dt.uint8
AX_X = mybir.AxisListType.X

N_NODES = 6250
N_EDGES = 100000
D = 256
D_EDGE = 128
KC = D // P
T = -(-N_NODES // P)
LAST = N_NODES - (T - 1) * P
NPAD = T * P
COLS = 800
EP = N_EDGES // COLS
SLOPE = 0.2
LN_EPS = 1e-5
BN_EPS = 1e-5

G = 8
RG = 4
R = G * RG
MOST_SLOTS = (N_EDGES + T * (P - 1)) // P
ITERS = -(-MOST_SLOTS // R)
SLOTS = ITERS * R
GROUPS = SLOTS // G
RECORDS = P * SLOTS
UC = -(-SLOTS // P)
assert N_EDGES // P + 1 + T - 1 <= SLOTS

SC = 8
SG = 4
SITERS = COLS // (SC * SG)
EC = 4
ES = SC * SG // EC
AR = 4
OUT_OF_RANGE = 1 << 20
NOWHERE = 127 + P * 50000
NO_NODE = 8191
BIG = 1e30
FLOOR = -1e20
HW = D + 1
SB = 4
NB = -(-T // SB)
assert EP * COLS == N_EDGES and SB * (NB - 1) + 1 == T and NB % 2 and SITERS * SC * SG == COLS


def wait(eng, sem, n):
    if not isinstance(n, int) or n > 0:
        eng.wait_ge(sem, n)


def rounds(eng, n, body, first=True):
    if first:
        body(0)
    with eng.Fori(1 if first else 0, n) as i:
        body(i)


def batches(eng, body):
    body(0, 0, SB)
    body(1, 1, SB)
    with eng.Fori(1, (NB - 1) // 2) as i:
        for q in range(2):
            body(i * 2 + q, q, SB)
    body(NB - 1, 0, 1)


def staggered(eng, ahead, behind):
    def body(b, q, nt):
        ahead(b, q, nt)
        if not isinstance(b, int) or b > 0:
            behind(b - 1, 1 - q, SB)
    batches(eng, body)
    behind(NB - 1, 0, 1)


def each_batch(body):
    for b in range(NB):
        body(b, b % 2, min(SB, T - b * SB))


def gnn_program(nc, a, out):
    with ExitStack() as ctx:
        def sb(name, shape, dt=F32):
            return ctx.enter_context(nc.sbuf_tensor(name, shape, dt))

        table = [nc.dram_tensor(f"table{i}", [NPAD, HW if i == 3 else D], F32).ap() for i in range(4)]
        rec_src = nc.dram_tensor("rec_src", [RECORDS, 4], F32).ap()
        rec_dst = nc.dram_tensor("rec_dst", [RECORDS, 2], F32).ap()
        row_src = nc.dram_tensor("row_src", [P * COLS // P, P], I32).ap()
        row_dst = nc.dram_tensor("row_dst", [P * COLS // P, P], I32).ap()

        X = sb("X", [P, T, D])
        ACC = sb("ACC", [P, T * D])
        ZT = sb("ZT", [P, T * HW])
        meta_src = sb("meta_src", [P, SLOTS, 4])
        meta_dst = sb("meta_dst", [P, SLOTS, 2])
        tile_src = sb("tile_src", [P, SLOTS], I32)
        tile_dst = sb("tile_dst", [P, SLOTS], I32)
        reset = sb("reset", [P, SLOTS])
        cslot = sb("cslot", [P, SLOTS])
        W = sb("W", [P, 2 * KC, D])
        bc = sb("bc", [P, 3, D])
        ewW = sb("ewW", [P, D])
        xT = sb("xT", [P, 2, KC, SB * P])
        z1 = sb("z1", [P, SB * D])
        ident = sb("ident", [P, P])
        iota = sb("iota", [P, P])
        ones = sb("ones", [P, P])
        before = sb("before", [P, P])
        col = sb("col", [P, 24])
        ends = sb("ends", [P, 3, 3, T])
        small = sb("small", [P, 6, T])
        s1 = sb("s1", [P, T])
        s2 = sb("s2", [P, T])
        lin = sb("lin", [P, KC + 1])
        zsum = sb("zsum", [P, 2, 2, EC])
        endT = sb("endT", [P, 3, 3])
        next_key = sb("next_key", [P, 1], I32)
        unordered = sb("unordered", [P, 2])
        seen = sb("seen", [P, 1], I32)
        gidx = sb("gidx", [P, RG, G], I32)
        sidx = sb("sidx", [P, SG, SC], I32)
        spay = sb("spay", [P, SG, SC, 4])
        token = sb("token", [P, 1])
        lane_no = sb("lane_no", [P, 1])
        att = sb("att", [P, 5, G])
        runmax = sb("runmax", [P, 2, 1 + G])
        corr = sb("corr", [P, 2, G])
        rsum = sb("rsum", [P, 2, G])
        ev = sb("ev", [P, G])
        bias = sb("bias", [P, 2, G])
        mv = sb("mv", [P, KC, 8])

        acc3 = ACC[:, :].rearrange("p (t w) -> p t w", w=D)
        accd = acc3[:, :, 0:D]
        ztf = ZT[:, 0:KC * NPAD].rearrange("p (k n) -> p k n", k=KC)
        ht = ZT[:, :].rearrange("p (t w) -> p t w", w=HW)

        ring = ZT[:, 0:R * HW].rearrange("p (s w) -> p s w", w=HW)
        o = R * HW
        logit = ZT[:, o:o + G * P].rearrange("p (s e) -> p s e", e=P)
        o += G * P
        probT = ZT[:, o:o + G * P].rearrange("p (s e) -> p s e", e=P)
        assert o + G * P <= T * HW
        sel = xT[:, :, :, :].rearrange("p q k n -> p q (k n)")[:, :, 0:G * P].rearrange("p b (s e) -> p b s e", e=P)
        other_out = z1[:, :].rearrange("p (q j d) -> p q j d", q=1, j=SB)
        other = z1[:, 0:G * P].rearrange("p (s e) -> p s e", e=P)

        rows_ = ZT[:, 0:15 * COLS].rearrange("p (r c) -> p r c", c=COLS)
        key = [rows_[:, 0].bitcast(I32), rows_[:, 1].bitcast(I32)]
        bucket, pos = rows_[:, 2], rows_[:, 3]
        run = [rows_[:, 4], rows_[:, 5]]
        ibuf = rows_[:, 6].bitcast(I32)
        rec_of = [rows_[:, 7].bitcast(I32), rows_[:, 8].bitcast(I32)]
        pay_src = ZT[:, 9 * COLS:13 * COLS].rearrange("p (c f) -> p c f", f=4)
        pay_dst = ZT[:, 13 * COLS:15 * COLS].rearrange("p (c f) -> p c f", f=2)
        pay = [pay_src, pay_dst]
        mask = ACC[:, 0:T * COLS // 4].bitcast(U8).rearrange("p (b c) -> p b c", b=T)
        o = T * COLS // 4
        attr = ACC[:, o:o + AR * EC * D_EDGE].rearrange("p (b c d) -> p b c d", b=AR, d=D_EDGE)
        assert o + AR * EC * D_EDGE <= T * D
        slot_no, past = reset, cslot
        stats = cslot[:, 0:KC * NB * 6].rearrange("p (k b s) -> p k b s", k=KC, b=NB)
        o = 2 * COLS
        slot_of = ZT[:, o:o + SLOTS]
        o += SLOTS
        unit_row = [ZT[:, o + i * UC * P:o + (i + 1) * UC * P].bitcast(I32).rearrange("p (c e) -> p c e", e=P)
                    for i in range(2)]
        unit_val = [ZT[:, o + i * UC * P:o + (i + 1) * UC * P].rearrange("p (c e) -> p c e", e=P)
                    for i in range(2)]
        o += 2 * UC * P
        unit_at = ZT[:, o:o + UC].bitcast(I32)
        unit_tile = ZT[:, o + UC:o + 2 * UC]
        assert o + 2 * UC <= 6 * COLS
        wsum = meta_dst[:, :, :].rearrange("p s f -> p (s f)")[:, 0:SLOTS + 1]
        flat_src = meta_src[:, :, :].rearrange("p s f -> p (s f)")
        relu_out = flat_src[:, 0:2 * EC * D].rearrange("p (q j d) -> p q j d", q=2, j=EC)
        line_out = flat_src[:, 2 * EC * D:2 * EC * (D + P)].rearrange("p (q j d) -> p q j d", q=2, j=EC)
        a_relu = bc[:, 1, :]
        ewT = z1[:, 0:D]
        w_line = z1[:, D:D + P]
        z_bias = z1[:, 384:640].bitcast(BF16)
        ones16 = z1[:, 640:704].bitcast(BF16)
        term = z1[:, 704:832].bitcast(BF16)
        left = [bc[:, 2, :], relu_out[:, 0, 0, :]]
        attrT = xT[:, :, :, :].rearrange("p q k n -> p (q k) n")
        meta = [meta_src, meta_dst, meta_src, meta_src]
        slot_tile = [tile_src, tile_dst, tile_src, tile_src]

        def norms(n):
            o = 160 + (2 * SB * 12 if n == 2 else 0)
            return cslot[:, o:o + 2 * SB * 12].rearrange("p (q j s) -> p q j s", q=2, j=SB)

        EWB, A3, B1, L2B1, G1, BE1, L2B2, G2, BE2 = range(0, 18, 2)
        EPS1, EPS2, AB = 18, 19, 20

        ps = ctx.enter_context(nc.psum_tensor("ps", [P, 8, 512], F32))
        psf = ps[:, :, :].rearrange("p b c -> p (b c)")

        def slot_sum(j):
            return ps[:, j // 2, (j % 2) * D:(j % 2 + 1) * D]

        def slot_done(n, j):
            return n + (2 if j % 2 == 0 and j + 1 < G else 1)

        def att_bank(q):
            return psf[:, (4 + 2 * q) * 512:(4 + 2 * q) * 512 + G * P]

        names = """units_known units_in unit_values unit_psum dst_sorted order_known branch_chain
          records_dst scat2_ready token2 edge_part split_ready w_ready weighed one_ready
          scaled mask_part run_done weight_ready prefix_out ew_psum lin_ready consts
          ident_ready zeroed keys_in x_in fill_in records_in table_in stored weights_in
          cols_in dve_chain counted prefix scanned ranked record_ready ends_ready
          endT_psum endT_ready past_ready tile_psum tile_ready wT_psum wT_ready xT_psum
          xT_sbuf z_psum z_sbuf y_psum y_used attrT_psum attrT_sbuf ez_psum pay_ready
          scat_ready idx_ready idx_token sel_ready summed added acc_zero eps_ready
          ln_step0 ln_step1 ln_step2 ln_step3 stats_may act_may ln_step4 ln_step5
          ln_step_a ln_step_b ln_step_c rows_done acc_init scale_ready acc_scaled bn_in
          bn_var bn_sqrt bn_scale bn_applied back_psum back_used s1_ready h_step c_psum
          c_ready ht_ready ev_ready ne_ready mask_logit t_psum max_ready bias_ready
          corr_ready probT_ready p_psum"""
        sem = {n: ctx.enter_context(nc.semaphore(n)) for n in names.split()}
        gathered = [ctx.enter_context(nc.semaphore(f"gathered{i}")) for i in range(RG)]
        scattered = [ctx.enter_context(nc.semaphore(f"scattered{i}")) for i in range(SG)]
        ln_var = [ctx.enter_context(nc.semaphore(f"ln_var{i}")) for i in range(5)]
        ln_ready = [ctx.enter_context(nc.semaphore(f"ln_ready{i}")) for i in range(5)]
        ln_sqrt = [ctx.enter_context(nc.semaphore(f"ln_sqrt{i}")) for i in range(5)]
        scattered2 = [ctx.enter_context(nc.semaphore(f"scattered2_{i}")) for i in range(SG)]
        attr_in = [ctx.enter_context(nc.semaphore(f"attr_in{i}")) for i in range(AR)]

        TABLE_IN = [16 * NB * (i + 1) for i in range(4)]
        WEIGHTS = [80, 160, 192, 256]
        ZB = {1: 0, 2: NB, "2b": 2 * NB}
        YB = {0: 0, 1: NB, 3: 2 * NB}
        ESTEPS = COLS // EC
        KEYS_IN = 7 * 16
        LN_PLACE = {0: 0, 2: 1, 3: 2, 4: 3}
        FILL_IN = 4 * 16

        def tiles(view, b, nt):
            return view[:, b * SB:b * SB + nt] if isinstance(b, int) else view[:, bass.ds(b * SB, nt)]

        def nodes(b, n):
            return slice(b * SB * P, b * SB * P + n) if isinstance(b, int) else bass.ds(b * (SB * P), n)

        def nodes_of(b, nt):
            return slice(b * SB, b * SB + nt) if isinstance(b, int) else bass.ds(b * SB, nt)

        block = ctx.enter_context(nc.Block())

        def read_order(eng):
            eng.wait_ge(sem["order_known"], 1)
            return eng.value_load(seen[0:1, 0:1], min_val=0, max_val=1)

        @block.sync
        def _(sp):
            sp.wait_ge(sem["zeroed"], 7)
            with nc.allow_non_contiguous_dma(reason="one word a partition, once"):
                sp.dma_start(next_key[0:EP - 1, :], a["dst"].rearrange("(p c) -> p c", c=COLS)[1:EP, 0:1]).then_inc(sem["keys_in"], 16)
            for into, dram in ((key[0], a["src"]), (key[1], a["dst"]), (run[0], a["edge_weight"])):
                rows = dram.rearrange("(p c) -> p c", c=COLS)
                sp.dma_start(into[0:120, :], rows[0:120, :]).then_inc(sem["keys_in"], 16)
                sp.dma_start(into[120:EP, :], rows[120:EP, :]).then_inc(sem["keys_in"], 16)
            sp.dma_start(X[:, 0:T - 1, :], a["x"][0:(T - 1) * P, :].rearrange("(t p) d -> p t d", p=P)).then_inc(sem["x_in"], 16)
            sp.dma_start(X[0:LAST, T - 1, :], a["x"][(T - 1) * P:, :]).then_inc(sem["x_in"], 16)
            sp.dma_start(W[:, 0:KC, :], a["L0_gnn_W"].rearrange("(m p) d -> p m d", p=P)).then_inc(sem["weights_in"], 16)
            sp.dma_start(bc[:, 0, :], a["L0_gnn_b"].rearrange("(a d) -> a d", a=1).to_broadcast([P, D])).then_inc(sem["weights_in"], 16)
            sp.dma_start(ewW[:, :], a["L3_gnn_ew_W"]).then_inc(sem["weights_in"], 16)
            aw = a["L3_gnn_a_W"].rearrange("n o -> (n o)")
            sp.dma_start(bc[:, 1, :], aw[2 * D:3 * D].rearrange("(a d) -> a d", a=1).to_broadcast([P, D])).then_inc(sem["weights_in"], 16)
            sp.dma_start(bc[:, 2, :], a["L3_gnn_ew_b"].rearrange("(a d) -> a d", a=1).to_broadcast([P, D])).then_inc(sem["weights_in"], 16)
            with nc.allow_non_contiguous_dma(reason="a few hundred words, once"):
                for c, v in ((EWB, a["L3_gnn_ew_b"]), (A3, aw[2 * D:3 * D]), (B1, a["L1_gnn_b1"]),
                             (L2B1, a["L2_gnn_b1"]), (G1, a["L2_gnn_g1"]), (BE1, a["L2_gnn_be1"]),
                             (L2B2, a["L2_gnn_b2"]), (G2, a["L2_gnn_g2"]), (BE2, a["L2_gnn_be2"])):
                    sp.dma_start(col[:, c:c + 2], v.rearrange("(m p) -> p m", p=P)).then_inc(sem["cols_in"], 16)
                for c, v in ((EPS1, a["L1_gnn_eps"]), (EPS2, a["L2_gnn_eps"]), (AB, a["L3_gnn_a_b"])):
                    sp.dma_start(col[:, c:c + 1], v.rearrange("(a d) -> a d", a=1).to_broadcast([P, 1])).then_inc(sem["cols_in"], 16)
            sp.dma_start(rec_src.rearrange("(l s) f -> l s f", l=P), meta_src[:, :, :]).then_inc(sem["fill_in"], 16)
            sp.dma_start(rec_dst.rearrange("(l s) f -> l s f", l=P), meta_dst[:, :, :]).then_inc(sem["fill_in"], 16)

            sp.wait_ge(sem["keys_in"], KEYS_IN)
            for rows, into in ((row_src, key[0]), (row_dst, key[1])):
                sp.dma_start(rows.rearrange("r e -> (r e)").rearrange("(p c) -> p c", c=COLS), into).then_inc(sem["fill_in"], 16)

            def store0(b, q, nt):
                wait(sp, sem["y_used"], b + 1)
                rows = table[0][nodes(b, nt * P), :]
                sp.dma_start(rows.rearrange("(t p) d -> p t d", p=P),
                             z1[:, 0:nt * D].rearrange("p (t d) -> p t d", d=D)).then_inc(sem["table_in"], 16)
            batches(sp, store0)

            rows = a["edge_attr_128"].rearrange("(p c) d -> p c d", c=COLS)

            def load_attr(i):
                for u in range(ES):
                    n = i * ES + u
                    wait(sp, sem["pay_ready"], n - (AR - 1))
                    c = bass.ds(n * EC, EC)
                    sp.dma_start(attr[0:120, u % AR, :, :], rows[0:120, c, :]).then_inc(attr_in[u % AR], 16)
                    sp.dma_start(attr[120:EP, u % AR, :, :], rows[120:EP, c, :]).then_inc(attr_in[u % AR], 16)
            rounds(sp, SITERS, load_attr)

            for k in range(SG):
                sp.wait_ge(scattered[k], 16 * SC * SITERS)
            sp.dma_start(meta_src[:, :, :], rec_src.rearrange("(l s) f -> l s f", l=P)).then_inc(sem["records_in"], 16)
            with sp.If(read_order(sp) > 0):
                sp.wait_ge(sem["dst_sorted"], 1)
                for k in range(SG):
                    sp.wait_ge(scattered2[k], 16 * SC * SITERS)
                sp.dma_start(meta_dst[:, :, :], rec_dst.rearrange("(l s) f -> l s f", l=P)).then_inc(sem["records_dst"], 16)
                sp.wait_ge(sem["records_dst"], 16)

            def load_weights(w1, w2, vectors):
                for j, w in ((0, w1), (KC, w2)):
                    if w is not None:
                        sp.dma_start(W[:, j:j + KC, :], w.rearrange("(m p) d -> p m d", p=P)).then_inc(sem["weights_in"], 16)
                for j, v in enumerate(vectors):
                    sp.dma_start(bc[:, j, :], v.rearrange("(a d) -> a d", a=1).to_broadcast([P, D])).then_inc(sem["weights_in"], 16)

            def store_x(layer):
                def body(b, q, nt):
                    wait(sp, sem["rows_done"], b + ((layer - 1) * NB + 1))
                    sp.dma_start(table[layer][nodes(b, nt * P), :].rearrange("(t p) d -> p t d", p=P),
                                 tiles(X, b, nt)).then_inc(sem["table_in"], 16)
                batches(sp, body)

            store_x(1)
            load_weights(a["L1_gnn_W1"], a["L1_gnn_W2"], (a["L1_gnn_b2"], a["L1_gnn_gamma"], a["L1_gnn_beta"]))
            store_x(2)
            load_weights(a["L2_gnn_W1"], a["L2_gnn_W2"], ())
            sp.wait_ge(sem["back_psum"], NB)
            load_weights(a["L3_gnn_w_W"], None, (a["L3_gnn_w_b"], aw[0:D], aw[D:2 * D]))

            def store_h(b, q, nt):
                wait(sp, sem["ht_ready"], b + 1)
                sp.dma_start(table[3][nodes(b, nt * P), :].rearrange("(t p) d -> p t d", p=P),
                             tiles(ht, b, nt)).then_inc(sem["table_in"], 16)
            batches(sp, store_h)

            def store_out(b, q, nt):
                wait(sp, sem["rows_done"], b + (3 * NB + 1))
                if nt == SB:
                    sp.dma_start(out[nodes(b, nt * P), :].rearrange("(t p) d -> p t d", p=P),
                                 tiles(X, b, nt)).then_inc(sem["stored"], 16)
                else:
                    sp.dma_start(out[b * SB * P:, :], X[0:LAST, b * SB, :]).then_inc(sem["stored"], 16)
            batches(sp, store_out)
            sp.wait_ge(sem["stored"], 16 * NB)

        @block.gpsimd
        def _(pool):
            pool.memset(ones[:, :], 1.0).then_inc(sem["consts"], 1)
            pool.memset(ident[:, :], 0.0).then_inc(sem["consts"], 1)
            pool.memset(token[:, :], 0.0).then_inc(sem["idx_token"], 1)
            pool.iota(iota[:, :], [[1, P]], base=0, channel_multiplier=0,
                      allow_small_or_imprecise_dtypes=True).then_inc(sem["consts"], 1)
            pool.iota(slot_no[:, :], [[1, SLOTS]], base=0, channel_multiplier=0,
                      allow_small_or_imprecise_dtypes=True).then_inc(sem["consts"], 1)
            pool.iota(lane_no[:, :], [[0, 1]], base=0, channel_multiplier=1,
                      allow_small_or_imprecise_dtypes=True).then_inc(sem["consts"], 1)
            pool.wait_ge(sem["consts"], 5)
            pool.affine_select(out=ident[:, :], in_=ident[:, :], compare_op=ALU.not_equal, fill=1.0, base=0,
                               pattern=[[-1, P]], channel_multiplier=1).then_inc(sem["ident_ready"], 1)
            pool.affine_select(out=before[:, :], in_=ones[:, :], compare_op=ALU.is_gt, fill=0.0, base=0,
                               pattern=[[1, P]], channel_multiplier=-1).then_inc(sem["ident_ready"], 1)
            record_bound = pool.to_reg(RECORDS - 1)
            node_bound = pool.to_reg(N_NODES - 1)
            row_bound = pool.to_reg(COLS - 1)

            def hold(held, before_this, ready, n):
                pool.wait_ge(sem[held], before_this)
                pool.wait_ge(ready, n)
                pool.tensor_tensor(token[0:1, :], token[0:1, :], token[0:1, :], ALU.add).then_inc(sem[held], 1)

            def scatter(dram, fields, held, ready, scattered):
                with pool.Fori(0, SITERS) as i:
                    for k in range(SG):
                        g = i * SG + k
                        hold(held, g + 1, sem[ready], g * 2 + 2)
                        for c in range(SC):
                            pool.indirect_dma_start(
                                dram, bass.IndirectOffsetOnAxis(ap=sidx[:, k, c:c + 1], axis=0),
                                spay[:, k, c, 0:fields], None,
                                bounds_check=record_bound, oob_is_err=False).then_inc(scattered[k], 16)

            def gather(layer):
                width = HW if layer == 3 else D
                pool.wait_ge(sem["table_in"], TABLE_IN[layer])
                if layer == 0:
                    pool.wait_ge(sem["acc_zero"], 1)
                with pool.Fori(0, ITERS) as i:
                    for k in range(RG):
                        g = i * RG + (layer * GROUPS + k)
                        hold("idx_token", g + (SITERS * SG + 1), sem["idx_ready"], g + 1)
                        for j in range(G):
                            pool.indirect_dma_start(
                                ring[:, k * G + j, 0:width], None, table[layer],
                                bass.IndirectOffsetOnAxis(ap=gidx[:, k, j:j + 1], axis=0),
                                bounds_check=node_bound, oob_is_err=False).then_inc(gathered[k], 16)

            pool.wait_ge(sem["fill_in"], FILL_IN)
            scatter(rec_src, 4, "idx_token", "scat_ready", scattered)
            pool.wait_ge(sem["units_known"], 1)
            for rows, into in zip((row_src, row_dst), unit_row):
                for c in range(UC):
                    n = min(P, SLOTS - c * P)
                    pool.indirect_dma_start(into[0:n, c, :], None, rows,
                                            bass.IndirectOffsetOnAxis(ap=unit_at[0:n, c:c + 1], axis=0),
                                            bounds_check=row_bound, oob_is_err=False).then_inc(sem["units_in"], 16)
            with pool.If(read_order(pool) > 0):
                pool.wait_ge(sem["idx_token"], SITERS * SG + 1)
                pool.tensor_tensor(token[0:1, :], token[0:1, :], token[0:1, :], ALU.add).then_inc(sem["token2"], 1)
                scatter(rec_dst, 2, "token2", "scat2_ready", scattered2)
                pool.wait_ge(sem["token2"], SITERS * SG + 1)
            for layer in range(4):
                gather(layer)

        @block.scalar
        def _(act):
            def copy_xT(phase, used, used0):
                def body(b, q, nt):
                    wait(act, sem["xT_psum"], b + (phase * NB + 1))
                    wait(act, sem[used], b + (used0 - 1))
                    for k in range(KC):
                        nc.scalar.copy(xT[:, q, k, 0:nt * P], ps[:, 2 * q + k, 0:nt * P]).then_inc(sem["xT_sbuf"], 1)
                return body

            act.wait_ge(sem["wT_psum"], 1)
            act.wait_ge(sem["weights_in"], WEIGHTS[0])
            nc.scalar.copy(W[:, KC:2 * KC, :], ps[:, 6, :].rearrange("p (k d) -> p k d", k=KC)).then_inc(sem["wT_ready"], 1)

            def rows0(b, q, nt):
                copy_xT(0, "y_psum", YB[0])(b, q, nt)
                wait(act, sem["y_psum"], b + 1)
                wait(act, sem["table_in"], b * 16)
                nc.scalar.copy(z1[:, 0:nt * D], psf[:, 512 * 4:512 * 4 + nt * D]).then_inc(sem["y_used"], 1)
            batches(act, rows0)

            act.wait_ge(sem["cols_in"], 16 * 12)
            act.wait_ge(sem["table_in"], TABLE_IN[0])
            act.wait_ge(sem["ew_psum"], 1)
            nc.scalar.copy(ewT, ps[:, 6, 0:D]).then_inc(sem["lin_ready"], 1)
            nc.scalar.activation(lin[:, 0:KC], col[:, A3:A3 + KC], ACT.Copy, scale=SLOPE).then_inc(sem["lin_ready"], 1)
            nc.scalar.activation(a_relu, a_relu, ACT.Copy, scale=1.0 - SLOPE).then_inc(sem["w_ready"], 1)
            act.wait_ge(sem["ew_psum"], 2)
            nc.scalar.copy(w_line, ps[:, 6, D:D + P]).then_inc(sem["w_ready"], 1)
            nc.scalar.copy(lin[:, KC:KC + 1], ps[:, 6, D + P:D + P + 1]).then_inc(sem["w_ready"], 1)

            def copy_attrT(n, u):
                wait(act, sem["attrT_psum"], n + 1)
                wait(act, sem["ez_psum"], n - 3)
                nc.scalar.copy(attrT[:, u % 4, :], ps[:, u % 2, :]).then_inc(sem["attrT_sbuf"], 1)

            def hand_scatter(n, i, fields, ready, scattered):
                for k in range(SG):
                    wait(act, scattered[k], i * (16 * SC))
                    c = bass.ds(i * (SG * SC) + k * SC, SC)
                    nc.scalar.copy(sidx[:, k, :], rec_of[n][:, c]).then_inc(sem[ready], 1)
                    nc.scalar.copy(spay[:, k, :, 0:fields], pay[n][:, c, :]).then_inc(sem[ready], 1)

            def edge_round(i, first=False, early=False, last=False):
                for u in range(ES):
                    if not (last and u == ES - 1):
                        copy_attrT(i * ES + u + 1, u + 1)
                    if u == (1 if early else ES - 1) and not first:
                        wait(act, sem["record_ready"], 1)
                        wait(act, sem["pay_ready"], i * ES)
                        hand_scatter(0, i - 1, 4, "scat_ready", scattered)
            copy_attrT(0, 0)
            edge_round(0, first=True)
            edge_round(1, early=True)
            with act.Fori(2, SITERS - 1) as i:
                edge_round(i)
            edge_round(SITERS - 1, last=True)
            act.wait_ge(sem["pay_ready"], ESTEPS)
            hand_scatter(0, SITERS - 1, 4, "scat_ready", scattered)
            with act.If(read_order(act) > 0):
                act.wait_ge(sem["record_ready"], 2)
                for k in range(SG):
                    act.wait_ge(scattered[k], 16 * SC * SITERS)
                rounds(act, SITERS, lambda i: hand_scatter(1, i, 2, "scat2_ready", scattered2))
                act.wait_ge(sem["records_dst"], 16)

            def hand_gather(layer, i):
                for k in range(RG):
                    wait(act, sem["summed"], i * R + (layer * SLOTS + (k - RG + 1) * G))
                    src = meta[layer][:, bass.ds(i * R + k * G, G), 0].bitcast(I32)
                    nc.scalar.copy(gidx[:, k, :], src).then_inc(sem["idx_ready"], 1)

            def root(n):
                def body(b, q, nt):
                    wait(act, ln_var[n], b + 1)
                    nc.scalar.activation(norms(n)[:, q, 0:nt, 9], norms(n)[:, q, 0:nt, 8], ACT.Sqrt).then_inc(ln_sqrt[n], 1)
                return body

            def normalize(n):
                def body(b, q, nt):
                    wait(act, ln_ready[n], b + 1)
                    act.sem_inc(sem["act_may"], 1)
                    for j in range(nt):
                        t = b * SB + j
                        one = slice(t, t + 1) if isinstance(t, int) else bass.ds(t, 1)
                        ins = nc.scalar.activation(X[:, one, :].rearrange("p o d -> p (o d)"),
                                                   acc3[:, one, :].rearrange("p o d -> p (o d)"), ACT.Identity,
                                                   scale=norms(n)[:, q, j, 10:11], bias=norms(n)[:, q, j, 11:12])
                    ins.then_inc(sem["rows_done"], 1)
                return body

            def init_acc(layer):
                def body(b, q, nt):
                    wait(act, sem["rows_done"], b + ((layer - 1) * NB + 1))
                    act.sem_inc(sem["act_may"], 1)
                    eps = col[:, EPS1 + layer - 1:EPS1 + layer]
                    nc.scalar.activation(tiles(accd, b, nt), tiles(X[:, :, :], b, nt), ACT.Copy,
                                         scale=eps).then_inc(sem["acc_init"], 1)
                return body

            act.wait_ge(sem["records_in"], 16)
            rounds(act, ITERS, lambda i: hand_gather(0, i))
            act.wait_ge(sem["eps_ready"], 1)

            def rows_0(b, q, nt):
                normalize(0)(b, q, nt)
                init_acc(1)(b, q, nt)
            staggered(act, root(0), rows_0)
            act.wait_ge(sem["dst_sorted"], 1)
            rounds(act, ITERS, lambda i: hand_gather(1, i), first=False)

            copy_xT(1, "z_psum", ZB[1])(0, 0, SB)

            def mlp1(b, q, nt):
                wait(act, sem["z_psum"], b + 1)
                wait(act, sem["y_psum"], b + YB[1])
                for m in range(KC):
                    nc.scalar.activation(z1[:, m * 512:m * 512 + nt * P], ps[:, 4 + m, 0:nt * P], ACT.Relu,
                                         bias=col[:, B1 + m:B1 + m + 1]).then_inc(sem["z_sbuf"], 1)
                if not isinstance(b, int) or b > 0:
                    root(1)(b - 1, 1 - q, SB)
                if not isinstance(b, int) or b + 1 < NB:
                    copy_xT(1, "z_psum", ZB[1])(b + 1, 1 - q, SB)
                if not isinstance(b, int) or b > 0:
                    root(2)(b - 1, 1 - q, SB)
                if not isinstance(b, int) or b > 1:
                    normalize(2)(b - 2, q, SB)
                    init_acc(2)(b - 2, q, SB)
            batches(act, mlp1)
            root(1)(NB - 1, 0, 1)
            root(2)(NB - 1, 0, 1)
            for b, nt in ((NB - 2, SB), (NB - 1, 1)):
                normalize(2)(b, b % 2, nt)
                init_acc(2)(b, b % 2, nt)
            def weigh(g, c0, q):
                wait(act, sem["one_ready"], g + 1)
                wait(act, sem["summed"], g * G + (2 * SLOTS - G))
                for j in range(G):
                    nc.scalar.activation(sel[:, q, j, :], other[:, j, :], ACT.Copy,
                                         scale=meta_src[:, bass.ds(c0 + j, 1), 2:3].rearrange("p o f -> p (o f)")).then_inc(sem["weighed"], 1)
                act.wait_ge(sem["weighed"], g * G + G)
                act.sem_inc(sem["scaled"], 1)
                act.sem_inc(sem["sel_ready"], 1)

            def weighted_round(i, last=False):
                for k in range(RG):
                    weigh(i * RG + k, i * R + k * G, k % 2)
                    if not last and k > 0:
                        hand_next(2, i, k - 1)
                if not last:
                    hand_next(2, i, RG - 1)

            def hand_next(layer, i, k):
                wait(act, sem["summed"], i * R + (layer * SLOTS + (k + 1) * G))
                src = meta[layer][:, bass.ds(i * R + (R + k * G), G), 0].bitcast(I32)
                nc.scalar.copy(gidx[:, k, :], src).then_inc(sem["idx_ready"], 1)
            hand_gather(2, 0)
            weighted_round(0)
            with act.Fori(1, ITERS - 1) as i:
                weighted_round(i)
            weighted_round(ITERS - 1, last=True)

            def lin2(which):
                def body(b, q, nt):
                    if which == 0 and (not isinstance(b, int) or b + 1 < NB):
                        copy_xT(2, "z_psum", ZB[2])(b + 1, 1 - q, SB)
                    wait(act, sem["z_psum"], b + (ZB[2] + which * NB + 1))
                    act.sem_inc(sem["act_may"], 1)
                    bcol = (L2B1, L2B2)[which]
                    for m in range(KC):
                        nc.scalar.activation(ztf[:, m, nodes(b, nt * P)], ps[:, 4 + m, 0:nt * P], ACT.Identity,
                                             bias=col[:, bcol + m:bcol + m + 1]).then_inc(sem["z_sbuf"], 1)
                return body

            def bn_root(which):
                act.wait_ge(sem["bn_var"], which + 1)
                nc.scalar.activation(mv[:, :, 3], mv[:, :, 2], ACT.Sqrt).then_inc(sem["bn_sqrt"], 1)
                act.wait_ge(sem["bn_scale"], which + 1)

            def bn_relu(b, q, nt):
                for m in range(KC):
                    part = ztf[:, m, nodes(b, nt * P)]
                    nc.scalar.activation(part, part, ACT.Relu, bias=mv[:, m, 6:7],
                                         scale=mv[:, m, 5:6]).then_inc(sem["bn_applied"], 1)
            copy_xT(2, "z_psum", ZB[2])(0, 0, SB)
            batches(act, lin2(0))
            bn_root(0)
            staggered(act, bn_relu, lin2(1))
            bn_root(1)

            def bn_relu_and_norm(b, q, nt):
                bn_relu(b, q, nt)
                if not isinstance(b, int) or b > 0:
                    root(3)(b - 1, 1 - q, SB)
                if not isinstance(b, int) or b > 1:
                    normalize(3)(b - 2, q, SB)
            batches(act, bn_relu_and_norm)
            root(3)(NB - 1, 0, 1)
            normalize(3)(NB - 2, 1, SB)
            normalize(3)(NB - 1, 0, 1)
            batches(act, copy_xT(3, "y_psum", YB[3]))
            def mask_logits(g):
                wait(act, sem["ne_ready"], g + 1)
                wait(act, sem["ev_ready"], g + 1)
                wait(act, sem["t_psum"], g)
                for j in range(G):
                    nc.scalar.activation(logit[:, j, :], other[:, j, :], ACT.Identity, scale=-BIG,
                                         bias=ev[:, j:j + 1]).then_inc(sem["mask_part"], 1)
                act.wait_ge(sem["mask_part"], g * G + G)
                act.sem_inc(sem["mask_logit"], 1)

            def exponentials(g, q):
                wait(act, sem["bias_ready"], g + 1)
                wait(act, sem["run_done"], g - 1)
                wait(act, sem["added"], g * G + (3 * SLOTS - G))
                nc.scalar.activation(corr[:, q, :], att[:, 4, :], ACT.Exp).then_inc(sem["corr_ready"], 1)
                wait(act, sem["p_psum"], g)
                for j in range(G):
                    nc.scalar.activation(probT[:, j, :], att_bank(q)[:, j * P:(j + 1) * P], ACT.Exp,
                                         bias=bias[:, q, j:j + 1], accum_out=rsum[:, q, j:j + 1]).then_inc(sem["probT_ready"], 1)

            def copy_probs(g, q):
                wait(act, sem["p_psum"], g + 1)
                wait(act, sem["summed"], g * G + (3 * SLOTS - G))
                nc.scalar.copy(sel[:, q, :, :].rearrange("p s e -> p (s e)"), att_bank(q)).then_inc(sem["sel_ready"], 1)

            def attend_round(i, last=False):
                for k in range(RG):
                    g = i * RG + k
                    if not last or k + 1 < RG:
                        exponentials(g + 1, (k + 1) % 2)
                    if not last:
                        hand_next(3, i, k)
                    if not last or k + 1 < RG:
                        copy_probs(g + 1, (k + 1) % 2)
                    if not last or k + 3 < RG:
                        mask_logits(g + 3)

            hand_gather(3, 0)
            act.wait_ge(sem["h_step"], 2 * NB)
            nc.scalar.activation(ACC[:, :], ones[:, 0:1].to_broadcast([P, T * D]), ACT.Copy,
                                 scale=0.0).then_inc(sem["acc_init"], 1)
            mask_logits(0)
            mask_logits(1)
            exponentials(0, 0)
            mask_logits(2)
            copy_probs(0, 0)
            attend_round(0)
            with act.Fori(1, ITERS - 1) as i:
                attend_round(i)
            attend_round(ITERS - 1, last=True)
            act.wait_ge(sem["scale_ready"], 1)

            def scale(b, q, nt):
                for j in range(nt):
                    t = b * SB + j
                    one = slice(t, t + 1) if isinstance(t, int) else bass.ds(t, 1)
                    rows = acc3[:, one, :].rearrange("p o d -> p (o d)")
                    ins = nc.scalar.activation(rows, rows, ACT.Copy, scale=small[:, 1, one])
                ins.then_inc(sem["acc_scaled"], 1)

            def scale_and_root(b, q, nt):
                scale(b, q, nt)
                if not isinstance(b, int) or b > 0:
                    root(4)(b - 1, 1 - q, SB)
                if not isinstance(b, int) or b > 1:
                    normalize(4)(b - 2, q, SB)
            batches(act, scale_and_root)
            root(4)(NB - 1, 0, 1)
            normalize(4)(NB - 2, 1, SB)
            normalize(4)(NB - 1, 0, 1)

        @block.tensor
        def _(pe):
            def counts(n):
                pe.wait_ge(sem["counted"], (n + 1) * T)
                pe.wait_ge(sem["ident_ready"], 2)
                nc.tensor.matmul(ps[:, 7, 64:64 + T], ones[:, :], small[:, min(n, 1), :], start=True, stop=True)
                if n == 1:
                    nc.tensor.matmul(ps[:, 7, 120:121], ones[:, :], unordered[:, 1:2], start=True, stop=True)
                nc.tensor.matmul(ps[:, 7, 0:T], before[:, :], small[:, min(n, 1), :], start=True, stop=True).then_inc(sem["prefix"], 1)

            def end_columns(n):
                pe.wait_ge(sem["ends_ready"], n + 1)
                for j in range(3 if n == 1 else 2):
                    mm = nc.tensor.matmul(ps[0:T, 7, 128 + j:129 + j], ends[0:1, n, j, :], ones[0:1, 0:1],
                                          start=True, stop=True)
                mm.then_inc(sem["endT_psum"], 1)

            def slot_tiles(n):
                pe.wait_ge(sem["past_ready"], n + 1)
                h = SLOTS // 2
                nc.tensor.matmul(ps[:, 7, 0:h], ones[0:T, :], past[0:T, 0:h], start=True, stop=True).then_inc(sem["tile_psum"], 1)
                pe.wait_ge(sem["tile_ready"], 2 * n + 1)
                nc.tensor.matmul(ps[:, 7, 0:h], ones[0:T, :], past[0:T, h:], start=True, stop=True).then_inc(sem["tile_psum"], 1)

            def turn(phase, view):
                def body(b, q, nt):
                    wait(pe, sem["xT_sbuf"], b * 2 + (2 * phase * NB - 2))
                    src = tiles(view, b, nt)
                    for k in range(KC):
                        for j in range(nt):
                            mm = nc.tensor.transpose(ps[:, 2 * q + k, j * P:(j + 1) * P],
                                                     src[:, j, k * P:(k + 1) * P], ident[:, :])
                    mm.then_inc(sem["xT_psum"], 1)
                return body

            def rows_out(b, nt, lhs, w0, b0, used0, bias_row=None):
                wait(pe, sem["y_used"], b + used0)
                for j in range(nt):
                    o = ps[:, b0 + j // 2, (j % 2) * D:(j % 2 + 1) * D]
                    if bias_row is not None:
                        nc.tensor.matmul(o, ones[0:1, :], bias_row, start=True, stop=False)
                    for k in range(KC):
                        mm = nc.tensor.matmul(o, lhs(k, j), W[:, w0 + k, :], start=(k == 0 and bias_row is None),
                                              stop=(k == KC - 1))
                mm.then_inc(sem["y_psum"], 1)

            def columns_out(b, nt, rhs, w0, batch0):
                wait(pe, sem["z_sbuf"], b * 2 + 2 * batch0)
                for m in range(KC):
                    for k in range(KC):
                        mm = nc.tensor.matmul(ps[:, 4 + m, 0:nt * P], W[:, w0 + k, m * P:(m + 1) * P], rhs(k),
                                              start=(k == 0), stop=(k == KC - 1))
                mm.then_inc(sem["z_psum"], 1)

            pe.wait_ge(sem["weights_in"], WEIGHTS[0])
            pe.wait_ge(sem["ident_ready"], 2)
            for k in range(KC):
                for m in range(KC):
                    mm = nc.tensor.transpose(ps[:, 6, k * D + m * P:k * D + (m + 1) * P],
                                             W[:, m, k * P:(k + 1) * P], ident[:, :])
            mm.then_inc(sem["wT_psum"], 1)
            pe.wait_ge(sem["wT_ready"], 1)
            pe.wait_ge(sem["x_in"], 32)
            pe.wait_ge(sem["zeroed"], 7)

            def first_rows(b, q, nt):
                turn(0, X)(b, q, nt)
                wait(pe, sem["xT_sbuf"], b * 2 + 2)
                rows_out(b, nt, lambda k, j: xT[:, q, k, j * P:(j + 1) * P], KC, 4, YB[0], bc[0:1, 0, :])
                if b == 2:
                    counts(0)
            each_batch(first_rows)

            pe.wait_ge(sem["cols_in"], 16 * 12)
            for m in range(KC):
                mm = nc.tensor.transpose(ps[:, 6, m * P:(m + 1) * P], ewW[:, m * P:(m + 1) * P], ident[:, :])
            mm.then_inc(sem["ew_psum"], 1)
            pe.wait_ge(sem["lin_ready"], 2)
            for m in range(KC):
                nc.tensor.matmul(ps[:, 6, D:D + P], lin[:, m:m + 1].to_broadcast([P, P]), ewT[:, m * P:(m + 1) * P],
                                 start=(m == 0), stop=(m == KC - 1))
            for m in range(KC):
                mm = nc.tensor.matmul(ps[:, 6, D + P:D + P + 1], col[:, EWB + m:EWB + m + 1].to_broadcast([P, P]),
                                      lin[:, m:m + 1], start=(m == 0), stop=(m == KC - 1))
            mm.then_inc(sem["ew_psum"], 1)
            pe.wait_ge(sem["y_used"], NB)
            pe.wait_ge(sem["split_ready"], 2)

            def turn_attr(i, u):
                q, n = u % 2, i * ES + u
                wait(pe, attr_in[u % AR], i * (32 * ES // AR) + 32 * (u // AR + 1))
                wait(pe, sem["attrT_sbuf"], n - 1)
                for j in range(EC):
                    mm = nc.tensor.transpose(ps[:, q, j * P:(j + 1) * P], attr[:, u % AR, j, :], ident[:, :])
                mm.then_inc(sem["attrT_psum"], 1)

            def edge_z(i, u):
                q, n = u % 2, i * ES + u
                wait(pe, sem["attrT_sbuf"], n + 1)
                wait(pe, sem["pay_ready"], n - 1)
                for j in range(EC):
                    o = ps[:, 2 + 2 * q + j // 2, (j % 2) * D:(j % 2 + 1) * D]
                    nc.tensor.matmul(o, ones16, z_bias[:, 0:D], start=True, stop=False)
                    mm = nc.tensor.matmul(o, attrT[:, u % 4, j * P:(j + 1) * P], ewW[:, :], start=False, stop=True)
                mm.then_inc(sem["ez_psum"], 1)

            def edge_round(i, last=False):
                for u in range(ES):
                    if not (last and u == ES - 1):
                        turn_attr(i, u + 1)
                    edge_z(i, u)
            turn_attr(0, 0)
            edge_round(0)
            end_columns(0)
            slot_tiles(0)
            with pe.Fori(1, SITERS - 1) as i:
                edge_round(i)
            edge_round(SITERS - 1, last=True)
            pe.wait_ge(sem["tile_ready"], 2)
            counts(1)
            pe.wait_ge(sem["prefix_out"], 2)
            end_columns(1)
            slot_tiles(1)
            pe.wait_ge(sem["tile_ready"], 4)
            pe.wait_ge(sem["unit_values"], 1)
            for c in range(UC):
                n = min(P, SLOTS - c * P)
                for j, (of, val) in enumerate(((slot_of, endT[0:T, 1, 2:3]), (past, ones[0:T, 0:1]))):
                    mm = nc.tensor.matmul(ps[0:n, 7, j * UC + c:j * UC + c + 1], of[0:T, c * P:c * P + n], val,
                                          start=True, stop=True)
            mm.then_inc(sem["unit_psum"], 1)
            pe.wait_ge(sem["unit_values"], 2)
            for i in range(2):
                for c in range(UC):
                    n = min(P, SLOTS - c * P)
                    mm = nc.tensor.transpose(ps[:, 3 + 2 * i + c // 4, (c % 4) * P:(c % 4) * P + n],
                                             unit_val[i][0:n, c, :], ident[0:n, 0:n])
            mm.then_inc(sem["unit_psum"], 1)
            with pe.If(read_order(pe) > 0):
                counts(2)
                pe.wait_ge(sem["prefix_out"], 3)
                end_columns(2)
                slot_tiles(2)

            def aggregate(layer, i):
                for k in range(RG):
                    slot_sums(layer, i * RG + k, i, k)

            def slot_sums(layer, g, i, k):
                wait(pe, gathered[k], i * (16 * G) + (layer * ITERS + 1) * 16 * G)
                wait(pe, sem["sel_ready"], g + (layer * GROUPS + 1))
                for j in range(G):
                    n = g * G + (layer * SLOTS + j)
                    if j % 2 == 0:
                        wait(pe, sem["added"], n - G + min(2, G - j))
                    nc.tensor.matmul(slot_sum(j), sel[:, k % 2, j, :], ring[:, k * G + j, 0:D],
                                     start=True, stop=True).then_inc(sem["summed"], 1)

            rounds(pe, ITERS, lambda i: aggregate(0, i))
            rounds(pe, ITERS, lambda i: aggregate(1, i), first=False)
            pe.wait_ge(sem["added"], 2 * SLOTS)
            pe.wait_ge(sem["weights_in"], WEIGHTS[1])

            turn(1, accd)(0, 0, SB)

            def mlp1(b, q, nt):
                wait(pe, sem["xT_sbuf"], b * 2 + (2 * NB + 2))
                columns_out(b, nt, lambda k: xT[:, q, k, 0:nt * P], 0, ZB[1])
                if b + 1 < NB:
                    turn(1, accd)(b + 1, 1 - q, min(SB, T - (b + 1) * SB))
                wait(pe, sem["z_sbuf"], b * 2 + 2)
                rows_out(b, nt, lambda k, j: z1[:, k * 512 + j * P:k * 512 + (j + 1) * P], KC, 6, YB[1])
            each_batch(mlp1)
            rounds(pe, ITERS, lambda i: aggregate(2, i), first=False)
            pe.wait_ge(sem["added"], 3 * SLOTS)
            pe.wait_ge(sem["weights_in"], WEIGHTS[2])

            turn(2, accd)(0, 0, SB)

            def lin2a(b, q, nt):
                if b + 1 < NB:
                    turn(2, accd)(b + 1, 1 - q, min(SB, T - (b + 1) * SB))
                wait(pe, sem["xT_sbuf"], b * 2 + (4 * NB + 2))
                columns_out(b, nt, lambda k: xT[:, q, k, 0:nt * P], 0, ZB[2])
            each_batch(lin2a)

            def lin2b(b, q, nt):
                pe.wait_ge(sem["bn_applied"], (b + 1) * KC)
                columns_out(b, nt, lambda k: ztf[:, k, nodes(b, nt * P)], KC, ZB["2b"])
            each_batch(lin2b)

            def turn_back(b, q, nt):
                pe.wait_ge(sem["bn_applied"], (NB + b + 1) * KC)
                wait(pe, sem["back_used"], b - 1)
                for j in range(nt):
                    for k in range(KC):
                        c = (j % 2) * D + k * P
                        src = ztf[:, k, nodes(b, nt * P)][:, j * P:(j + 1) * P]
                        mm = nc.tensor.transpose(ps[:, 2 * q + j // 2, c:c + P], src, ident[:, :])
                mm.then_inc(sem["back_psum"], 1)
            each_batch(turn_back)
            pe.wait_ge(sem["back_used"], NB)
            pe.wait_ge(sem["weights_in"], WEIGHTS[3])

            def node_rows(b, q, nt):
                wait(pe, sem["rows_done"], b + (2 * NB + 1))
                turn(3, X)(b, q, nt)
                wait(pe, sem["xT_sbuf"], b * 2 + (6 * NB + 2))
                rows_out(b, nt, lambda k, j: xT[:, q, k, j * P:(j + 1) * P], 0, 4, YB[3])
            each_batch(node_rows)
            pe.wait_ge(sem["s1_ready"], 1)
            nc.tensor.transpose(ps[0:T, 6, 0:P], s1[:, :], ident[:, :]).then_inc(sem["c_psum"], 1)
            pe.wait_ge(sem["c_ready"], 1)
            h = SLOTS // 2
            for j in range(2):
                nc.tensor.matmul(ps[:, 4 + j, 0:h], before[0:T, :], reset[0:T, j * h:(j + 1) * h], start=True,
                                 stop=True).then_inc(sem["c_psum"], 1)
            pe.wait_ge(sem["c_ready"], 4)

            def turn_logits(g, q):
                wait(pe, sem["mask_logit"], g + 1)
                wait(pe, sem["sel_ready"], g + (3 * GROUPS - 1))
                for j in range(G):
                    mm = nc.tensor.transpose(att_bank(q)[:, j * P:(j + 1) * P], logit[:, j, :], ident[:, :])
                mm.then_inc(sem["t_psum"], 1)

            def turn_probs(g, q):
                wait(pe, sem["probT_ready"], (g + 1) * G)
                for j in range(G):
                    mm = nc.tensor.transpose(att_bank(q)[:, j * P:(j + 1) * P], probT[:, j, :], ident[:, :])
                mm.then_inc(sem["p_psum"], 1)

            turn_logits(0, 0)
            turn_logits(1, 1)
            turn_probs(0, 0)
            slot_sums(3, 0, 0, 0)
            turn_logits(2, 0)

            def attend_round(i, last=False):
                for k in range(RG):
                    g = i * RG + k
                    if not last or k + 1 < RG:
                        turn_probs(g + 1, (k + 1) % 2)
                        slot_sums(3, g + 1, *((i, k + 1) if k + 1 < RG else (i + 1, 0)))
                    if not last or k + 3 < RG:
                        turn_logits(g + 3, (k + 1) % 2)
            attend_round(0)
            with pe.Fori(1, ITERS - 1) as i:
                attend_round(i)
            attend_round(ITERS - 1, last=True)

        @block.vector
        def _(dve):
            chain = {"dve_chain": 0, "branch_chain": 0}
            linked = ["dve_chain"]

            def link(ins):
                n = linked[0]
                chain[n] += 1
                ins.then_inc(sem[n], 1)
                dve.wait_ge(sem[n], chain[n])

            v = nc.vector
            link(v.memset(X[:, T - 1, :], 0.0))
            v.memset(key[0][96:P, :], NO_NODE).then_inc(sem["zeroed"], 1)
            v.memset(key[1][96:P, :], NO_NODE).then_inc(sem["zeroed"], 1)
            v.memset(run[0][96:P, :], 0.0).then_inc(sem["zeroed"], 1)
            v.memset(attr[96:P, :, :, :], 0.0).then_inc(sem["zeroed"], 1)
            v.memset(next_key[:, :], NO_NODE).then_inc(sem["zeroed"], 1)
            for rec in (meta_src, meta_dst):
                link(v.memset(rec[:, :, :], 0.0))
                link(v.memset(rec[:, :, 0].bitcast(I32), OUT_OF_RANGE))
                v.memset(rec[:, :, 1], -1.0).then_inc(sem["zeroed"], 1)
            dve.wait_ge(sem["keys_in"], KEYS_IN)
            dve.wait_ge(sem["consts"], 5)
            link(v.tensor_copy(pay_src[:, :, 2], run[0]))
            link(v.tensor_copy(pay_src[:, :, 0].bitcast(I32), key[1]))
            link(v.tensor_copy(pay_dst[:, :, 0].bitcast(I32), key[0]))

            def tile_counts(n, which):
                link(v.tensor_scalar(ibuf, key[which], 7, None, ALU.arith_shift_right))
                link(v.tensor_copy(bucket, ibuf))
                if n == 1:
                    link(v.tensor_tensor(run[0][:, 0:COLS - 1], bucket[:, 1:], bucket[:, 0:COLS - 1], ALU.is_lt))
                    link(v.tensor_scalar(next_key[:, :], next_key[:, :], 7, None, ALU.arith_shift_right))
                    link(v.tensor_copy(unordered[:, 0:1], next_key[:, :]))
                    link(v.tensor_tensor(run[0][:, COLS - 1:], unordered[:, 0:1], bucket[:, COLS - 1:], ALU.is_lt))
                    link(v.tensor_reduce(unordered[:, 1:2], run[0], AX_X, ALU.add))
                with dve.Fori(0, T) as b:
                    v.tensor_scalar(mask[:, bass.ds(b, 1), :].rearrange("p o c -> p (o c)"), bucket,
                                    iota[:, bass.ds(b, 1)], None, ALU.is_equal, ALU.add,
                                    accum_out=small[:, which, bass.ds(b, 1)]).then_inc(sem["counted"], 1)
                dve.wait_ge(sem["prefix"], n + 1)
                link(v.tensor_copy(small[:, 5, :], ps[:, 7, 0:T]))
                if n == 1:
                    v.tensor_scalar(seen[:, :], ps[:, 7, 120:121], 1.0, None, ALU.min).then_inc(sem["order_known"], 1)
                    dve.wait_ge(sem["order_known"], 1)
                v.tensor_copy(small[:, 2, :], ps[:, 7, 64:64 + T]).then_inc(sem["prefix_out"], 1)
                dve.wait_ge(sem["prefix_out"], n + 1)

            def cut(into, x, add=0.0):
                link(v.tensor_scalar(small[:, 3, :].bitcast(I32), x, add, None, ALU.add))
                link(v.tensor_scalar(small[:, 3, :].bitcast(I32), small[:, 3, :].bitcast(I32), 7, None, ALU.arith_shift_right))
                link(v.tensor_copy(into, small[:, 3, :].bitcast(I32)))

            def tile_ends(n):
                link(v.tensor_tensor_scan(ends[:, n, 0, :], ones[:, 0:T], small[:, 4, :], 0.0, ALU.mult, ALU.add))
                v.tensor_tensor(ends[:, n, 1, :], ends[:, n, 0, :], small[:, 4, :], ALU.subtract).then_inc(sem["ends_ready"], 1)
                dve.wait_ge(sem["ends_ready"], n + 1)

            def rank_edges(n, which):
                link(v.tensor_scalar(rec_of[which], key[which], P - 1, None, ALU.bitwise_and))
                link(v.tensor_copy(pay[which][:, :, 1], rec_of[which]))
                link(v.memset(pos, float(NOWHERE)))
                cut(small[:, 4, :], small[:, 2, :], float(P - 1))
                tile_ends(n)
                link(v.scalar_tensor_tensor(small[:, 5, :], ends[:, n, 1, :], float(P), small[:, 5, :], ALU.mult, ALU.add))
                link(v.tensor_scalar(small[:, 5, :], small[:, 5, :], -1.0, None, ALU.add))

                for b in range(T):
                    wait(dve, sem["ranked"], which * T + b - 1)
                    v.tensor_tensor_scan(run[b % 2], ones[:, 0:1].to_broadcast([P, COLS]), mask[:, b, :],
                                         small[:, 5, b:b + 1], ALU.mult, ALU.add).then_inc(sem["scanned"], 1)
                    dve.wait_ge(sem["scanned"], which * T + b + 1)
                    wait(dve, sem["ranked"], which * T + b)
                    v.copy_predicated(pos, mask[:, b, :], run[b % 2]).then_inc(sem["ranked"], 1)
                dve.wait_ge(sem["ranked"], (which + 1) * T)
                lane, slot = run[0].bitcast(I32), run[1].bitcast(I32)
                link(v.tensor_copy(ibuf, pos))
                link(v.tensor_scalar(lane, ibuf, P - 1, None, ALU.bitwise_and))
                link(v.tensor_scalar(slot, ibuf, 7, None, ALU.arith_shift_right))
                v.scalar_tensor_tensor(rec_of[which], lane, float(SLOTS), slot, ALU.mult, ALU.add).then_inc(sem["record_ready"], 1)
                dve.wait_ge(sem["record_ready"], which + 1)

            def tiles_of_slots(n, into):
                dve.wait_ge(sem["endT_psum"], n + 1)
                w = 3 if n == 1 else 2
                v.tensor_copy(endT[0:T, n, 0:w], ps[0:T, 7, 128:128 + w]).then_inc(sem["endT_ready"], 1)
                dve.wait_ge(sem["endT_ready"], n + 1)
                v.tensor_scalar(past[0:T, :], slot_no[0:T, :], endT[0:T, n, 0:1], None, ALU.is_ge).then_inc(sem["past_ready"], 1)
                h = SLOTS // 2
                for j in range(2):
                    dve.wait_ge(sem["tile_psum"], 2 * n + j + 1)
                    v.tensor_scalar(into[:, j * h:(j + 1) * h], ps[:, 7, 0:h], float(T - 1), float(D), ALU.min,
                                    ALU.mult).then_inc(sem["tile_ready"], 1)

            def rows_from(bank, b, nt, into, add, signal):
                src = psf[:, 512 * bank:512 * bank + nt * D].rearrange("p (t d) -> p t d", d=D)
                v.tensor_tensor(into, src, add, ALU.add).then_inc(sem[signal], 1)

            tile_counts(0, 0)
            rank_edges(0, 0)
            dve.wait_ge(sem["cols_in"], 16 * 12)
            v.tensor_scalar(col[:, EPS1:EPS2 + 1], col[:, EPS1:EPS2 + 1], 1.0, None, ALU.add).then_inc(sem["eps_ready"], 1)
            dve.wait_ge(sem["weights_in"], WEIGHTS[0])
            dve.wait_ge(sem["fill_in"], FILL_IN)
            dve.wait_ge(sem["table_in"], TABLE_IN[0])
            link(v.memset(z_bias, 0.0))
            for i in range(3):
                link(v.tensor_copy(term, left[i % 2]))
                link(v.tensor_copy(z_bias[32 * i:32 * i + 1, 0:D], term[32 * i:32 * i + 1, :]))
                if i < 2:
                    link(v.tensor_tensor(left[1 - i], left[i], term, ALU.subtract))
            v.memset(ones16, 1.0).then_inc(sem["split_ready"], 1)
            dve.wait_ge(sem["dve_chain"], chain["dve_chain"])
            v.memset(zsum[:, :, :, :], 0.0).then_inc(sem["split_ready"], 1)
            dve.wait_ge(sem["split_ready"], 2)
            dve.wait_ge(sem["w_ready"], 3)

            def edge_sums(i, u):
                q, n = u % 2, i * ES + u
                wait(dve, sem["edge_part"], n * 8)
                wait(dve, sem["ez_psum"], n + 1)
                for j in range(EC):
                    z = ps[:, 2 + 2 * q + j // 2, (j % 2) * D:(j % 2 + 1) * D]
                    v.scalar_tensor_tensor(relu_out[:, q, j, :], z, 0.0, a_relu, ALU.max, ALU.mult,
                                           accum_out=zsum[:, q, 0, j:j + 1]).then_inc(sem["edge_part"], 1)
                for j in range(EC):
                    v.scalar_tensor_tensor(line_out[:, q, j, :], attr[:, u % AR, j, :], 1.0, w_line, ALU.mult, ALU.mult,
                                           accum_out=zsum[:, q, 1, j:j + 1]).then_inc(sem["edge_part"], 1)
                wait(dve, sem["edge_part"], n * 8 + 8)
                v.scalar_tensor_tensor(pay_src[:, bass.ds(n * EC, EC), 3], zsum[:, q, 0, :], lin[:, KC:KC + 1],
                                       zsum[:, q, 1, :], ALU.add, ALU.add).then_inc(sem["pay_ready"], 1)

            def edge_round(i):
                for u in range(ES):
                    edge_sums(i, u)
            edge_round(0)
            tiles_of_slots(0, tile_src)
            with dve.Fori(1, SITERS) as i:
                edge_round(i)
            dve.wait_ge(sem["pay_ready"], ESTEPS)

            tile_counts(1, 1)
            link(v.tensor_tensor_scan(ends[:, 1, 0, :], ones[:, 0:T], small[:, 2, :], 0.0, ALU.mult, ALU.add))
            link(v.tensor_tensor(ends[:, 1, 1, :], ends[:, 1, 0, :], small[:, 2, :], ALU.subtract))
            cut(small[:, 4, :], ends[:, 1, 0, :], float(P - 1))
            cut(ends[:, 1, 2, :], ends[:, 1, 1, :])
            link(v.tensor_scalar(small[:, 3, :], small[:, 2, :], 1.0, None, ALU.min))
            link(v.tensor_tensor(small[:, 4, :], small[:, 4, :], ends[:, 1, 2, :], ALU.subtract))
            link(v.tensor_tensor(small[:, 4, :], small[:, 4, :], small[:, 3, :], ALU.mult))
            link(v.tensor_tensor_scan(ends[:, 1, 0, :], ones[:, 0:T], small[:, 4, :], 0.0, ALU.mult, ALU.add))
            link(v.tensor_tensor(ends[:, 1, 1, :], ends[:, 1, 0, :], small[:, 4, :], ALU.subtract))
            v.tensor_tensor(ends[:, 1, 2, :], ends[:, 1, 2, :], ends[:, 1, 1, :], ALU.subtract).then_inc(sem["ends_ready"], 1)
            tiles_of_slots(1, tile_dst)
            dve.wait_ge(sem["tile_ready"], 4)
            link(v.tensor_scalar(slot_of[0:T, :], slot_no[0:T, :], endT[0:T, 1, 1:2], None, ALU.is_ge))
            v.tensor_tensor(slot_of[0:T, :], slot_of[0:T, :], past[0:T, :], ALU.subtract).then_inc(sem["unit_values"], 1)
            dve.wait_ge(sem["unit_psum"], 1)
            link(v.memset(unit_at, 0))
            link(v.memset(unit_tile, 0.0))
            for c in range(UC):
                n = min(P, SLOTS - c * P)
                link(v.tensor_scalar(unit_tile[0:n, c:c + 1], ps[0:n, 7, UC + c:UC + c + 1], float(P), None, ALU.mult))
                link(v.tensor_scalar(unit_at[0:n, c:c + 1], ps[0:n, 7, c:c + 1], lane_no[0:n, 0:1], float(c * P), ALU.add, ALU.add))
            v.tensor_scalar(unit_at, unit_at, float(COLS - 1), None, ALU.min).then_inc(sem["units_known"], 1)
            dve.wait_ge(sem["units_in"], 16 * 2 * UC)
            rest = SLOTS - (UC - 1) * P
            for c0, c1, n in ((0, UC - 1, P), (UC - 1, UC, rest)):
                link(v.tensor_copy(unit_val[0][0:n, c0:c1, :], unit_row[0][0:n, c0:c1, :]))
                link(v.tensor_tensor(unit_val[1][0:n, c0:c1, :], unit_row[1][0:n, c0:c1, :],
                                     unit_tile[0:n, c0:c1].rearrange("p (c o) -> p c o", o=1).to_broadcast([n, c1 - c0, P]),
                                     ALU.subtract))
            dve.sem_inc(sem["unit_values"], 1)
            dve.wait_ge(sem["unit_psum"], 2)
            for i, col_i in enumerate((meta_dst[:, :, 0].bitcast(I32), meta_dst[:, :, 1])):
                for h in range(2):
                    n = min(4 * P, SLOTS - h * 4 * P)
                    link(v.tensor_copy(col_i[:, h * 4 * P:h * 4 * P + n], ps[:, 3 + 2 * i + h, 0:n]))
            dve.sem_inc(sem["dst_sorted"], 1)
            dve.wait_ge(sem["x_in"], 32)
            link(v.tensor_copy(accd, X[:, :, :]))

            with dve.If(read_order(dve) > 0):
                linked[0] = "branch_chain"
                tile_counts(2, 1)
                rank_edges(2, 1)
                tiles_of_slots(2, tile_dst)
                dve.wait_ge(sem["records_dst"], 16)
                link(v.tensor_copy(accd, X[:, :, :]))
                linked[0] = "dve_chain"
            for k in range(SG):
                dve.wait_ge(scattered[k], 16 * SC * SITERS)
            v.memset(ZT[:, :], 0.0).then_inc(sem["acc_zero"], 1)
            dve.wait_ge(sem["acc_zero"], 1)

            def select(layer, i, k):
                g = i * RG + k
                if layer != 2:
                    wait(dve, sem["summed"], g * G + (layer * SLOTS - G))
                m = meta[layer]
                c0 = i * R + k * G
                if layer == 2:
                    wait(dve, sem["scaled"], g)
                into, done = (other, "one_ready") if layer == 2 else (sel[:, k % 2, :, :], "sel_ready")
                v.tensor_tensor(into, iota[:, :].rearrange("p (o e) -> p o e", o=1).to_broadcast([P, G, P]),
                                m[:, bass.ds(c0, G), 1:2].to_broadcast([P, G, P]), ALU.is_equal).then_inc(sem[done], 1)

            def tile_sums(tiles, i, k):
                _, found = nc.values_load_multi_w_load_instructions(
                    tiles[0:1, bass.ds(i * R + k * G, G)], engines=(mybir.EngineType.DVE,), min_val=0,
                    max_val=(T - 1) * D, skip_runtime_bounds_check_because="a slot's tile is one of T")
                return found

            def accumulate(layer, i, k):
                into = tile_sums(slot_tile[layer], i, k)
                for j in range(G):
                    n = i * R + (layer * SLOTS + k * G + j)
                    dst = ACC[:, bass.ds(into[j], D)]
                    if j % 2 == 0:
                        wait(dve, sem["summed"], slot_done(n, j))
                    wait(dve, sem["added"], n)
                    v.tensor_tensor(dst, slot_sum(j), dst, ALU.add).then_inc(sem["added"], 1)

            def aggregate(layer, i, last=False):
                for k in range(RG):
                    if not (last and k == RG - 1):
                        if k < RG - 1:
                            select(layer, i, k + 1)
                        else:
                            select(layer, i + 1, 0)
                    accumulate(layer, i, k)

            def aggregate_all(layer):
                select(layer, 0, 0)
                if layer == 0:
                    aggregate(layer, 0)
                with dve.Fori(1 if layer == 0 else 0, ITERS - 1) as i:
                    aggregate(layer, i)
                aggregate(layer, ITERS - 1, last=True)
                dve.wait_ge(sem["added"], (layer + 1) * SLOTS)

            def norm_steps(name, per_batch):
                done = [0]

                def step(b, ins):
                    done[0] += 1
                    ins.then_inc(sem[name], 1)
                    wait(dve, sem[name], b * per_batch + ((done[0] - 1) % per_batch + 1))
                return step

            def pass_on():
                dve.sem_inc(sem["stats_may"], 1)

            def row_stats(n, step, rows, b, q, nt):
                s = norms(n)[:, q]
                pass_on()
                for j in range(nt):
                    ins = v.bn_stats(s[:, j, 0:6], tile_of(rows, b, j))
                step(b, ins)
                pass_on()
                for j in range(nt):
                    ins = v.bn_aggr(s[:, j, 6:8], s[:, j, 0:6])
                step(b, ins)
                v.tensor_scalar(s[:, 0:nt, 8], s[:, 0:nt, 7], LN_EPS, None, ALU.add).then_inc(ln_var[n], 1)

            def one_over(n, step, b, q, nt):
                wait(dve, ln_sqrt[n], b + 1)
                if n in LN_PLACE:
                    wait(dve, sem["rows_done"], b + (LN_PLACE[n] * NB - 1))
                s = norms(n)[:, q, 0:nt]
                step(b, v.reciprocal(s[:, :, 10], s[:, :, 9]))
                if n in LN_PLACE:
                    v.scalar_tensor_tensor(s[:, :, 11], s[:, :, 6], -1.0, s[:, :, 10], ALU.mult, ALU.mult).then_inc(ln_ready[n], 1)

            def tile_of(view, b, j):
                t = b * SB + j
                one = slice(t, t + 1) if isinstance(t, int) else bass.ds(t, 1)
                return view[:, one, :].rearrange("p o d -> p (o d)")

            dve.wait_ge(sem["records_in"], 16)
            aggregate_all(0)
            def stats0(b, q, nt):
                row_stats(0, stats_step0, accd, b, q, nt)

            def rows_0(b, q, nt):
                one_over(0, recip_step0, b, q, nt)
            stats_step0, recip_step0 = norm_steps("ln_step0", 2), norm_steps("ln_step1", 1)
            staggered(dve, stats0, rows_0)
            dve.wait_ge(sem["acc_init"], NB)
            aggregate_all(1)
            dve.wait_ge(sem["weights_in"], WEIGHTS[1])
            stepA, stepB, stepC = norm_steps("ln_step_a", 3), norm_steps("ln_step_b", 6), norm_steps("ln_step_c", 1)

            def over_batch(vec, nt):
                return vec.rearrange("p (o d) -> p o d", o=1).to_broadcast([P, nt, D])

            def mlp1(b, q, nt):
                wait(dve, sem["y_psum"], b + (YB[1] + 1))
                rows = tiles(accd, b, nt)
                rows_from(6, b, nt, rows, tiles(X[:, :, :], b, nt), "y_used")
                wait(dve, sem["y_used"], b + (YB[1] + 1))
                stepA(b, v.tensor_tensor(rows, rows, over_batch(bc[:, 0, :], nt), ALU.add))
                row_stats(1, stepA, accd, b, q, nt)
                if not isinstance(b, int) or b > 0:
                    last1(b - 1, 1 - q, SB)
                one_over(1, stepB, b, q, nt)
                for j in range(nt):
                    ins = v.scalar_tensor_tensor(tile_of(accd, b, j), tile_of(accd, b, j), norms(1)[:, q, j, 6:7],
                                                 bc[:, 1, :], ALU.subtract, ALU.mult)
                stepB(b, ins)
                for j in range(nt):
                    ins = v.scalar_tensor_tensor(tile_of(accd, b, j), tile_of(accd, b, j), norms(1)[:, q, j, 10:11],
                                                 bc[:, 2, :], ALU.mult, ALU.add)
                stepB(b, ins)
                stepB(b, v.scalar_tensor_tensor(rows, rows, 0.0, tiles(X[:, :, :], b, nt), ALU.max, ALU.add))
                row_stats(2, stepB, accd, b, q, nt)

            def last1(b, q, nt):
                one_over(2, stepC, b, q, nt)
            batches(dve, mlp1)
            last1(NB - 1, 0, 1)
            dve.wait_ge(sem["acc_init"], 2 * NB)
            aggregate_all(2)
            for which, (g, be) in enumerate(((G1, BE1), (G2, BE2))):
                def gather_stats(b, q, nt):
                    wait(dve, sem["z_sbuf"], b * 2 + 2 * (ZB[2] + which * NB + 1))
                    n = nt * P if not isinstance(b, int) else min(nt * P, N_NODES - b * SB * P)
                    for m in range(KC):
                        v.bn_stats(stats[:, m, bass.ds(b, 1), :].rearrange("p o s -> p (o s)"),
                                   ztf[:, m, nodes(b, n)]).then_inc(sem["bn_in"], 1)
                batches(dve, gather_stats)
                dve.wait_ge(sem["bn_in"], (which + 1) * NB * KC)
                for m in range(KC):
                    link(v.bn_aggr(mv[:, m, 0:2], stats[:, m, :, :].rearrange("p b s -> p (b s)")))
                v.tensor_scalar(mv[:, :, 2], mv[:, :, 1], BN_EPS, None, ALU.add).then_inc(sem["bn_var"], 1)
                dve.wait_ge(sem["bn_sqrt"], which + 1)
                link(v.reciprocal(mv[:, :, 4], mv[:, :, 3]))
                link(v.tensor_tensor(mv[:, :, 5], mv[:, :, 4], col[:, g:g + 2], ALU.mult))
                link(v.tensor_tensor(mv[:, :, 7], mv[:, :, 0], mv[:, :, 5], ALU.mult))
                v.tensor_tensor(mv[:, :, 6], col[:, be:be + 2], mv[:, :, 7], ALU.subtract).then_inc(sem["bn_scale"], 1)
                dve.wait_ge(sem["bn_scale"], which + 1)

            back_step, back_last = norm_steps("ln_step2", 2), norm_steps("ln_step3", 1)

            def back(b, q, nt):
                wait(dve, sem["back_psum"], b + 1)
                rows_from(2 * q, b, nt, tiles(accd, b, nt), tiles(X[:, :, :], b, nt), "back_used")
                wait(dve, sem["back_used"], b + 1)
                row_stats(3, back_step, accd, b, q, nt)

            def rows_2(b, q, nt):
                one_over(3, back_last, b, q, nt)
            staggered(dve, back, rows_2)
            dve.wait_ge(sem["weights_in"], WEIGHTS[3])
            h_step = norm_steps("h_step", 2)

            def node_rows(b, q, nt):
                wait(dve, sem["y_psum"], b + (YB[3] + 1))
                h = tiles(ht, b, nt)[:, :, 0:D]
                rows_from(4, b, nt, h, over_batch(bc[:, 0, :], nt), "y_used")
                wait(dve, sem["y_used"], b + (YB[3] + 1))
                h_step(b, v.scalar_tensor_tensor(h, h, SLOPE, h, ALU.mult, ALU.max))
                for j in range(nt):
                    t = b * SB + j
                    one = slice(t, t + 1) if isinstance(t, int) else bass.ds(t, 1)
                    row = tile_of(ht[:, :, 0:D], b, j)
                    v.scalar_tensor_tensor(tile_of(accd, b, j), row, 1.0, bc[:, 1, :], ALU.mult, ALU.mult,
                                           accum_out=s1[:, one])
                    ins = v.scalar_tensor_tensor(other_out[:, 0, j, :], row, 1.0, bc[:, 2, :], ALU.mult, ALU.mult,
                                                 accum_out=s2[:, one])
                h_step(b, ins)
                v.tensor_copy(tiles(ht, b, nt)[:, :, D], s2[:, nodes_of(b, nt)]).then_inc(sem["ht_ready"], 1)
            batches(dve, node_rows)
            dve.wait_ge(sem["h_step"], 2 * NB)
            v.tensor_scalar(s1[:, :], s1[:, :], col[:, AB:AB + 1], None, ALU.add).then_inc(sem["s1_ready"], 1)
            dve.wait_ge(sem["ht_ready"], NB)
            link(v.tensor_scalar(cslot[0:T, :], slot_no[0:T, :], endT[0:T, 0, 0:1], None, ALU.is_ge))
            link(v.tensor_scalar(reset[0:T, :], slot_no[0:T, :], endT[0:T, 0, 1:2], None, ALU.is_ge))
            link(v.tensor_tensor(reset[0:T, :], reset[0:T, :], cslot[0:T, :], ALU.subtract))
            dve.wait_ge(sem["c_psum"], 1)
            v.tensor_copy(before[0:T, :], ps[0:T, 6, 0:P]).then_inc(sem["c_ready"], 1)
            h = SLOTS // 2
            for j in range(2):
                dve.wait_ge(sem["c_psum"], 2 + j)
                v.tensor_copy(cslot[:, j * h:(j + 1) * h], ps[:, 4 + j, 0:h]).then_inc(sem["c_ready"], 1)
            link(v.memset(reset[:, 0:1], -BIG))
            link(v.tensor_tensor(reset[:, 1:], tile_src[:, 1:], tile_src[:, 0:SLOTS - 1], ALU.not_equal))
            link(v.tensor_scalar(reset[:, 1:], reset[:, 1:], -BIG, None, ALU.mult))
            link(v.memset(wsum[:, :], 0.0))
            v.memset(runmax[:, :, :], FLOOR).then_inc(sem["c_ready"], 1)
            dve.wait_ge(sem["c_ready"], 4)
            dve.wait_ge(sem["table_in"], TABLE_IN[3])

            def edge_values(i, k):
                g = i * RG + k
                dve.wait_ge(gathered[k], i * (16 * G) + (3 * ITERS + 1) * 16 * G)
                slots = bass.ds(i * R + k * G, G)
                wait(dve, sem["mask_part"], g * G)
                v.tensor_tensor(ev[:, :], ring[:, k * G:(k + 1) * G, D], meta_src[:, slots, 3],
                                ALU.add).then_inc(sem["ev_ready"], 1)
                v.tensor_tensor(other, iota[:, :].rearrange("p (o e) -> p o e", o=1).to_broadcast([P, G, P]),
                                meta_src[:, slots, 1:2].to_broadcast([P, G, P]), ALU.not_equal).then_inc(sem["ne_ready"], 1)

            MAX_STEPS = 4

            def maxima(i, k, s):
                g, q = i * RG + k, k % 2
                slots = bass.ds(i * R + k * G, G)
                now = runmax[:, q, 1:1 + G]
                if s > 0:
                    wait(dve, sem["max_ready"], g * MAX_STEPS + s)
                if s == 0:
                    wait(dve, sem["t_psum"], g + 1)
                    v.tensor_copy(runmax[:, q, 0:1], runmax[:, 1 - q, G:G + 1])
                    v.tensor_reduce(att[:, 1, :], att_bank(q).rearrange("p (s e) -> p s e", e=P), AX_X,
                                    ALU.max).then_inc(sem["max_ready"], 1)
                elif s == 1:
                    v.scalar_tensor_tensor(att[:, 2, :], att[:, 1, :], FLOOR, cslot[:, slots], ALU.max,
                                           ALU.add).then_inc(sem["max_ready"], 1)
                elif s == 2:
                    v.tensor_tensor_scan(now, reset[:, slots], att[:, 2, :], runmax[:, q, 0:1], ALU.add,
                                         ALU.max).then_inc(sem["max_ready"], 1)
                elif s == 3:
                    v.tensor_tensor(bias[:, q, :], cslot[:, slots], now, ALU.subtract)
                    v.tensor_tensor(att[:, 3, :], runmax[:, q, 0:G], reset[:, slots], ALU.add).then_inc(sem["max_ready"], 1)
                elif s == 4:
                    wait(dve, sem["corr_ready"], g)
                    v.tensor_tensor(att[:, 4, :], att[:, 3, :], now, ALU.subtract).then_inc(sem["bias_ready"], 1)

            def after(i, k, n):
                return (i, k + n) if k + n < RG else (i + 1, k + n - RG)

            def attend(i, k, last):
                g, q = i * RG + k, k % 2
                into = tile_sums(tile_src, i, k)
                dve.wait_ge(sem["corr_ready"], g + 1)
                wait(dve, sem["run_done"], g)
                dve.wait_ge(sem["probT_ready"], g * G + G)
                c = bass.ds(i * R + (k * G + 1), G)
                v.tensor_tensor_scan(wsum[:, c], corr[:, q, :], rsum[:, q, :], wsum[:, bass.ds(i * R + k * G, 1)],
                                     ALU.mult, ALU.add).then_inc(sem["run_done"], 1)
                for j in range(G):
                    n = i * R + (3 * SLOTS + k * G + j)
                    dst = ACC[:, bass.ds(into[j], D)]
                    if j % 2 == 0:
                        wait(dve, sem["summed"], slot_done(n, j))
                    wait(dve, sem["added"], n)
                    v.scalar_tensor_tensor(dst, dst, corr[:, q, j:j + 1], slot_sum(j), ALU.mult,
                                           ALU.add).then_inc(sem["added"], 1)
                    if 2 <= j <= MAX_STEPS + 2 and (not last or k + 2 < RG):
                        maxima(*after(i, k, 2), j - 2)
                    if j == 3 and (not last or k + 3 < RG):
                        edge_values(*after(i, k, 3))

            def attend_round(i, last=False):
                for k in range(RG):
                    attend(i, k, last)
            for g in range(2):
                edge_values(0, g)
            for s in range(MAX_STEPS + 1):
                maxima(0, 0, s)
            edge_values(0, 2)
            for s in range(MAX_STEPS + 1):
                maxima(0, 1, s)
            dve.wait_ge(sem["acc_init"], 2 * NB + 1)
            attend_round(0)
            with dve.Fori(1, ITERS - 1) as i:
                attend_round(i)
            attend_round(ITERS - 1, last=True)
            dve.wait_ge(sem["added"], 4 * SLOTS)
            dve.wait_ge(sem["run_done"], GROUPS)
            link(v.tensor_copy(small[:, 3, :].bitcast(I32), ends[:, 0, 0, :]))
            some = 7
            with dve.Fori(0, T // some) as i:
                _, found = nc.values_load_multi_w_load_instructions(
                    small[0:1, 3, bass.ds(i * some, some)].bitcast(I32), engines=(mybir.EngineType.DVE,), min_val=0,
                    max_val=SLOTS, skip_runtime_bounds_check_because="a tile ends at a slot")
                for j, e in enumerate(found):
                    v.tensor_copy(small[:, 2, bass.ds(i * some + j, 1)], wsum[:, bass.ds(e, 1)]).then_inc(sem["weight_ready"], 1)
            assert T % some == 0
            dve.wait_ge(sem["weight_ready"], T)
            link(v.tensor_scalar(small[:, 0, :], small[:, 2, :], 1e-30, None, ALU.max))
            v.reciprocal(small[:, 1, :], small[:, 0, :]).then_inc(sem["scale_ready"], 1)
            out_step, out_last = norm_steps("ln_step4", 4), norm_steps("ln_step5", 1)

            def sums(b, q, nt):
                wait(dve, sem["acc_scaled"], b + 1)
                rows = tiles(accd, b, nt)
                out_step(b, v.scalar_tensor_tensor(rows, rows, SLOPE, rows, ALU.mult, ALU.max))
                out_step(b, v.tensor_tensor(rows, rows, tiles(X[:, :, :], b, nt), ALU.add))
                row_stats(4, out_step, accd, b, q, nt)

            def rows_3(b, q, nt):
                one_over(4, out_last, b, q, nt)
            staggered(dve, sums, rows_3)


INPUTS = ["x", "src", "dst", "edge_attr_128", "edge_weight", "L0_gnn_W", "L0_gnn_b", "L1_gnn_W1", "L1_gnn_b1",
          "L1_gnn_W2", "L1_gnn_b2", "L1_gnn_eps", "L1_gnn_gamma", "L1_gnn_beta", "L2_gnn_eps", "L2_gnn_W1",
          "L2_gnn_b1", "L2_gnn_g1", "L2_gnn_be1", "L2_gnn_W2", "L2_gnn_b2", "L2_gnn_g2", "L2_gnn_be2",
          "L3_gnn_w_W", "L3_gnn_w_b", "L3_gnn_ew_W", "L3_gnn_ew_b", "L3_gnn_a_W", "L3_gnn_a_b"]


def kernel(**inputs):
    import numpy as np
    import concourse.bacc as bacc
    from concourse import mybir
    from concourse.bass_utils import run_bass_kernel_spmd as run

    nc = bacc.Bacc("TRN2", target_bir_lowering=False, num_devices=1)
    arrays, args = {}, {}
    for name in INPUTS:
        v = np.ascontiguousarray(inputs[name])
        if v.ndim == 0:
            v = v.reshape(1)
        arrays[f"in_{name}"] = v
        args[name] = nc.dram_tensor(f"in_{name}", v.shape, mybir.dt.from_np(v.dtype), kind="ExternalInput").ap()
    out = nc.dram_tensor("out", (N_NODES, D), mybir.dt.float32, kind="ExternalOutput").ap()
    gnn_program(nc, args, out)
    return run(nc, [arrays], core_ids=[0]).results[0]["out"]
```
